# Optimizing a Trainium2 kernel written in Bass

```python
import numpy as np
import jax
import jax.numpy as jnp

def _softmax(x, axis=-1):
    return jax.nn.softmax(x, axis=axis)

def _gelu(x):
    return jax.nn.gelu(x, approximate=True)

def _silu(x):
    return jax.nn.silu(x)

def _sigmoid(x):
    return jax.nn.sigmoid(x)

def _layernorm(x, axis=-1, eps=1e-05):
    m = jnp.mean(x, axis=axis, keepdims=True)
    v = jnp.var(x, axis=axis, keepdims=True)
    return (x - m) / jnp.sqrt(v + eps)

def _scatter_add(tgt, idx, src, axis=0):
    return tgt.at[idx].add(src)

def _segment_sum(src, seg, n):
    return jax.ops.segment_sum(src, seg, n)
kernel_name = 'mk_adaln_d1_jaxref_r8_40161d'

def setup_inputs(seed: int=0):
    np.random.seed(seed)
    _w = jnp.asarray

    def _L0_attn_setup():
        import jax, jax.numpy as jnp
        import numpy as np
        B, L, E, H = (4, 128, 128, 16)
        D = E // H
        SPARSITY = 0.4
        NEG_INF = jnp.float32(-1e+30)
        key = jax.random.key(seed)
        ks = jax.random.split(key, 8)
        s = 0.02
        return {'hidden_states': jax.random.normal(ks[0], (B, L, E), jnp.float32), 'qkv_w': jax.random.normal(ks[1], (3 * E, E), jnp.float32) * s, 'qkv_b': jax.random.normal(ks[2], (3 * E,), jnp.float32) * s, 'r_w1': jax.random.normal(ks[3], (E // 4, E), jnp.float32) * s, 'r_b1': jax.random.normal(ks[4], (E // 4,), jnp.float32) * s, 'r_w2': jax.random.normal(ks[5], (H, E // 4), jnp.float32) * s, 'r_b2': jax.random.normal(ks[6], (H,), jnp.float32) * s}
    _L0_attn_in = _L0_attn_setup()

    def _L0_ffn_setup():
        import jax, jax.numpy as jnp
        import numpy as np
        B, T, D, E = (4, 128, 128, 8)
        HD = 4 * D
        key = jax.random.key(seed)
        k1, k2, k3, k4 = jax.random.split(key, 4)
        std = 0.5 * D ** (-0.5)
        bound = 3.0 ** 0.5 * std
        x = jax.random.normal(k1, (B, T, D), dtype=jnp.float32)
        router_w = jax.random.normal(k2, (E, D), dtype=jnp.float32) * 0.02
        expert_fc = jax.random.uniform(k3, (E, D, HD), dtype=jnp.float32, minval=-bound, maxval=bound)
        expert_proj = jax.random.normal(k4, (E, D, HD), dtype=jnp.float32) * 0.02
        return {'x': x, 'router_w': router_w, 'expert_fc': expert_fc, 'expert_proj': expert_proj}
    _L0_ffn_in = _L0_ffn_setup()
    _L0_c = _w((lambda *s: np.random.randn(*s).astype(np.float32) * 0.05)(1, 128))
    _L0_wmod = _w((lambda *s: np.random.randn(*s).astype(np.float32) * 0.05)(128, 6 * 128) * 128 ** (-0.5))
    _d = {'L0_attn_hidden_states': _L0_attn_in['hidden_states'], 'L0_attn_qkv_w': _L0_attn_in['qkv_w'], 'L0_attn_qkv_b': _L0_attn_in['qkv_b'], 'L0_attn_r_w1': _L0_attn_in['r_w1'], 'L0_attn_r_b1': _L0_attn_in['r_b1'], 'L0_attn_r_w2': _L0_attn_in['r_w2'], 'L0_attn_r_b2': _L0_attn_in['r_b2'], 'L0_ffn_router_w': _L0_ffn_in['router_w'], 'L0_ffn_expert_fc': _L0_ffn_in['expert_fc'], 'L0_ffn_expert_proj': _L0_ffn_in['expert_proj'], 'L0_c': _L0_c, 'L0_wmod': _L0_wmod}
    _x0 = _d['L0_attn_hidden_states']
    _d['L0_attn_hidden_states'] = jax.random.normal(jax.random.fold_in(jax.random.key(seed), 1), (1, 2048, 128), dtype=_x0.dtype)
    del _x0
    return _d

def reference(L0_attn_hidden_states, L0_attn_qkv_w, L0_attn_qkv_b, L0_attn_r_w1, L0_attn_r_b1, L0_attn_r_w2, L0_attn_r_b2, L0_ffn_router_w, L0_ffn_expert_fc, L0_ffn_expert_proj, L0_c, L0_wmod):

    def _L0_attn_ref(hidden_states, qkv_w, qkv_b, r_w1, r_b1, r_w2, r_b2):
        import jax, jax.numpy as jnp
        import numpy as np
        B, L, E, H = (4, 128, 128, 16)
        D = E // H
        SPARSITY = 0.4
        NEG_INF = jnp.float32(-1e+30)
        bsz, tgt_len, embed_dim = hidden_states.shape
        qkv = (hidden_states @ qkv_w.T + qkv_b).reshape(bsz, tgt_len, 3, H, D)
        qkv = jnp.transpose(qkv, (2, 0, 3, 1, 4))
        q, k, v = (qkv[0], qkv[1], qkv[2])
        h1 = jax.nn.relu(hidden_states @ r_w1.T + r_b1)
        routing_logits = jax.nn.sigmoid(h1 @ r_w2.T + r_b2)
        routing_scores = jax.nn.sigmoid(routing_logits)
        attn = jnp.einsum('bhqd,bhkd->bhqk', q, k) / jnp.sqrt(jnp.float32(D))
        k_keep = max(1, int(tgt_len * SPARSITY))
        rs_t = jnp.transpose(routing_scores, (0, 2, 1))
        _, top_idx = jax.lax.top_k(rs_t, k_keep)
        keep = jnp.zeros((bsz, H, tgt_len), dtype=bool)
        keep = keep.at[jnp.arange(bsz)[:, None, None], jnp.arange(H)[None, :, None], top_idx].set(True)
        sparse = jnp.where(keep[:, :, None, :], attn, NEG_INF)
        w = jax.nn.softmax(sparse.astype(jnp.float32), axis=-1).astype(q.dtype)
        out = jnp.einsum('bhqk,bhkd->bhqd', w, v)
        out = jnp.transpose(out, (0, 2, 1, 3)).reshape(bsz, tgt_len, embed_dim)
        return out

    def _L0_ffn_ref(x, router_w, expert_fc, expert_proj):
        import jax, jax.numpy as jnp
        import numpy as np
        B, T, D, E = (4, 128, 128, 8)
        HD = 4 * D
        logits = jnp.einsum('btd,ed->bte', x, router_w)
        probs = jax.nn.softmax(logits, axis=-1)
        expert_ids = jnp.argmax(probs, axis=-1)
        mask = jax.nn.one_hot(expert_ids, E, dtype=x.dtype)
        h = jnp.einsum('btd,edh->ebth', x, expert_fc)
        h = jnp.square(jax.nn.relu(h))
        out_e = jnp.einsum('ebth,edh->ebtd', h, expert_proj)
        output = jnp.einsum('ebtd,bte->btd', out_e, mask)
        return output
    x = L0_attn_hidden_states
    mod = (_silu(L0_c) @ L0_wmod).reshape(L0_c.shape[0], 6, 1, -1)
    sa, ca, ga, sb, cb, gb = (mod[:, 0], mod[:, 1], mod[:, 2], mod[:, 3], mod[:, 4], mod[:, 5])
    ga = (2 * (ga >= 0) - 1) * jnp.maximum(jnp.abs(ga), 0.25)
    gb = (2 * (gb >= 0) - 1) * jnp.maximum(jnp.abs(gb), 0.25)
    h = _layernorm(x, axis=-1) * (1 + ca) + sa
    x = x + ga * _L0_attn_ref(h, L0_attn_qkv_w, L0_attn_qkv_b, L0_attn_r_w1, L0_attn_r_b1, L0_attn_r_w2, L0_attn_r_b2)
    h = _layernorm(x, axis=-1) * (1 + cb) + sb
    x = x + gb * _L0_ffn_ref(h, L0_ffn_router_w, L0_ffn_expert_fc, L0_ffn_expert_proj)
    return x

_drawn_inputs = setup_inputs


def setup_inputs(seed=0):
    import zlib

    import numpy as np

    out = dict(_drawn_inputs(seed))
    spreads = {}
    factors = {'L0_attn_qkv_w': 8.0,
     'L0_attn_qkv_b': 8.0,
     'L0_attn_r_w1': 8.0,
     'L0_attn_r_b1': 8.0,
     'L0_attn_r_w2': 8.0}
    for name, (base, spread) in spreads.items():
        noise = np.random.default_rng([zlib.crc32(name.encode()), seed]).standard_normal(out[name].shape)
        drawn = base * np.exp(spread * noise) if base else spread * noise
        out[name] = jnp.asarray(drawn.astype(out[name].dtype))
    for name, factor in factors.items():
        out[name] = (out[name] * factor).astype(out[name].dtype)
    return out
```

```python
import itertools
from contextlib import ExitStack

import concourse.bass as bass
from concourse import mybir

P = 128
F32 = mybir.dt.float32
BF16 = mybir.dt.bfloat16
FP16 = mybir.dt.float16
I32 = mybir.dt.int32
U32 = mybir.dt.uint32
ALU = mybir.AluOpType
ACT = mybir.ActivationFunctionType
AX = mybir.AxisListType

L = 2048
E = 128
H = 16
D = E // H
KEEP = int(L * 0.4)
NT = L // P
NP = H // 2
RH = E // 4
EPS = 1e-5

REM = KEEP - 6 * P
GAP = P - REM
BLOCKS = 7
SHARED = 3
STEPS = 13
EVEN_ORDER = [0, 1, 2, 4, 5, 6, 3]
ODD_ORDER = [3, 0, 1, 2, 4, 5, 6]
STEP_BLOCK = EVEN_ORDER + ODD_ORDER[1:]
NOT_KEPT = 1023.0
PARTS = 3
KROWS = 6 * D
SROWS = KROWS + PARTS
SUNITS = 64
TURNED = [4, 5, 6, 0, 1, 2]
STEP_COLUMN = [TURNED.index(x) for x in EVEN_ORDER[:6]] + [6] + [7 + TURNED.index(x) for x in ODD_ORDER[1:]]
SCORE_COLS = [[(3 * P, 6 * P + REM), (0, 3 * P)], [(10 * P, 13 * P), (6 * P + GAP, 10 * P)]]
LEAD = 46
UNITS = list(range(SUNITS))
for after, kind in ((54, "turn_m_even"), (43, "turn_k"), (22, "turn_m_odd"), (13, "index"), (5, "turn_o")):
    UNITS.insert(after + 1, kind)
RING = 3
NE = 8
HD = 4 * E
SLOT_TILES = NT + NE
assert len(UNITS) % RING == 0
ROUNDS = 11
CHUNKS = 8
CT = L // CHUNKS


def constants():
    import numpy as np

    p = np.arange(P)
    cols = {}
    cols["ident"] = np.eye(P)
    cols["same_head"] = (p[:, None] % H == p[None, :] % H)
    cols["before"] = (p[:, None] % H == p[None, :] % H) & (p[:, None] // H < p[None, :] // H)
    cols["place"] = np.broadcast_to(p, (P, P))
    u, js = np.arange(NT) // CHUNKS, np.arange(NT) % CHUNKS
    cols["token"] = (CT * js + P * u)[None, :] + p[:, None]
    cols["blocks"] = np.broadcast_to(EVEN_ORDER + ODD_ORDER, (P, 2 * BLOCKS))
    add = np.zeros((P, NP, STEPS))
    for i in range(NP):
        add[:, i, :6] = 2 * i
        add[:, i, 7:] = 2 * i + 1
        add[:, i, 6] = np.where(p < REM, 2 * i, np.where(p >= GAP, 2 * i + 1, 1 << 20))
    cols["row_add"] = add.reshape(P, -1)
    lo = np.where(p % H % 2 == 0, SHARED * P + REM, SHARED * P)
    cols["gap_from"] = lo[:, None]
    holds = ((p < REM) | (p >= GAP))
    cols["holds"] = holds[:, None]
    cols["lower"] = (p[:, None] < p[None, :])
    cols["expert"] = np.broadcast_to(np.repeat(np.arange(NE), NT) - NE, (P, NE * NT))
    cols["slot_tile"] = np.broadcast_to(np.repeat(np.arange(SLOT_TILES), NE), (P, SLOT_TILES * NE))
    st = np.zeros((ROUNDS + 1, 4))
    for r in range(ROUNDS):
        st[r] = np.arange(4) * (2.0 ** -4) * 4.0 ** -r
    cols["steps"] = np.broadcast_to(st.reshape(1, -1), (P, 4 * (ROUNDS + 1)))
    at, n = {}, 0
    for k, v in cols.items():
        at[k] = (n, n + v.shape[1])
        n += v.shape[1]
    table = np.concatenate([np.asarray(v, np.float32) for v in cols.values()], axis=1)
    return np.ascontiguousarray(table), at


def build(nc, x, w_q, w_kv, b_q, b_kv, w_r1, b_r1, w_r2, b_r2, c_col, wmod, w_route, w_fc, w_proj, const, out):
    _, at = constants()
    NCONST = const.shape[1]
    q_parts_dram = nc.dram_tensor("q_parts_dram", (H, PARTS, D, L), BF16, kind="Internal").ap()
    kv_dram = nc.dram_tensor("kv_dram", (L * H, 2 * D), F32, kind="Internal").ap()

    slots_dram = nc.dram_tensor("slots_dram", (SLOT_TILES * P, E), F32, kind="Internal").ap()
    y_dram = nc.dram_tensor("y_dram", (SLOT_TILES * P, E), F32, kind="Internal").ap()

    with ExitStack() as ctx:
        def sb(name, shape, dt=F32):
            return ctx.enter_context(nc.sbuf_tensor(name, shape, dt))

        def ps(name, shape, dt=F32):
            return ctx.enter_context(nc.psum_tensor(name, shape, dt))

        def sem(name):
            return ctx.enter_context(nc.semaphore(name))

        X = sb("X", [P, NT, E])
        C = sb("C", [P, NCONST])
        WQ = sb("WQ", [P, E])
        WKV = sb("WKV", [P, 2 * E])
        WR1 = sb("WR1", [P, RH])
        WR2 = sb("WR2", [P, 2, P])
        WMOD = sb("WMOD", [P, 6 * E])
        BQ = sb("BQ", [P, 1])
        BKV = sb("BKV", [1, 2 * E])
        BR1 = sb("BR1", [P, 1])
        BR2 = sb("BR2", [P, 1])
        ccol = sb("ccol", [P, 1])
        csig = sb("csig", [P, 1])
        silu = sb("silu", [P, 1])
        silu_b = sb("silu_b", [P, P])
        ones = sb("ones", [P, P])
        eps = sb("eps", [P, 1])
        mod_col = sb("mod_col", [P, 6])
        one_ca = sb("one_ca", [P, 1])
        stats = sb("stats", [P, NT, 6])
        mv = sb("mv", [P, NT, 2])
        std = sb("std", [P, NT])
        rstd = sb("rstd", [P, NT])
        XN = sb("XN", [P, NT, E])
        HT = sb("HT", [P, SLOT_TILES * P])
        H1 = sb("H1", [P, 512])
        R0 = sb("R0", [P, CT])
        R = sb("R", [P, CT])
        QBUF = sb("QBUF", [P, 3 * L + PARTS * L // 2])
        QF = QBUF[:, 0:L]
        QR = QBUF[:, L:3 * L].rearrange("p (a l) -> p a l", a=2)
        QP = QBUF[:, 3 * L:].bitcast(BF16).rearrange("p (a l) -> p a l", a=PARTS)
        WE = QBUF[:, 0:NE * 2 * HD].rearrange("p (n c) -> p n c", n=NE)
        KV = sb("KV", [P, NT, 2 * E])
        junk = sb("junk", [P, CT])
        cand = sb("cand", [P, ROUNDS + 1, 4])
        cnt = sb("cnt", [P, ROUNDS, 3])
        nge = sb("nge", [P, ROUNDS])
        njunk = sb("njunk", [P, ROUNDS, 3])
        etab = sb("etab", [P, ROUNDS, 4])
        GT = sb("GT", [P, CT])
        EQ = sb("EQ", [P, CT])
        tot = sb("tot", [P, 2])
        offs = sb("offs", [P, 4])
        need = sb("need", [P, 2])
        rF = sb("rF", [P, NT, H])
        aF = sb("aF", [P, NT, H])
        place16 = sb("place16", [P, P], FP16)
        ABUF = sb("ABUF", [P, 2 * L])
        A1 = ABUF[:, :].bitcast(FP16).rearrange("p (b e t q) -> p b e t q", b=2, e=2, t=NT)
        B0 = sb("B0", [P, H, NT, BLOCKS])
        B1 = sb("B1", [P, H, NT, BLOCKS], FP16)
        idx = sb("idx", [P, 2, STEPS], I32)
        G = sb("G", [P, 2, STEPS, 2 * D])
        KR = sb("KR", [P, 2, 2, STEPS, D])
        KS = sb("KS", [P, 2, STEPS, 64], BF16)
        RS = sb("RS", [P, 2, P], BF16)
        VS = sb("VS", [P, 2, STEPS, 32])
        KTM = sb("KTM", [P, 2, STEPS * P], BF16)
        KTE = sb("KTE", [P, 2, STEPS * P], BF16)
        QSM = sb("QSM", [P, 2, L], BF16)
        QSE = sb("QSE", [P, 2, L], BF16)
        identb = sb("identb", [P, P], BF16)
        MXU = sb("MXU", [P, 2, SUNITS])
        NM = sb("NM", [P, 3, 2 * NT])
        SM = sb("SM", [P, 2, PARTS, NT], BF16)
        MT = sb("MT", [PARTS * NT, 2, P], BF16)
        PR = sb("PR", [P, 2, L])
        work = PR[:, :, :].rearrange("p a (n c) -> p (a n) c", c=CT)
        jnk3 = work[:, 0:3, :]
        SG, SE, W1, W2, W3, W4, W5 = [work[:, 3 + n, :] for n in range(7)]
        posI, rI, aI = [work[:, 10 + n, :].bitcast(I32) for n in range(3)]
        OS = sb("OS", [P, 512])
        REC = sb("REC", [P, 4, 4, 2])
        AT = sb("AT", [P, NT, E])
        gate = sb("gate", [P, 2, E])
        gsign = sb("gsign", [P, 2, E])
        gabs = sb("gabs", [P, 2, E])
        gneg = sb("gneg", [P, 2, E])
        one_cb = sb("one_cb", [P, 1])
        WROUTE = sb("WROUTE", [P, NE])
        lowerb = sb("lowerb", [P, P], BF16)
        onesb = sb("onesb", [P, P], BF16)
        zeros = sb("zeros", [P, E])
        LM = sb("LM", [P, 4, NT])
        LE = KTM[:, 0, 0:2 * 6 * P].bitcast(F32).rearrange("p (a c) -> p a c", a=6)
        OH = sb("OH", [P, NE, NT])
        OHB = sb("OHB", [P, NE * NT], BF16)
        TOT = sb("TOT", [P, NE, NT])
        CUM = sb("CUM", [P, 1 + NE * NT])
        EN = sb("EN", [P, 6, NE])
        ENI = sb("ENI", [P, 2, NE], I32)
        SLB = sb("SLB", [P, NE, NT])
        SLC = sb("SLC", [P, NE, NT])
        slotF = sb("slotF", [P, NT])
        slot = sb("slot", [P, NT], I32)
        TE = KTM[:, 1, 0:2 * SLOT_TILES * NE].bitcast(F32).rearrange("p (s e) -> p s e", e=NE)
        TEF = sb("TEF", [P, SLOT_TILES])
        TEI = sb("TEI", [P, SLOT_TILES], I32)
        X2 = X[:, :, :]
        GAT, XN2 = [ABUF[:, L * n:L * (n + 1)].rearrange("p (t e) -> p t e", e=E) for n in range(2)]
        WB = QSM[:, :, :].bitcast(F32)
        RELU = QSE[:, :, :].bitcast(F32)
        RL, R2 = RELU[:, 0, :].rearrange("p (a c) -> p a c", a=2), RELU[:, 1, :].rearrange("p (a c) -> p a c", a=2)
        WFC, WPROJ = WB[:, :, 0:HD], WB[:, :, HD:]
        YG = XN[:, :, :]
        HS = KV[:, :, :].rearrange("p t c -> p (t c)")[:, 0:SLOT_TILES * P].rearrange("p (t e) -> p t e", e=E)
        H2T = AT[:, :, :].rearrange("p t e -> p (t e)")
        YS = PR[:, :, :].rearrange("p a c -> p (a c)")[:, 0:SLOT_TILES * P].rearrange("p (t e) -> p t e", e=E)

        ST = ps("ST", [P, 2, 1024])
        SC = ps("SC", [P, RING, 512])
        OP = ps("OP", [P, 512])
        MI = SC[:, 2, :]

        def bank(pos):
            return SC[:, pos % RING, :]

        def bank16(pos):
            return SC[:, pos % RING, :].bitcast(BF16)

        def cc(name):
            a, b = at[name]
            return C[:, a:b]

        ident, same_head, before = cc("ident"), cc("same_head"), cc("before")
        token, blocks, row_add, steps = cc("token"), cc("blocks"), cc("row_add"), cc("steps")

        dve_step = sem("dve_step")
        pool_step = sem("pool_step")
        tail_step = sem("tail_step")
        const_in = sem("const_in")
        x_in = sem("x_in")
        w_in = sem("w_in")
        wr2_zero = sem("wr2_zero")
        wr2_in = sem("wr2_in")
        silu_ready = sem("silu_ready")
        mod_done = sem("mod_done")
        mod_ready = sem("mod_ready")
        stats_ready = sem("stats_ready")
        std_ready = sem("std_ready")
        xn_ready = sem("xn_ready")
        xt_done = sem("xt_done")
        ht_ready = sem("ht_ready")
        h1_done = sem("h1_done")
        h1_ready = sem("h1_ready")
        logit_done = sem("logit_done")
        score0 = sem("score0")
        q_done = sem("q_done")
        q_ready = sem("q_ready")
        kv_done = sem("kv_done")
        kv_ready = sem("kv_ready")
        qpart_a = sem("qpart_a")
        qpart_p = sem("qpart_p")
        qparts_out = sem("qparts_out")
        kv_out = sem("kv_out")
        search_dve = sem("search_dve")
        search_pe = sem("search_pe")
        sel_pe = sem("sel_pe")
        pos_done = sem("pos_done")
        pos_ready = sem("pos_ready")
        onehot_ready = sem("onehot_ready")
        idx_mm = sem("idx_mm")
        idx_ready = sem("idx_ready")
        gathered = sem("gathered")
        prep_ready = sem("prep_ready")
        v_ready = sem("v_ready")
        init_pool = sem("init_pool")
        init_dve = sem("init_dve")
        ktr_done = sem("ktr_done")
        kt_odd = sem("kt_odd")
        kt_even = sem("kt_even")
        kte_ready = sem("kte_ready")
        qsm_even = sem("qsm_even")
        qsm_odd = sem("qsm_odd")
        qse_even = sem("qse_even")
        qse_odd = sem("qse_odd")
        s_filled = sem("s_filled")
        s_reduced = sem("s_reduced")
        m_chain = sem("m_chain")
        m_split_even = sem("m_split_even")
        m_split_odd = sem("m_split_odd")
        mtr_even = sem("mtr_even")
        mtr_odd = sem("mtr_odd")
        mt_even = sem("mt_even")
        mt_odd = sem("mt_odd")
        mrow_even = sem("mrow_even")
        mrow_odd = sem("mrow_odd")
        st_filled = sem("st_filled")
        exp_done = sem("exp_done")
        pv_done = sem("pv_done")
        o_copied = sem("o_copied")
        otr_done = sem("otr_done")
        o_norm = sem("o_norm")
        rec_ready = sem("rec_ready")
        out_in = sem("out_in")
        b_parts = sem("b_parts")
        we_in = sem("we_in")
        slots_zero = sem("slots_zero")
        gate_ready = sem("gate_ready")
        tail_dve = sem("tail_dve")
        gated = sem("gated")
        x2_ready = sem("x2_ready")
        stats2_ready = sem("stats2_ready")
        std2_ready = sem("std2_ready")
        xn2_ready = sem("xn2_ready")
        xt2_done = sem("xt2_done")
        h2_ready = sem("h2_ready")
        route_done = sem("route_done")
        exp2_done = sem("exp2_done")
        oh_ready = sem("oh_ready")
        rank_done = sem("rank_done")
        slot_ready = sem("slot_ready")
        scattered = sem("scattered")
        slots_in = sem("slots_in")
        hst_done = sem("hst_done")
        hst_ready = sem("hst_ready")
        fc_ready = sem("fc_ready")
        proj_ready = sem("proj_ready")
        up_done = sem("up_done")
        relu_done = sem("relu_done")
        sq_done = sem("sq_done")
        down_done = sem("down_done")
        y_ready = sem("y_ready")
        y_out = sem("y_out")
        y_back_0 = sem("y_back_0")
        y_back_1 = sem("y_back_1")
        y_back_2 = sem("y_back_2")
        y_back_3 = sem("y_back_3")
        tile_ready = sem("tile_ready")
        out_ready = sem("out_ready")

        block = ctx.enter_context(nc.Block())
        x_t = x[0].rearrange("(t p) e -> p t e", p=P)
        out_t = out[0].rearrange("(t p) e -> p t e", p=P)
        kv_t = kv_dram.rearrange("(t p h) d -> p t (h d)", p=P, h=H)

        LEAD_UNITS = list(range(36)) + ["turn_m_even"] + list(range(36, LEAD))
        KT1_POS = len(LEAD_UNITS) % RING

        @block.sync
        def _(sp):
            sp.dma_start(X[:, 0:4, :], x_t[:, 0:4, :]).then_inc(x_in, 16)
            sp.dma_start(C[:, :], const).then_inc(const_in, 16)
            for g in range(1, 4):
                sp.wait_ge(x_in, 16 * g)
                sp.dma_start(X[:, 4 * g:4 * g + 4, :], x_t[:, 4 * g:4 * g + 4, :]).then_inc(x_in, 16)
            sp.wait_ge(qpart_a, 2)
            sp.wait_ge(qpart_p, 2)
            sp.wait_ge(q_ready, 8)
            for part in range(PARTS):
                sp.dma_start(q_parts_dram[:, part, :, :], QP[:, part, :]).then_inc(qparts_out, 16)
            sp.wait_ge(kv_ready, NT // 2)
            sp.dma_start(kv_t, KV[:, :, :]).then_inc(kv_out, 16)
            sp.wait_ge(qparts_out, 16 * PARTS)
            sp.wait_ge(init_dve, 1)

            def load_q(dst, i, par, loaded):
                for e in range(2):
                    src = q_parts_dram[2 * i + e, :, :, :].rearrange("a d l -> (a d) l")
                    for row, n in ((0, 3), (3, 2), (5, 1)):
                        sp.dma_start(dst[64 * e + D * row:64 * e + D * (row + n), par, :],
                                     src[0:D * n, :]).then_inc(loaded, 16)

            def m_rows(i, par, e):
                sp.wait_ge([mt_even, mt_odd][e], i + 1)
                dst = QSE[64 * e + KROWS:64 * e + SROWS, par, :].rearrange("a (t q) -> a t q", q=P)
                sp.dma_start(dst, MT[:, e, :]).then_inc([mrow_even, mrow_odd][e], 16)

            load_q(QSM, 0, 0, qsm_even)
            load_q(QSE, 0, 0, qse_even)
            load_q(QSM, 1, 1, qsm_odd)
            m_rows(0, 0, 0)
            for i in range(NP):
                if i + 1 < NP:
                    if i >= 1:
                        sp.wait_ge(st_filled, 2 * STEPS * i)
                    load_q(QSE, i + 1, (i + 1) % 2, [qse_even, qse_odd][(i + 1) % 2])
                m_rows(i, i % 2, 1)
                if i == 1:
                    for n, w_part in enumerate((w_fc, w_proj)):
                        sp.dma_start(WE[:, :, HD * n:HD * (n + 1)], w_part.rearrange("n p c -> p n c"))\
                            .then_inc(we_in, 16)
                if i + 2 < NP:
                    sp.wait_ge(s_filled, SUNITS * (i + 1))
                    load_q(QSM, i + 2, i % 2, [qsm_even, qsm_odd][i % 2])
                if i + 1 < NP:
                    m_rows(i + 1, (i + 1) % 2, 0)
            sp.wait_ge(scattered, 16 * NT)
            slots_t = slots_dram.rearrange("(t p) e -> p t e", p=P)
            y_t = y_dram.rearrange("(t p) e -> p t e", p=P)
            sp.dma_start(HS[:, :, :], slots_t).then_inc(slots_in, 16)
            for q in range(SLOT_TILES // 4):
                sp.wait_ge(y_ready, 4 * q + 4)
                sp.dma_start(y_t[:, 4 * q:4 * q + 4, :], YS[:, 4 * q:4 * q + 4, :]).then_inc(y_out, 16)
            for g in range(4):
                sp.wait_ge(out_ready, g + 1)
                sp.dma_start(out_t[:, 4 * g:4 * g + 4, :], GAT[:, 4 * g:4 * g + 4, :]).then_inc(out_in, 16)
            sp.wait_ge(out_in, 64)
            sp.wait_ge(slots_zero, 16)

        @block.gpsimd
        def _(pool):
            next_step = itertools.count(1).__next__

            nc.gpsimd.memset(WR2[:, :, :], 0.0).then_inc(wr2_zero, 1)
            nc.gpsimd.memset(KS[:, :, :, :], 0.0).then_inc(pool_step, 1)
            pool.wait_ge(pool_step, next_step())
            nc.gpsimd.memset(VS[:, :, :, :], 0.0).then_inc(pool_step, 1)
            pool.wait_ge(pool_step, next_step())
            nc.gpsimd.memset(RS[:, :, :], 0.0).then_inc(init_pool, 1)
            nc.gpsimd.memset(G[:, :, :, :], 0.0).then_inc(init_pool, 1)
            pool.wait_ge(const_in, 16)
            holds = cc("holds")
            for b in range(2):
                nc.gpsimd.memset(KS[:, b, :, KROWS:SROWS], 1.0).then_inc(pool_step, 1)
                pool.wait_ge(pool_step, next_step())
                nc.gpsimd.tensor_copy(KS[:, b, 6, KROWS:SROWS], holds.to_broadcast([P, PARTS])).then_inc(pool_step, 1)
                pool.wait_ge(pool_step, next_step())
                nc.gpsimd.memset(VS[:, b, 0:6, D:D + 1], 1.0).then_inc(pool_step, 1)
                pool.wait_ge(pool_step, next_step())
                nc.gpsimd.memset(VS[:, b, 7:13, 16 + D:16 + D + 1], 1.0).then_inc(pool_step, 1)
                pool.wait_ge(pool_step, next_step())
                nc.gpsimd.tensor_copy(VS[0:64, b, 6, D:D + 1], holds[0:64, :]).then_inc(pool_step, 1)
                pool.wait_ge(pool_step, next_step())
                nc.gpsimd.tensor_copy(VS[64:128, b, 6, 16 + D:16 + D + 1], holds[64:128, :]).then_inc(pool_step, 1)
                pool.wait_ge(pool_step, next_step())
            pool.wait_ge(q_ready, 8)
            nc.gpsimd.tensor_tensor(QR[:, 0, :], QF[:, :], QP[:, 0, :], ALU.subtract).then_inc(qpart_p, 1)
            pool.wait_ge(qpart_a, 1)
            nc.gpsimd.tensor_tensor(QR[:, 1, :], QR[:, 0, :], QP[:, 1, :], ALU.subtract).then_inc(qpart_p, 1)

            pool.wait_ge(kv_out, 16)
            pool.wait_ge(init_pool, 2)

            def onehot(i, b):
                pool.wait_ge(idx_mm, i - 1)
                pool.wait_ge(prep_ready, i)
                for e in range(2):
                    for t in range(NT):
                        last = nc.gpsimd.tensor_scalar(A1[:, b, e, t, :], place16[:, :],
                                                       rF[:, t, 2 * i + e:2 * i + e + 1], None, ALU.is_equal)
                last.then_inc(onehot_ready, 1)

            def gathers(i, b):
                pool.wait_ge(idx_ready, i + 1)
                if i >= 1:
                    pool.wait_ge(v_ready, i)
                for s in range(STEPS):
                    pool.indirect_dma_start(
                        G[:, b, s, :], None, kv_dram, bass.IndirectOffsetOnAxis(ap=idx[:, b, s:s + 1].bitcast(U32), axis=0),
                        bounds_check=L * H - 1, oob_is_err=False).then_inc(gathered, 16)

            def prep(i, b):
                pool.wait_ge(gathered, 16 * STEPS * (i + 1))
                k = G[:, b, :, 0:D]
                if i >= 2:
                    pool.wait_ge(ktr_done, i - 1)

                def rep(ap, n):
                    return ap.rearrange("p s (a d) -> p s a d", a=1).to_broadcast([P, STEPS, n, D])

                def stack(c, n):
                    return KS[:, b, :, D * c:D * (c + n)].rearrange("p s (a d) -> p s a d", a=n)

                nc.gpsimd.tensor_copy(stack(0, 3), rep(k, 3)).then_inc(pool_step, 1)
                pool.wait_ge(pool_step, next_step())
                nc.gpsimd.tensor_tensor(KR[:, b, 0, :, :], k, KS[:, b, :, 0:D], ALU.subtract).then_inc(pool_step, 1)
                pool.wait_ge(pool_step, next_step())
                nc.gpsimd.tensor_copy(stack(3, 2), rep(KR[:, b, 0, :, :], 2)).then_inc(pool_step, 1)
                pool.wait_ge(pool_step, next_step())
                nc.gpsimd.tensor_tensor(KR[:, b, 1, :, :], KR[:, b, 0, :, :], KS[:, b, :, 3 * D:4 * D],
                                        ALU.subtract).then_inc(pool_step, 1)
                pool.wait_ge(pool_step, next_step())
                nc.gpsimd.tensor_copy(stack(5, 1), rep(KR[:, b, 1, :, :], 1)).then_inc(pool_step, 1)
                pool.wait_ge(pool_step, next_step())
                nc.gpsimd.tensor_copy(RS[0:64, b, 0:64], KS[0:64, b, 6, :]).then_inc(pool_step, 1)
                pool.wait_ge(pool_step, next_step())
                nc.gpsimd.tensor_copy(RS[64:128, b, 64:128], KS[64:128, b, 6, :]).then_inc(prep_ready, 1)

            def prep_v(i, b):
                pool.wait_ge(prep_ready, i + 1)
                if i >= 2:
                    pool.wait_ge(pv_done, STEPS * (i - 1))
                nc.gpsimd.tensor_copy(VS[:, b, 0:6, 0:D], G[:, b, 0:6, D:2 * D]).then_inc(pool_step, 1)
                pool.wait_ge(pool_step, next_step())
                nc.gpsimd.tensor_copy(VS[:, b, 7:13, 16:16 + D], G[:, b, 7:13, D:2 * D]).then_inc(pool_step, 1)
                pool.wait_ge(pool_step, next_step())
                nc.gpsimd.tensor_copy(VS[0:64, b, 6, 0:D], G[0:64, b, 6, D:2 * D]).then_inc(pool_step, 1)
                pool.wait_ge(pool_step, next_step())
                nc.gpsimd.tensor_copy(VS[64:128, b, 6, 16:16 + D], G[64:128, b, 6, D:2 * D])\
                    .then_inc(v_ready, 1)

            gathers(0, 0)
            prep(0, 0)
            prep_v(0, 0)
            gathers(1, 1)
            prep(1, 1)
            onehot(2, 0)
            prep_v(1, 1)
            for i in range(2, NP):
                gathers(i, i % 2)
                prep(i, i % 2)
                if i + 1 < NP:
                    onehot(i + 1, (i + 1) % 2)
                prep_v(i, i % 2)
            pool.wait_ge(gate_ready, 1)
            pool.wait_ge(o_norm, 2 * NP)
            for g in range(4):
                nc.gpsimd.tensor_tensor(GAT[:, 4 * g:4 * g + 4, :], AT[:, 4 * g:4 * g + 4, :],
                                        gate[:, 0:1, :].to_broadcast([P, 4, E]), ALU.mult).then_inc(gated, 1)
            pool.wait_ge(slot_ready, 1)
            pool.wait_ge(slots_zero, 16)
            for t in range(NT):
                pool.indirect_dma_start(
                    slots_dram, bass.IndirectOffsetOnAxis(ap=slot[:, t:t + 1].bitcast(U32), axis=0), XN2[:, t, :], None,
                    bounds_check=SLOT_TILES * P - 1, oob_is_err=False).then_inc(scattered, 16)
            pool.wait_ge(y_out, 4 * SLOT_TILES)
            for t in range(NT):
                pool.indirect_dma_start(
                    YG[:, t, :], None, y_dram, bass.IndirectOffsetOnAxis(ap=slot[:, t:t + 1].bitcast(U32), axis=0),
                    bounds_check=SLOT_TILES * P - 1, oob_is_err=False).then_inc([y_back_0, y_back_1, y_back_2, y_back_3][t // 4], 16)

        @block.scalar
        def _(act):
            act.dma_start(ccol[:, :], c_col).then_inc(w_in, 16)
            act.dma_start(WMOD[:, :], wmod).then_inc(w_in, 16)
            act.dma_start(WR1[:, :], w_r1).then_inc(w_in, 16)
            act.dma_start(BR1[:, :], b_r1).then_inc(w_in, 16)
            act.dma_start(BR2[:, :], b_r2).then_inc(w_in, 16)
            act.dma_start(WQ[:, :], w_q).then_inc(w_in, 16)
            act.dma_start(WKV[:, :], w_kv).then_inc(w_in, 16)
            act.dma_start(BQ[:, :], b_q).then_inc(w_in, 16)
            act.dma_start(BKV[:, :], b_kv).then_inc(w_in, 16)
            act.dma_start(WROUTE[:, :], w_route).then_inc(w_in, 16)
            act.wait_ge(wr2_zero, 1)
            for j in range(4):
                for s in range(2):
                    c0 = 32 * j + H * s
                    act.dma_start(WR2[32 * j:32 * j + RH, s, c0:c0 + H], w_r2).then_inc(wr2_in, 16)
            act.wait_ge(w_in, 16 * 10)
            nc.scalar.activation(csig[:, :], ccol[:, :], ACT.Sigmoid).then_inc(silu_ready, 1)
            act.wait_ge(init_dve, 1)
            act.dma_start(slots_dram.rearrange("(t p) e -> p t e", p=P),
                          zeros[:, :].rearrange("p (a e) -> p a e", a=1).to_broadcast([P, SLOT_TILES, E]))\
               .then_inc(slots_zero, 16)
            for g in range(4):
                act.wait_ge(stats_ready, 8 * g + 8)
                nc.scalar.activation(std[:, 4 * g:4 * g + 4], mv[:, 4 * g:4 * g + 4, 1], ACT.Sqrt,
                                     bias=eps[:, 0:1]).then_inc(std_ready, 1)
            act.wait_ge(mod_ready, 2)
            for g in range(4):
                act.wait_ge(xt_done, g + 1)
                nc.scalar.activation(HT[:, 512 * g:512 * g + 512], ST[:, g // 2, 512 * (g % 2):512 * (g % 2) + 512],
                                     ACT.Identity, bias=mod_col[:, 0:1], scale=one_ca[:, 0:1])\
                    .then_inc(ht_ready, 1)
            act.wait_ge(h1_done, 1)
            nc.scalar.activation(H1[:, :], SC[:, 0, :], ACT.Relu, bias=BR1[:, 0:1]).then_inc(h1_ready, 1)
            act.wait_ge(logit_done, 1)
            nc.scalar.activation(R0[:, :], SC[:, 1, 0:CT], ACT.Sigmoid, bias=BR2[:, 0:1]).then_inc(score0, 1)
            act.wait_ge(score0, 1)
            nc.scalar.activation(junk[:, :], R0[:, :], ACT.Sigmoid).then_inc(score0, 1)
            for g in range(4):
                act.wait_ge(q_done, g + 1)
                src = ST[:, g // 2, 512 * (g % 2):512 * (g % 2) + 512]
                nc.scalar.activation(QF[:, 512 * g:512 * g + 512], src, ACT.Identity, bias=BQ[:, 0:1])\
                    .then_inc(q_ready, 1)
                nc.scalar.activation(QP[:, 0, 512 * g:512 * g + 512], src, ACT.Identity, bias=BQ[:, 0:1])\
                    .then_inc(q_ready, 1)
            for n in range(NT // 2):
                act.wait_ge(kv_done, n + 1)
                nc.scalar.activation(KV[:, 2 * n:2 * n + 2, :].rearrange("p t c -> p (t c)"),
                                     [OP[:, :], MI][n % 2], ACT.Copy).then_inc(kv_ready, 1)
            act.wait_ge(qpart_p, 1)
            nc.scalar.activation(QP[:, 1, :], QR[:, 0, :], ACT.Copy).then_inc(qpart_a, 1)
            act.wait_ge(qpart_p, 2)
            nc.scalar.activation(QP[:, 2, :], QR[:, 1, :], ACT.Copy).then_inc(qpart_a, 1)

            def copy_kt(i, b, pos):
                act.wait_ge(ktr_done, i + 1)
                nc.scalar.activation(KTM[64:128, b, 6 * P:13 * P], bank16(pos)[64:128, 0:7 * P], ACT.Copy)\
                    .then_inc(kt_odd, 1)

            def copy_o(i):
                act.wait_ge(pv_done, STEPS * (i + 1))
                if i >= 1:
                    act.wait_ge(otr_done, i)
                nc.scalar.activation(OS[:, :], OP[:, :], ACT.Copy).then_inc(o_copied, 1)

            KT_STEP = UNITS.index("turn_k") * STEPS // len(UNITS)
            copy_kt(0, 0, 2)
            copy_kt(1, 1, KT1_POS)
            for i in range(NP):
                for s in range(STEPS):
                    n = STEPS * i + s
                    for half in range(2):
                        act.wait_ge(st_filled, 2 * n + half + 1)
                        if n >= 2:
                            act.wait_ge(pv_done, n - 1)
                        nc.scalar.activation(PR[:, n % 2, 1024 * half:1024 * half + 1024], ST[:, half, :], ACT.Exp,
                                             scale=float(D) ** -0.5).then_inc(exp_done, 1)
                    if s == 0 and i >= 1:
                        copy_o(i - 1)
                    if s == KT_STEP and i + 2 < NP:
                        copy_kt(i + 2, i % 2, UNITS.index("turn_k"))
            copy_o(NP - 1)
            def turned2(g):
                act.wait_ge(xt2_done, g + 1)
                nc.scalar.activation(H2T[:, 512 * g:512 * g + 512], ST[:, g // 2, 512 * (g % 2):512 * (g % 2) + 512],
                                     ACT.Identity, bias=mod_col[:, 3:4], scale=one_cb[:, 0:1])\
                    .then_inc(h2_ready, 1)

            for g in range(4):
                act.wait_ge(stats2_ready, 8 * g + 8)
                nc.scalar.activation(std[:, 4 * g:4 * g + 4], mv[:, 4 * g:4 * g + 4, 1], ACT.Sqrt,
                                     bias=eps[:, 0:1]).then_inc(std2_ready, 1)
                if g:
                    turned2(g - 1)
            turned2(3)
            act.wait_ge(tail_dve, 2)
            nc.scalar.activation(LE[:, 1, :], LE[:, 0, :], ACT.Exp).then_inc(exp2_done, 1)
            for q in range((SLOT_TILES + 3) // 4):
                n = min(4, SLOT_TILES - 4 * q)
                act.wait_ge(hst_done, q + 1)
                nc.scalar.activation(HT[:, 512 * q:512 * q + P * n], ST[:, q % 2, 0:P * n],
                                     ACT.Identity, bias=mod_col[:, 3:4], scale=one_cb[:, 0:1])\
                    .then_inc(hst_ready, 1)
            def relu(n, b):
                act.wait_ge(up_done, n + 1)
                if not isinstance(n, int) or n >= 2:
                    act.wait_ge(sq_done, n - 1)
                nc.scalar.activation(RL[:, b, :], SC[:, b, :], ACT.Relu).then_inc(relu_done, 1)

            def y_out_of_psum(n, b):
                act.wait_ge(down_done, n + 1)
                nc.scalar.activation(YS[:, bass.ds(n, 1), :].rearrange("p a e -> p (a e)"), ST[:, b, 0:E], ACT.Copy)\
                    .then_inc(y_ready, 1)

            relu(0, 0)
            relu(1, 1)
            y_out_of_psum(0, 0)
            with act.Fori(2, SLOT_TILES - 1, 2) as n:
                relu(n, 0)
                y_out_of_psum(n - 1, 1)
                relu(n + 1, 1)
                y_out_of_psum(n, 0)
            y_out_of_psum(SLOT_TILES - 1, 1)

        @block.vector
        def _(dve):
            v = nc.vector
            dve.wait_ge(const_in, 16)
            next_step = itertools.count(1).__next__

            v.memset(ones[:, :], 1.0).then_inc(dve_step, 1)
            dve.wait_ge(dve_step, next_step())
            v.memset(eps[:, :], EPS).then_inc(dve_step, 1)
            dve.wait_ge(dve_step, next_step())
            v.memset(zeros[:, :], 0.0).then_inc(dve_step, 1)
            dve.wait_ge(dve_step, next_step())
            v.memset(onesb[:, :], 1.0).then_inc(dve_step, 1)
            dve.wait_ge(dve_step, next_step())
            v.memset(CUM[:, 0:1], 0.0).then_inc(dve_step, 1)
            dve.wait_ge(dve_step, next_step())
            v.tensor_copy(lowerb[:, :], cc("lower")).then_inc(dve_step, 1)
            dve.wait_ge(dve_step, next_step())
            v.memset(QSM[:, :, :], 0.0).then_inc(dve_step, 1)
            dve.wait_ge(dve_step, next_step())
            v.memset(KTM[:, :, :], 0.0).then_inc(dve_step, 1)
            dve.wait_ge(dve_step, next_step())
            v.memset(QSE[:, :, :], 0.0).then_inc(dve_step, 1)
            dve.wait_ge(dve_step, next_step())
            v.tensor_copy(place16[:, :], cc("place")).then_inc(dve_step, 1)
            dve.wait_ge(dve_step, next_step())
            v.tensor_copy(identb[:, :], ident).then_inc(init_dve, 1)
            dve.wait_ge(silu_ready, 1)
            v.tensor_tensor(silu[:, :], ccol[:, :], csig[:, :], ALU.mult).then_inc(dve_step, 1)
            dve.wait_ge(dve_step, next_step())
            v.tensor_scalar(silu_b[:, :], ones[:, :], silu[:, 0:1], None, ALU.mult).then_inc(silu_ready, 1)
            dve.wait_ge(mod_done, 1)
            v.tensor_copy(mod_col[:, :], OP[:, 0:6]).then_inc(mod_ready, 1)
            dve.wait_ge(mod_ready, 1)
            v.tensor_scalar(one_ca[:, :], mod_col[:, 1:2], 1.0, None, ALU.add).then_inc(mod_ready, 1)
            v.tensor_scalar(one_cb[:, :], mod_col[:, 4:5], 1.0, None, ALU.add).then_inc(dve_step, 1)
            dve.wait_ge(dve_step, next_step())
            g_ps = OP[:, P:3 * P]
            g2 = "p a e -> p (a e)"
            v.tensor_scalar(gsign[:, :, :].rearrange(g2), g_ps, 0.0, 2.0, ALU.is_ge, ALU.mult).then_inc(dve_step, 1)
            dve.wait_ge(dve_step, next_step())
            v.tensor_scalar(gneg[:, :, :].rearrange(g2), g_ps, -1.0, 0.25, ALU.mult, ALU.max).then_inc(dve_step, 1)
            dve.wait_ge(dve_step, next_step())
            v.tensor_tensor(gabs[:, :, :].rearrange(g2), g_ps, gneg[:, :, :].rearrange(g2), ALU.max)\
                .then_inc(dve_step, 1)
            dve.wait_ge(dve_step, next_step())
            v.scalar_tensor_tensor(gate[:, :, :], gsign[:, :, :], -1.0, gabs[:, :, :], ALU.add, ALU.mult)\
                .then_inc(gate_ready, 1)
            for g in range(4):
                dve.wait_ge(x_in, 16 * (g + 1))
                for t in range(4 * g, 4 * g + 4):
                    v.bn_stats(stats[:, t, :], X[:, t, :]).then_inc(stats_ready, 1)
                for t in range(4 * g, 4 * g + 4):
                    dve.wait_ge(stats_ready, 8 * g + t - 4 * g + 1)
                    v.bn_aggr(mv[:, t, :], stats[:, t, :]).then_inc(stats_ready, 1)
                dve.wait_ge(std_ready, g + 1)
                v.reciprocal(rstd[:, 4 * g:4 * g + 4], std[:, 4 * g:4 * g + 4]).then_inc(dve_step, 1)
                dve.wait_ge(dve_step, next_step())
                for t in range(4 * g, 4 * g + 4):
                    v.tensor_scalar(XN[:, t, :], X[:, t, :], mv[:, t, 0:1], rstd[:, t:t + 1], ALU.subtract,
                                    ALU.mult).then_inc(xn_ready, 1)
            dve.wait_ge(score0, 2)
            v.tensor_scalar(R[:, :], junk[:, :], 0.5, None, ALU.max).then_inc(dve_step, 1)
            dve.wait_ge(dve_step, next_step())
            v.tensor_scalar(cand[:, 0, :], steps[:, 0:4], 0.5, None, ALU.add).then_inc(dve_step, 1)
            dve.wait_ge(dve_step, next_step())
            for r in range(ROUNDS):
                for k in range(3):
                    v.tensor_scalar(jnk3[:, k, :], R[:, :], cand[:, r, k + 1:k + 2], None, ALU.is_ge, ALU.add,
                                    accum_out=cnt[:, r, k:k + 1]).then_inc(search_dve, 1)
                if r + 1 <= ROUNDS:
                    v.tensor_scalar(etab[:, r, :], steps[:, 4 * (r + 1):4 * (r + 2)], cand[:, r, 0:1], None,
                                    ALU.add).then_inc(dve_step, 1)
                    dve.wait_ge(dve_step, next_step())
                dve.wait_ge(search_pe, r + 1)
                v.tensor_scalar(njunk[:, r, :], SC[:, r % 2, 0:3], KEEP - 0.5, None, ALU.is_ge, ALU.add,
                                accum_out=nge[:, r:r + 1]).then_inc(dve_step, 1)
                dve.wait_ge(dve_step, next_step())
                v.scalar_tensor_tensor(cand[:, r + 1, :], nge[:, r:r + 1].to_broadcast([P, 4]),
                                       2.0 ** -4 * 4.0 ** -r, etab[:, r, :], ALU.mult, ALU.add).then_inc(dve_step, 1)
                dve.wait_ge(dve_step, next_step())
            T = cand[:, ROUNDS, 0:1]
            v.tensor_scalar(GT[:, :], R[:, :], T, None, ALU.is_gt, ALU.add, accum_out=tot[:, 0:1])\
                .then_inc(sel_pe, 1)
            v.tensor_scalar(EQ[:, :], R[:, :], T, None, ALU.is_equal, ALU.add, accum_out=tot[:, 1:2])\
                .then_inc(sel_pe, 1)
            dve.wait_ge(sel_pe, 2)
            v.tensor_tensor_scan(SG[:, :], ones[:, 0:1].to_broadcast([P, CT]), GT[:, :], 0.0, ALU.mult, ALU.add)\
                .then_inc(dve_step, 1)
            dve.wait_ge(dve_step, next_step())
            v.tensor_tensor_scan(SE[:, :], ones[:, 0:1].to_broadcast([P, CT]), EQ[:, :], 0.0, ALU.mult, ALU.add)\
                .then_inc(dve_step, 1)
            dve.wait_ge(dve_step, next_step())
            dve.wait_ge(pos_done, 1)
            v.tensor_copy(offs[:, :], MI[:, 0:4]).then_inc(dve_step, 1)
            dve.wait_ge(dve_step, next_step())
            v.tensor_scalar(need[:, 0:1], offs[:, 2:3], -1.0, float(KEEP), ALU.mult, ALU.add).then_inc(dve_step, 1)
            dve.wait_ge(dve_step, next_step())
            v.tensor_tensor(need[:, 1:2], need[:, 0:1], offs[:, 1:2], ALU.subtract).then_inc(dve_step, 1)
            dve.wait_ge(dve_step, next_step())
            v.scalar_tensor_tensor(W1[:, :], SE[:, :], need[:, 1:2], EQ[:, :], ALU.is_le, ALU.mult)\
                .then_inc(dve_step, 1)
            dve.wait_ge(dve_step, next_step())
            v.tensor_tensor(W2[:, :], GT[:, :], W1[:, :], ALU.add).then_inc(dve_step, 1)
            dve.wait_ge(dve_step, next_step())
            v.tensor_scalar(W3[:, :], SE[:, :], offs[:, 1:2], need[:, 0:1], ALU.add, ALU.min).then_inc(dve_step, 1)
            dve.wait_ge(dve_step, next_step())
            v.scalar_tensor_tensor(W4[:, :], SG[:, :], offs[:, 0:1], W3[:, :], ALU.add, ALU.add).then_inc(dve_step, 1)
            dve.wait_ge(dve_step, next_step())
            v.tensor_scalar(W5[:, :], W4[:, :], cc("gap_from"), float(GAP), ALU.is_gt, ALU.mult).then_inc(dve_step, 1)
            dve.wait_ge(dve_step, next_step())
            v.tensor_tensor(W3[:, :], W4[:, :], W5[:, :], ALU.add).then_inc(dve_step, 1)
            dve.wait_ge(dve_step, next_step())
            v.scalar_tensor_tensor(W1[:, :], W3[:, :], -1.0 - NOT_KEPT, W2[:, :], ALU.add, ALU.mult)\
                .then_inc(dve_step, 1)
            dve.wait_ge(dve_step, next_step())
            v.tensor_scalar(W5[:, :], W1[:, :], NOT_KEPT, None, ALU.add).then_inc(pos_ready, 1)
            dve.wait_ge(pos_done, 2)
            v.tensor_copy(posI[:, :], MI[:, 0:CT]).then_inc(dve_step, 1)
            dve.wait_ge(dve_step, next_step())
            v.tensor_single_scalar(rI[:, :], posI[:, :], P - 1, ALU.bitwise_and).then_inc(dve_step, 1)
            dve.wait_ge(dve_step, next_step())
            v.tensor_single_scalar(aI[:, :], posI[:, :], 7, ALU.logical_shift_right).then_inc(dve_step, 1)
            dve.wait_ge(dve_step, next_step())
            v.tensor_copy(rF[:, :, :].rearrange("p t h -> p (t h)"), rI[:, :]).then_inc(pos_ready, 1)
            v.tensor_copy(aF[:, :, :].rearrange("p t h -> p (t h)"), aI[:, :]).then_inc(pos_ready, 1)

            def index(i, b, pos):
                dve.wait_ge(idx_mm, i + 1)
                if i >= 2:
                    dve.wait_ge(gathered, 16 * STEPS * (i - 1))
                v.scalar_tensor_tensor(idx[:, b, :], bank(pos)[:, 0:STEPS], float(H),
                                       row_add[:, STEPS * i:STEPS * (i + 1)],
                                       ALU.mult, ALU.add).then_inc(idx_ready, 1)

            def maximum(i, b, u, pos):
                e, half = u // 32, u % 2
                a, z = SCORE_COLS[e][half]
                dve.wait_ge(s_filled, SUNITS * i + u + 1)
                v.tensor_reduce(MXU[:, b, u:u + 1], bank(pos)[:, 0:z - a], AX.X, ALU.max)\
                    .then_inc(s_reduced, 1)

            def split_max(i, b, e):
                k = 5 * (2 * i + e)
                dve.wait_ge(s_reduced, SUNITS * i + 32 * (e + 1))
                v.tensor_reduce(NM[:, 0, 0:NT], MXU[:, b, 32 * e:32 * e + 32].rearrange("p (n two) -> p n two", two=2),
                                AX.X, ALU.max, negate=True).then_inc(m_chain, 1)
                dve.wait_ge(m_chain, k + 1)
                if i >= 1:
                    dve.wait_ge([mtr_even, mtr_odd][e], i)
                for part in range(PARTS - 1):
                    v.tensor_copy(SM[:, e, part, :], NM[:, part, 0:NT]).then_inc(m_chain, 1)
                    dve.wait_ge(m_chain, k + 2 * part + 2)
                    v.tensor_tensor(NM[:, part + 1, 0:NT], NM[:, part, 0:NT], SM[:, e, part, :], ALU.subtract)\
                        .then_inc(m_chain, 1)
                    dve.wait_ge(m_chain, k + 2 * part + 3)
                v.tensor_copy(SM[:, e, 2, :], NM[:, 2, 0:NT]).then_inc([m_split_even, m_split_odd][e], 1)

            def copy_mt(i, e, pos):
                dve.wait_ge([mtr_even, mtr_odd][e], i + 1)
                if i >= 1:
                    dve.wait_ge([mrow_even, mrow_odd][e], 16 * i)
                v.tensor_copy(MT[:, e, :], bank16(pos)[0:PARTS * NT, 0:P]).then_inc([mt_even, mt_odd][e], 1)

            def copy_kt(i, b, pos):
                dve.wait_ge(ktr_done, i + 1)
                v.tensor_copy(KTM[0:64, b, 0:7 * P], bank16(pos)[0:64, 0:7 * P]).then_inc(kt_even, 1)

            def copy_kte(i, b):
                dve.wait_ge(kt_odd, i + 1)
                dve.wait_ge(kt_even, i + 1)
                if i >= 2:
                    dve.wait_ge(st_filled, 2 * STEPS * (i - 1))
                v.tensor_copy(KTE[:, b, :], KTM[:, b, :]).then_inc(kte_ready, 1)

            def normalize(i, pos):
                dve.wait_ge(otr_done, i + 1)
                t = bank(pos).rearrange("p (b g c) -> p b g c", b=4, g=4)
                if i >= 1:
                    dve.wait_ge(o_norm, 2 * i)
                v.reciprocal(REC[:, :, :, :], t[:, :, :, D::16]).then_inc(rec_ready, 1)
                dve.wait_ge(rec_ready, i + 1)
                for e in range(2):
                    dst = AT[:, :, (2 * i + e) * D:(2 * i + e + 1) * D].rearrange("p (g b) d -> p b g d", g=4)
                    v.tensor_tensor(dst, t[:, :, :, 16 * e:16 * e + D],
                                    REC[:, :, :, e:e + 1].to_broadcast([P, 4, 4, D]), ALU.mult)\
                        .then_inc(o_norm, 1)

            def onehot(i, b):
                for e in range(2):
                    for t in range(NT):
                        last = v.tensor_scalar(A1[:, b, e, t, :], place16[:, :], rF[:, t, 2 * i + e:2 * i + e + 1],
                                               None, ALU.is_equal)
                last.then_inc(onehot_ready, 1)

            def columns(h0, h1):
                for h in range(h0, h1):
                    e = h % 2
                    v.tensor_tensor(B0[:, h, :, :], aF[:, :, h:h + 1].to_broadcast([P, NT, BLOCKS]),
                                    blocks[:, BLOCKS * e:BLOCKS * (e + 1)].rearrange("p (a n) -> p a n", a=1)
                                    .to_broadcast([P, NT, BLOCKS]), ALU.is_equal).then_inc(b_parts, 1)
                dve.wait_ge(b_parts, h1)
                last = v.tensor_tensor(B1[:, h0:h1, :, :], B0[:, h0:h1, :, :],
                                       token.rearrange("p (a t b) -> p a t b", a=1, b=1)
                                       .to_broadcast([P, h1 - h0, NT, BLOCKS]), ALU.mult)
                last.then_inc(onehot_ready, 1)

            dve.wait_ge(pos_ready, 3)
            columns(0, 2)
            onehot(0, 0)
            index(0, 0, 0)
            onehot(1, 1)
            columns(2, H)
            index(1, 1, 1)
            copy_kt(0, 0, 2)
            copy_kte(0, 0)
            for n, kind in enumerate(LEAD_UNITS):
                if kind == "turn_m_even":
                    copy_mt(0, 0, n)
                else:
                    if kind == 32:
                        split_max(0, 0, 0)
                    maximum(0, 0, kind, n)
            copy_kt(1, 1, KT1_POS)
            for i in range(NP):
                b = i % 2
                last_pair = i + 1 == NP
                for pos, kind in enumerate(UNITS):
                    if kind == "turn_o":
                        if i >= 1:
                            normalize(i - 1, pos)
                    elif kind == "index":
                        if i + 2 < NP:
                            index(i + 2, b, pos)
                    elif kind == "turn_m_odd":
                        copy_mt(i, 1, pos)
                        if not last_pair:
                            copy_kte(i + 1, 1 - b)
                    elif kind == "turn_m_even":
                        if not last_pair:
                            copy_mt(i + 1, 0, pos)
                    elif kind == "turn_k":
                        if i + 2 < NP:
                            copy_kt(i + 2, b, pos)
                    else:
                        u = LEAD + kind
                        if u < SUNITS:
                            maximum(i, b, u, pos)
                            if u == SUNITS - 1:
                                split_max(i, b, 1)
                        elif not last_pair:
                            maximum(i + 1, 1 - b, u - SUNITS, pos)
                            if u - SUNITS == 31:
                                split_max(i + 1, 1 - b, 0)
            normalize(NP - 1, 0)
            next_tail = itertools.count(1).__next__

            def residual_and_stats(g):
                dve.wait_ge(gated, g + 1)
                v.tensor_tensor(X2[:, 4 * g:4 * g + 4, :], GAT[:, 4 * g:4 * g + 4, :], X[:, 4 * g:4 * g + 4, :],
                                ALU.add).then_inc(x2_ready, 1)
                dve.wait_ge(x2_ready, g + 1)
                for t in range(4 * g, 4 * g + 4):
                    v.bn_stats(stats[:, t, :], X2[:, t, :]).then_inc(stats2_ready, 1)
                for t in range(4 * g, 4 * g + 4):
                    dve.wait_ge(stats2_ready, 8 * g + t - 4 * g + 1)
                    v.bn_aggr(mv[:, t, :], stats[:, t, :]).then_inc(stats2_ready, 1)

            def normalize2(g):
                dve.wait_ge(std2_ready, g + 1)
                v.reciprocal(rstd[:, 4 * g:4 * g + 4], std[:, 4 * g:4 * g + 4]).then_inc(tail_step, 1)
                dve.wait_ge(tail_step, next_tail())
                for t in range(4 * g, 4 * g + 4):
                    v.tensor_scalar(XN2[:, t, :], X2[:, t, :], mv[:, t, 0:1], rstd[:, t:t + 1], ALU.subtract,
                                    ALU.mult).then_inc(xn2_ready, 1)

            residual_and_stats(0)
            for g in range(1, 4):
                residual_and_stats(g)
                normalize2(g - 1)
            normalize2(3)
            dve.wait_ge(route_done, 1)

            def te(ap):
                return ap.rearrange("p (t e) -> p t e", e=NE)

            def bc(ap):
                return ap.rearrange("p (t a) -> p t a", a=1).to_broadcast([P, NT, NE])

            LG = OP[:, 0:NT * NE]
            v.tensor_reduce(LM[:, 0, :], te(LG), AX.X, ALU.max).then_inc(tail_dve, 1)
            dve.wait_ge(tail_dve, 1)
            v.tensor_tensor(te(LE[:, 0, :]), te(LG), bc(LM[:, 0, :]), ALU.subtract).then_inc(tail_dve, 1)
            dve.wait_ge(exp2_done, 1)
            v.tensor_reduce(LM[:, 1, :], te(LE[:, 1, :]), AX.X, ALU.add).then_inc(tail_step, 1)
            dve.wait_ge(tail_step, next_tail())
            v.reciprocal(LM[:, 2, :], LM[:, 1, :]).then_inc(tail_step, 1)
            dve.wait_ge(tail_step, next_tail())
            v.tensor_tensor(te(LE[:, 2, :]), te(LE[:, 1, :]), bc(LM[:, 2, :]), ALU.mult).then_inc(tail_step, 1)
            dve.wait_ge(tail_step, next_tail())
            v.tensor_reduce(LM[:, 3, :], te(LE[:, 2, :]), AX.X, ALU.max).then_inc(tail_step, 1)
            dve.wait_ge(tail_step, next_tail())
            v.tensor_tensor(te(LE[:, 3, :]), te(LE[:, 2, :]), bc(LM[:, 3, :]), ALU.is_equal).then_inc(tail_step, 1)
            dve.wait_ge(tail_step, next_tail())
            expert = cc("expert").rearrange("p (e t) -> p t e", e=NE)
            v.tensor_tensor(te(LE[:, 4, :]), te(LE[:, 3, :]), expert, ALU.mult).then_inc(tail_step, 1)
            dve.wait_ge(tail_step, next_tail())
            v.tensor_reduce(slotF[:, :], te(LE[:, 4, :]), AX.X, ALU.min).then_inc(tail_step, 1)
            dve.wait_ge(tail_step, next_tail())
            v.tensor_tensor(OH[:, :, :].rearrange("p e t -> p t e"), expert, bc(slotF[:, :]), ALU.is_equal)\
                .then_inc(tail_step, 1)
            dve.wait_ge(tail_step, next_tail())
            v.tensor_copy(OHB[:, :], OH[:, :, :].rearrange("p e t -> p (e t)")).then_inc(oh_ready, 1)
            dve.wait_ge(rank_done, 1)
            RANK = OP[:, 0:P]
            v.tensor_copy(TOT[:, :, :].rearrange("p e t -> p (e t)"), OP[:, P:2 * P]).then_inc(tail_step, 1)
            dve.wait_ge(tail_step, next_tail())
            v.tensor_tensor_scan(CUM[:, 1:], ones[:, 0:NE * NT], TOT[:, :, :].rearrange("p e t -> p (e t)"), 0.0,
                                 ALU.mult, ALU.add).then_inc(tail_step, 1)
            dve.wait_ge(tail_step, next_tail())
            ends = CUM[:, NT::NT]
            starts = CUM[:, 0:NE * NT:NT]
            v.tensor_tensor(EN[:, 0, :], ends, starts, ALU.subtract).then_inc(tail_step, 1)
            dve.wait_ge(tail_step, next_tail())
            v.tensor_scalar(EN[:, 1, :], EN[:, 0, :], P - 1.0, None, ALU.add).then_inc(tail_step, 1)
            dve.wait_ge(tail_step, next_tail())
            v.tensor_copy(ENI[:, 0, :], EN[:, 1, :]).then_inc(tail_step, 1)
            dve.wait_ge(tail_step, next_tail())
            v.tensor_single_scalar(ENI[:, 1, :], ENI[:, 0, :], 7, ALU.logical_shift_right).then_inc(tail_step, 1)
            dve.wait_ge(tail_step, next_tail())
            v.tensor_copy(EN[:, 2, :], ENI[:, 1, :]).then_inc(tail_step, 1)
            dve.wait_ge(tail_step, next_tail())
            v.tensor_tensor_scan(EN[:, 3, :], ones[:, 0:NE], EN[:, 2, :], 0.0, ALU.mult, ALU.add)\
                .then_inc(tail_step, 1)
            dve.wait_ge(tail_step, next_tail())
            v.tensor_tensor(TE[:, :, :], cc("slot_tile").rearrange("p (s e) -> p s e", e=NE),
                            EN[:, 3:4, :].to_broadcast([P, SLOT_TILES, NE]), ALU.is_ge).then_inc(tail_step, 1)
            dve.wait_ge(tail_step, next_tail())
            v.tensor_reduce(TEF[:, :], TE[:, :, :], AX.X, ALU.add).then_inc(tail_step, 1)
            dve.wait_ge(tail_step, next_tail())
            v.tensor_scalar(TEI[:, :], TEF[:, :], NE - 1.0, None, ALU.min).then_inc(tile_ready, 1)
            v.tensor_tensor(EN[:, 4, :], EN[:, 3, :], EN[:, 2, :], ALU.subtract).then_inc(tail_step, 1)
            dve.wait_ge(tail_step, next_tail())
            v.scalar_tensor_tensor(EN[:, 5, :], EN[:, 4, :], float(P), starts, ALU.mult, ALU.subtract)\
                .then_inc(tail_step, 1)
            dve.wait_ge(tail_step, next_tail())
            v.tensor_tensor(SLB[:, :, :].rearrange("p e t -> p (e t)"), CUM[:, 0:NE * NT], RANK, ALU.add)\
                .then_inc(tail_step, 1)
            dve.wait_ge(tail_step, next_tail())
            v.tensor_tensor(SLC[:, :, :], SLB[:, :, :],
                            EN[:, 5, :].rearrange("p (e a) -> p e a", a=1).to_broadcast([P, NE, NT]), ALU.add)\
                .then_inc(tail_step, 1)
            dve.wait_ge(tail_step, next_tail())
            v.tensor_tensor(SLB[:, :, :], SLC[:, :, :], OH[:, :, :], ALU.mult).then_inc(tail_step, 1)
            dve.wait_ge(tail_step, next_tail())
            v.tensor_reduce(slotF[:, :], SLB[:, :, :].rearrange("p e t -> p t e"), AX.X, ALU.add)\
                .then_inc(tail_step, 1)
            dve.wait_ge(tail_step, next_tail())
            v.tensor_copy(slot[:, :], slotF[:, :]).then_inc(slot_ready, 1)
            dve.wait_ge(tile_ready, 1)
            dve.wait_ge(we_in, 32)
            def expert_of(n):
                return dve.value_load(TEI[0:1, bass.ds(n, 1)], min_val=0, max_val=NE - 1)

            def take_fc(n, b, e):
                if not isinstance(n, int) or n >= 2:
                    dve.wait_ge(up_done, n - 1)
                v.tensor_copy(WFC[:, b, :], WE[:, bass.ds(e, 1), 0:HD].rearrange("p a c -> p (a c)"))\
                    .then_inc(fc_ready, 1)

            def take_proj(n, b, e):
                if not isinstance(n, int) or n >= 2:
                    dve.wait_ge(down_done, n - 1)
                v.tensor_copy(WPROJ[:, b, :], WE[:, bass.ds(e, 1), HD:].rearrange("p a c -> p (a c)"))\
                    .then_inc(proj_ready, 1)

            def square(n, b):
                dve.wait_ge(relu_done, n + 1)
                if not isinstance(n, int) or n >= 2:
                    dve.wait_ge(down_done, n - 1)
                v.tensor_tensor(R2[:, b, :], RL[:, b, :], RL[:, b, :], ALU.mult).then_inc(sq_done, 1)

            for n in range(2):
                e = expert_of(n)
                take_fc(n, n, e)
                take_proj(n, n, e)
            square(0, 0)
            with dve.Fori(2, SLOT_TILES - 1, 2) as n:
                for b in range(2):
                    e = expert_of(n + b)
                    take_fc(n + b, b, e)
                    square(n + b - 1, 1 - b)
                    take_proj(n + b, b, e)
            square(SLOT_TILES - 1, 1)
            for g in range(4):
                dve.wait_ge([y_back_0, y_back_1, y_back_2, y_back_3][g], 16 * 4)
                t4 = slice(4 * g, 4 * g + 4)
                v.tensor_tensor(H2T.rearrange("p (t e) -> p t e", e=E)[:, t4, :], YG[:, t4, :],
                                gate[:, 1:2, :].to_broadcast([P, 4, E]), ALU.mult).then_inc(tail_step, 1)
                dve.wait_ge(tail_step, next_tail())
                v.tensor_tensor(GAT[:, t4, :], H2T.rearrange("p (t e) -> p t e", e=E)[:, t4, :], X2[:, t4, :],
                                ALU.add).then_inc(out_ready, 1)

        @block.tensor
        def _(pe):
            mm = nc.tensor.matmul
            pe.wait_ge(const_in, 16)
            pe.wait_ge(silu_ready, 2)
            pe.wait_ge(init_dve, 1)
            for c in range(6):
                last = mm(OP[:, c:c + 1], WMOD[:, P * c:P * c + P], silu[:, :], start=True, stop=True)
            for a, c in ((0, 2), (1, 5)):
                last = mm(OP[:, P + P * a:2 * P + P * a], silu_b[:, :], WMOD[:, P * c:P * c + P], start=True, stop=True)
            last.then_inc(mod_done, 1)
            for g in range(4):
                for t in range(4 * g, 4 * g + 4):
                    pe.wait_ge(xn_ready, t + 1)
                    last = nc.tensor.transpose(ST[:, g // 2, 512 * (g % 2) + P * (t % 4):512 * (g % 2) + P * (t % 4) + P],
                                               XN[:, t, :], ident)
                last.then_inc(xt_done, 1)
            for j in range(4):
                pe.wait_ge(ht_ready, j + 1)
                last = mm(SC[32 * j:32 * j + RH, 0, :], WR1[:, :], HT[:, 512 * j:512 * j + 512], start=True, stop=True)
            last.then_inc(h1_done, 1)
            pe.wait_ge(wr2_in, 16 * 8)
            pe.wait_ge(h1_ready, 1)
            mm(SC[:, 1, 0:CT], WR2[:, 0, :], H1[:, 0:CT], start=True, stop=False)
            mm(SC[:, 1, 0:CT], WR2[:, 1, :], H1[:, CT:2 * CT], start=False, stop=True).then_inc(logit_done, 1)
            for g in range(4):
                mm(ST[:, g // 2, 512 * (g % 2):512 * (g % 2) + 512], WQ[:, :], HT[:, 512 * g:512 * g + 512],
                   start=True, stop=True).then_inc(q_done, 1)
            pe.wait_ge(gate_ready, 1)

            def kv(n):
                if n >= 2:
                    pe.wait_ge(kv_ready, n - 1)
                to = [OP[:, :], MI][n % 2]
                for t in range(2):
                    o = to[:, 2 * E * t:2 * E * t + 2 * E]
                    mm(o, ones[0:1, :], BKV[0:1, :], start=True, stop=False)
                    last = mm(o, HT[:, P * (2 * n + t):P * (2 * n + t) + P], WKV[:, :], start=False, stop=True)
                last.then_inc(kv_done, 1)

            pe.wait_ge(score0, 2)
            for r in range(ROUNDS):
                pe.wait_ge(search_dve, 3 * (r + 1))
                mm(SC[:, r % 2, 0:3], same_head, cnt[:, r, :], start=True, stop=True).then_inc(search_pe, 1)
                if r < NT // 2:
                    kv(r)
            pe.wait_ge(kv_ready, NT // 2)
            pe.wait_ge(sel_pe, 2)
            mm(MI[:, 0:2], before, tot[:, :], start=True, stop=True)
            mm(MI[:, 2:4], same_head, tot[:, :], start=True, stop=True).then_inc(pos_done, 1)
            pe.wait_ge(pos_ready, 1)
            for u in range(2):
                last = nc.tensor.transpose(MI[:, P * u:P * u + P], W5[:, P * u:P * u + P], ident)
            last.then_inc(pos_done, 1)

            def index_mm(i, b, pos):
                pe.wait_ge(onehot_ready, 2 if i == 0 else i + 3)
                for e in range(2):
                    for t in range(NT):
                        last = mm(bank(pos)[:, 6 * e:6 * e + BLOCKS], A1[:, b, e, t, :], B1[:, 2 * i + e, t, :],
                                  start=(e == 0 and t == 0), stop=(e == 1 and t == NT - 1), skip_group_check=True)
                last.then_inc(idx_mm, 1)

            def turn_k(i, b, pos):
                pe.wait_ge(prep_ready, i + 1)
                for s in range(STEPS):
                    col = STEP_COLUMN[s]
                    if s <= 6:
                        o = bank16(pos)[0:64, P * col:P * col + P]
                        last = nc.tensor.transpose(o, RS[:, b, 0:64] if s == 6 else KS[:, b, s, :], identb[:, :])
                    if s >= 6:
                        o = bank16(pos)[64:128, P * (col - 6):P * (col - 6) + P]
                        last = nc.tensor.transpose(o, RS[:, b, 64:128] if s == 6 else KS[:, b, s, :], identb[:, :])
                last.then_inc(ktr_done, 1)

            def turn_m(i, e, pos):
                pe.wait_ge([m_split_even, m_split_odd][e], i + 1)
                nc.tensor.transpose(bank16(pos)[0:PARTS * NT, 0:P], SM[:, e, :, :].rearrange("p a t -> p (a t)"),
                                    identb[:, :]).then_inc([mtr_even, mtr_odd][e], 1)

            def turn_o(i, pos):
                pe.wait_ge(o_copied, i + 1)
                for q in range(4):
                    last = nc.tensor.transpose(bank(pos)[:, P * q:P * q + P], OS[:, P * q:P * q + P], ident)
                last.then_inc(otr_done, 1)

            def score_tile(i, b, u, pos):
                e, qt, half = u // 32, u % 32 // 2, u % 2
                a, z = SCORE_COLS[e][half]
                mm(bank(pos)[:, 0:z - a], QSM[:, b, P * qt:P * qt + P], KTM[:, b, a:z],
                   start=True, stop=True).then_inc(s_filled, 1)

            def free_bank(i, pos):
                while True:
                    pos -= RING
                    if pos < 0:
                        i, pos = i - 1, pos + len(UNITS)
                    kind = UNITS[pos]
                    if i < 0:
                        pe.wait_ge(s_reduced, LEAD - len(UNITS) + pos + 1)
                    elif done(i, kind) or (kind == "turn_o" and i == 0):
                        continue
                    elif kind == "turn_o":
                        pe.wait_ge(o_norm, 2 * i)
                    elif kind == "index":
                        pe.wait_ge(idx_ready, i + 3)
                    elif kind == "turn_k":
                        pe.wait_ge(kt_odd, i + 3)
                        pe.wait_ge(kt_even, i + 3)
                    elif kind == "turn_m_odd":
                        pe.wait_ge(mt_odd, i + 1)
                    elif kind == "turn_m_even":
                        pe.wait_ge(mt_even, i + 2)
                    else:
                        pe.wait_ge(s_reduced, SUNITS * i + LEAD + kind + 1)
                    return

            def scores(i, b, s, c):
                half = c // 2
                n = 2 * (STEPS * i + s) + half
                if n >= 2 and c % 2 == 0:
                    pe.wait_ge(exp_done, n - 1)
                col = STEP_COLUMN[s]
                rows = 64 + KROWS if s < 6 else P
                last = mm(ST[:, half, 512 * (c % 2):512 * (c % 2) + 512], KTE[0:rows, b, P * col:P * col + P],
                          QSE[0:rows, b, 512 * c:512 * c + 512], start=True, stop=True)
                if c % 2:
                    last.then_inc(st_filled, 1)

            def weigh_v(i, b, s):
                n = STEPS * i + s
                pe.wait_ge(exp_done, 2 * n + 2)
                if s == 0:
                    pe.wait_ge(v_ready, i + 1)
                    if i >= 1:
                        pe.wait_ge(o_copied, i)
                for g in range(4):
                    last = mm(OP[32 * g:32 * g + 32, :], VS[:, b, s, :], PR[:, n % 2, 512 * g:512 * g + 512],
                              start=(s == 0), stop=(s == STEPS - 1))
                last.then_inc(pv_done, 1)

            def done(i, kind):
                if kind in ("index", "turn_k"):
                    return i + 2 >= NP
                if kind == "turn_m_odd" or kind == "turn_o":
                    return False
                return i + 1 >= NP and (kind == "turn_m_even" or LEAD + kind >= SUNITS)

            def unit(i, b, pos):
                kind = UNITS[pos]
                last_pair = i + 1 == NP
                if done(i, kind):
                    return
                free_bank(i, pos)
                if kind == "turn_o":
                    if i >= 1:
                        turn_o(i - 1, pos)
                elif kind == "index":
                    if i + 2 < NP:
                        index_mm(i + 2, b, pos)
                elif kind == "turn_k":
                    if i + 2 < NP:
                        turn_k(i + 2, b, pos)
                elif kind == "turn_m_odd":
                    turn_m(i, 1, pos)
                elif kind == "turn_m_even":
                    if not last_pair:
                        turn_m(i + 1, 0, pos)
                else:
                    u = LEAD + kind
                    if u < SUNITS:
                        score_tile(i, b, u, pos)
                    elif not last_pair:
                        if u == SUNITS:
                            pe.wait_ge([qsm_even, qsm_odd][1 - b], 16 * 6 * ((i + 1) // 2 + 1))
                            pe.wait_ge(kt_odd, i + 2)
                            pe.wait_ge(kt_even, i + 2)
                        score_tile(i + 1, 1 - b, u - SUNITS, pos)

            index_mm(0, 0, 0)
            pe.wait_ge(pos_ready, 3)
            index_mm(1, 1, 1)
            turn_k(0, 0, 2)
            pe.wait_ge(kt_odd, 1)
            pe.wait_ge(kt_even, 1)
            pe.wait_ge(idx_ready, 2)
            pe.wait_ge(qsm_even, 16 * 6)
            for n, kind in enumerate(LEAD_UNITS):
                if n >= RING:
                    before_it = LEAD_UNITS[n - RING]
                    if before_it == "turn_m_even":
                        pe.wait_ge(mt_even, 1)
                    else:
                        pe.wait_ge(s_reduced, before_it + 1)
                if kind == "turn_m_even":
                    turn_m(0, 0, n)
                else:
                    score_tile(0, 0, kind, n)
            pe.wait_ge(s_reduced, LEAD)
            turn_k(1, 1, KT1_POS)
            pe.wait_ge(kt_odd, 2)
            pe.wait_ge(kt_even, 2)
            for i in range(NP):
                b = i % 2
                last_pair = i + 1 == NP
                pe.wait_ge(kte_ready, i + 1)
                pe.wait_ge([qse_even, qse_odd][b], 16 * 6 * (i // 2 + 1))
                pe.wait_ge(mrow_even, 16 * (i + 1))
                if i == 0:
                    pe.wait_ge(init_dve, 1)
                at_unit = 0
                for s in range(STEPS):
                    if s == 6:
                        pe.wait_ge(mrow_odd, 16 * (i + 1))
                    pieces = [("scores", c) for c in range(4)] + ([("weigh", s - 1)] if s else [])
                    upto = len(UNITS) * (s + 1) // STEPS
                    n_units = upto - at_unit
                    for n, (piece, arg) in enumerate(pieces):
                        if piece == "scores":
                            scores(i, b, s, arg)
                        else:
                            weigh_v(i, b, arg)
                        stop = upto if n == len(pieces) - 1 else at_unit + 1
                        while at_unit < stop:
                            unit(i, b, at_unit)
                            at_unit += 1
                weigh_v(i, b, STEPS - 1)
            pe.wait_ge(s_reduced, SUNITS * NP)
            pe.wait_ge(o_norm, 2 * (NP - 1))
            pe.wait_ge(mt_odd, NP)
            turn_o(NP - 1, 0)
            for g in range(4):
                for t in range(4 * g, 4 * g + 4):
                    pe.wait_ge(xn2_ready, t + 1)
                    c0 = 512 * (g % 2) + P * (t % 4)
                    last = nc.tensor.transpose(ST[:, g // 2, c0:c0 + P], XN2[:, t, :], ident)
                last.then_inc(xt2_done, 1)
            for t in range(NT):
                pe.wait_ge(h2_ready, t // 4 + 1)
                last = mm(OP[:, NE * t:NE * t + NE], H2T[:, P * t:P * t + P], WROUTE[:, :], start=True, stop=True)
            last.then_inc(route_done, 1)
            pe.wait_ge(oh_ready, 1)
            mm(OP[:, 0:P], lowerb[:, :], OHB[:, :], start=True, stop=True)
            mm(OP[:, P:2 * P], onesb[:, :], OHB[:, :], start=True, stop=True).then_inc(rank_done, 1)
            pe.wait_ge(slots_in, 16)
            for q in range((SLOT_TILES + 3) // 4):
                if q >= 2:
                    pe.wait_ge(hst_ready, q - 1)
                for t in range(4 * q, min(4 * q + 4, SLOT_TILES)):
                    c0 = P * (t % 4)
                    last = nc.tensor.transpose(ST[:, q % 2, c0:c0 + P], HS[:, t, :], ident)
                last.then_inc(hst_done, 1)
            pe.wait_ge(hst_ready, (SLOT_TILES + 3) // 4)

            def up(n, b):
                pe.wait_ge(fc_ready, n + 1)
                if not isinstance(n, int) or n >= 2:
                    pe.wait_ge(relu_done, n - 1)
                for c in range(4):
                    last = mm(SC[:, b, P * c:P * c + P], WFC[:, b, P * c:P * c + P], HT[:, bass.ds(n * P, P)],
                              start=True, stop=True)
                last.then_inc(up_done, 1)

            def down(n, b):
                pe.wait_ge(proj_ready, n + 1)
                pe.wait_ge(sq_done, n + 1)
                if not isinstance(n, int) or n >= 2:
                    pe.wait_ge(y_ready, n - 1)
                for c in range(4):
                    last = mm(ST[:, b, 0:E], R2[:, b, P * c:P * c + P], WPROJ[:, b, P * c:P * c + P],
                              start=(c == 0), stop=(c == 3))
                last.then_inc(down_done, 1)

            pe.wait_ge(o_norm, 2 * NP)
            up(0, 0)
            up(1, 1)
            down(0, 0)
            with pe.Fori(2, SLOT_TILES - 1, 2) as n:
                up(n, 0)
                down(n - 1, 1)
                up(n + 1, 1)
                down(n, 0)
            down(SLOT_TILES - 1, 1)


def kernel(**inputs):
    import numpy as np
    import concourse.bacc as bacc
    from concourse.bass_utils import run_bass_kernel_spmd

    g = {k: np.asarray(v) for k, v in inputs.items()}
    w = g["L0_attn_qkv_w"].T.reshape(E, 3, H, D)
    b = g["L0_attn_qkv_b"].reshape(3, H, D)
    table, _ = constants()
    arrays = {
        "x": g["L0_attn_hidden_states"],
        "w_q": w[:, 0].reshape(E, E),
        "w_kv": w[:, 1:].transpose(0, 2, 1, 3).reshape(E, 2 * E),
        "b_q": b[0].reshape(E, 1),
        "b_kv": b[1:].transpose(1, 0, 2).reshape(1, 2 * E),
        "w_r1": g["L0_attn_r_w1"].T,
        "b_r1": np.tile(g["L0_attn_r_b1"], 4).reshape(P, 1),
        "w_r2": g["L0_attn_r_w2"].T,
        "b_r2": np.tile(g["L0_attn_r_b2"], CHUNKS).reshape(P, 1),
        "c_col": g["L0_c"].reshape(E, 1),
        "wmod": g["L0_wmod"],
        "w_route": g["L0_ffn_router_w"].T,
        "w_fc": g["L0_ffn_expert_fc"],
        "w_proj": g["L0_ffn_expert_proj"].transpose(0, 2, 1).reshape(NE, 4, P, E).transpose(0, 2, 1, 3)
        .reshape(NE, P, HD),
        "const": table,
    }
    nc = bacc.Bacc("TRN2", target_bir_lowering=False, num_devices=1)
    arrays = {f"in_{k}": np.ascontiguousarray(a) for k, a in arrays.items()}
    args = [nc.dram_tensor(k, a.shape, mybir.dt.from_np(a.dtype), kind="ExternalInput").ap() for k, a in arrays.items()]
    args.append(nc.dram_tensor("out_0", (1, L, E), F32, kind="ExternalOutput").ap())
    build(nc, *args)
    r = run_bass_kernel_spmd(nc, [arrays], core_ids=[0])
    return r.results[0]["out_0"]
```

```python
import itertools
from contextlib import ExitStack

import concourse.bass as bass
from concourse import mybir

P = 128
F32 = mybir.dt.float32
BF16 = mybir.dt.bfloat16
FP16 = mybir.dt.float16
I32 = mybir.dt.int32
U32 = mybir.dt.uint32
ALU = mybir.AluOpType
ACT = mybir.ActivationFunctionType
AX = mybir.AxisListType

L = 2048
E = 128
H = 16
D = E // H
KEEP = int(L * 0.4)
NT = L // P
NP = H // 2
RH = E // 4
EPS = 1e-5

REM = KEEP - 6 * P
GAP = P - REM
BLOCKS = 7
SHARED = 3
STEPS = 13
EVEN_ORDER = [0, 1, 2, 4, 5, 6, 3]
ODD_ORDER = [3, 0, 1, 2, 4, 5, 6]
STEP_BLOCK = EVEN_ORDER + ODD_ORDER[1:]
NOT_KEPT = 1023.0
PARTS = 3
KROWS = 6 * D
SROWS = KROWS + PARTS
SUNITS = 64
TURNED = [4, 5, 6, 0, 1, 2]
STEP_COLUMN = [TURNED.index(x) for x in EVEN_ORDER[:6]] + [6] + [7 + TURNED.index(x) for x in ODD_ORDER[1:]]
SCORE_COLS = [[(3 * P, 6 * P + REM), (0, 3 * P)], [(10 * P, 13 * P), (6 * P + GAP, 10 * P)]]
LEAD = 46
UNITS = list(range(SUNITS))
for after, kind in ((55, "turn_k"), (54, "turn_m_even"), (22, "turn_m_odd"), (16, "index"), (8, "turn_o")):
    UNITS.insert(after + 1, kind)
RING = 3
NE = 8
HD = 4 * E
SLOT_TILES = NT + NE
assert len(UNITS) % RING == 0
ROUNDS = 11
CHUNKS = 8
CT = L // CHUNKS


def constants():
    import numpy as np

    p = np.arange(P)
    cols = {}
    cols["ident"] = np.eye(P)
    cols["same_head"] = (p[:, None] % H == p[None, :] % H)
    cols["before"] = (p[:, None] % H == p[None, :] % H) & (p[:, None] // H < p[None, :] // H)
    cols["place"] = np.broadcast_to(p, (P, P))
    u, js = np.arange(NT) // CHUNKS, np.arange(NT) % CHUNKS
    cols["token"] = (CT * js + P * u)[None, :] + p[:, None]
    cols["blocks"] = np.broadcast_to(EVEN_ORDER + ODD_ORDER, (P, 2 * BLOCKS))
    add = np.zeros((P, NP, STEPS))
    for i in range(NP):
        add[:, i, :6] = 2 * i
        add[:, i, 7:] = 2 * i + 1
        add[:, i, 6] = np.where(p < REM, 2 * i, np.where(p >= GAP, 2 * i + 1, 1 << 20))
    cols["row_add"] = add.reshape(P, -1)
    lo = np.where(p % H % 2 == 0, SHARED * P + REM, SHARED * P)
    cols["gap_from"] = lo[:, None]
    holds = ((p < REM) | (p >= GAP))
    cols["holds"] = holds[:, None]
    cols["lower"] = (p[:, None] < p[None, :])
    cols["expert"] = np.broadcast_to(np.repeat(np.arange(NE), NT) - NE, (P, NE * NT))
    cols["slot_tile"] = np.broadcast_to(np.repeat(np.arange(SLOT_TILES), NE), (P, SLOT_TILES * NE))
    st = np.zeros((ROUNDS + 1, 4))
    for r in range(ROUNDS):
        st[r] = np.arange(4) * (2.0 ** -4) * 4.0 ** -r
    cols["steps"] = np.broadcast_to(st.reshape(1, -1), (P, 4 * (ROUNDS + 1)))
    at, n = {}, 0
    for k, v in cols.items():
        at[k] = (n, n + v.shape[1])
        n += v.shape[1]
    table = np.concatenate([np.asarray(v, np.float32) for v in cols.values()], axis=1)
    return np.ascontiguousarray(table), at


def has(i, step):
    return not isinstance(i, int) or 0 <= i + step < NP


def product(engine, factor, i):
    return factor * i if isinstance(i, int) else engine.snap(factor * i)


def build(nc, x, w_q, w_kv, b_q, b_kv, w_r1, b_r1, w_r2, b_r2, c_col, wmod, w_route, w_fc, w_proj, const, out):
    _, at = constants()
    NCONST = const.shape[1]
    q_parts_dram = nc.dram_tensor("q_parts_dram", (H, PARTS, D, L), BF16, kind="Internal").ap()
    kv_dram = nc.dram_tensor("kv_dram", (L * H, 2 * D), F32, kind="Internal").ap()

    slots_dram = nc.dram_tensor("slots_dram", (SLOT_TILES * P, E), F32, kind="Internal").ap()
    y_dram = nc.dram_tensor("y_dram", (SLOT_TILES * P, E), F32, kind="Internal").ap()

    with ExitStack() as ctx:
        def sb(name, shape, dt=F32):
            return ctx.enter_context(nc.sbuf_tensor(name, shape, dt))

        def ps(name, shape, dt=F32):
            return ctx.enter_context(nc.psum_tensor(name, shape, dt))

        def sem(name):
            return ctx.enter_context(nc.semaphore(name))

        X = sb("X", [P, NT, E])
        C = sb("C", [P, NCONST])
        WQ = sb("WQ", [P, E])
        WKV = sb("WKV", [P, 2 * E])
        WR1 = sb("WR1", [P, RH])
        WR2 = sb("WR2", [P, 2, P])
        WR2S = sb("WR2S", [P, H])
        WMOD = sb("WMOD", [P, 6 * E])
        BQ = sb("BQ", [P, 1])
        BKV = sb("BKV", [P, 2 * E])
        BR1 = sb("BR1", [P, 1])
        BR2 = sb("BR2", [P, 1])
        ccol = sb("ccol", [P, 1])
        csig = sb("csig", [P, 1])
        silu = sb("silu", [P, 1])
        silu_b = sb("silu_b", [P, P])
        ones = sb("ones", [P, P])
        eps = sb("eps", [P, 1])
        warmed = sb("warmed", [P, 1])
        mod_col = sb("mod_col", [P, 6])
        one_ca = sb("one_ca", [P, 1])
        stats = sb("stats", [P, NT, 6])
        mv = sb("mv", [P, NT, 2])
        std = sb("std", [P, NT])
        rstd = sb("rstd", [P, NT])
        XN = sb("XN", [P, NT, E])
        HT = sb("HT", [P, SLOT_TILES * P])
        H1 = sb("H1", [P, 512])
        R0 = sb("R0", [P, CT])
        R = sb("R", [P, CT])
        QBUF = sb("QBUF", [P, 3 * L + PARTS * L // 2])
        QF = QBUF[:, 0:L]
        QR = QBUF[:, L:3 * L].rearrange("p (a l) -> p a l", a=2)
        QP = QBUF[:, 3 * L:].bitcast(BF16).rearrange("p (a l) -> p a l", a=PARTS)
        WE = QBUF[:, 0:NE * 2 * HD].rearrange("p (n c) -> p n c", n=NE)
        KV = sb("KV", [P, NT, 2 * E])
        junk = sb("junk", [P, CT])
        cand = sb("cand", [P, ROUNDS + 1, 4])
        cnt = sb("cnt", [P, ROUNDS, 3])
        nge = sb("nge", [P, ROUNDS])
        njunk = sb("njunk", [P, ROUNDS, 3])
        etab = sb("etab", [P, ROUNDS, 4])
        GT = sb("GT", [P, CT])
        EQ = sb("EQ", [P, CT])
        tot = sb("tot", [P, 2])
        offs = sb("offs", [P, 4])
        need = sb("need", [P, 2])
        rF = sb("rF", [P, NT, H])
        aF = sb("aF", [P, NT, H])
        place16 = sb("place16", [P, P], FP16)
        ABUF = sb("ABUF", [P, 2 * L])
        rP = sb("rP", [P, NT])
        rA = sb("rA", [P, NT])
        BP = sb("BP", [P, 2, 2, NT * BLOCKS], FP16)
        apart = sb("apart", [P, NT, P], FP16)
        A1 = ABUF[:, :].bitcast(FP16).rearrange("p (b e t q) -> p b e t q", b=2, e=2, t=NT)
        B1 = sb("B1", [P, H, NT, BLOCKS], FP16)
        idx = sb("idx", [P, 2, STEPS], I32)
        G = sb("G", [P, 2, STEPS, 2 * D])
        KR = sb("KR", [P, 2, 2, STEPS, D])
        KS = sb("KS", [P, 2, STEPS, 64], BF16)
        RS = sb("RS", [P, 2, P], BF16)
        VS = sb("VS", [P, 2, STEPS, 32])
        KTM = sb("KTM", [P, 2, STEPS * P], BF16)
        KTE = sb("KTE", [P, 2, STEPS * P], BF16)
        QSM = sb("QSM", [P, 2, L], BF16)
        QSE = sb("QSE", [P, 2, L], BF16)
        identb = sb("identb", [P, P], BF16)
        MXU = sb("MXU", [P, 2, SUNITS])
        NM = sb("NM", [P, 3, 2 * NT])
        SM = sb("SM", [P, 2, PARTS, NT], BF16)
        MT = sb("MT", [PARTS * NT, 2, P], BF16)
        PR = sb("PR", [P, 2, L])
        work = PR[:, :, :].rearrange("p a (n c) -> p (a n) c", c=CT)
        jnk3 = work[:, 0:3, :]
        SG, SE, W1, W2, W3, W4, W5 = [work[:, 3 + n, :] for n in range(7)]
        posI, rI, aI = [work[:, 10 + n, :].bitcast(I32) for n in range(3)]
        OS = sb("OS", [P, 512])
        REC = sb("REC", [P, 4, 4, 2])
        AT = sb("AT", [P, NT, E])
        gate = sb("gate", [P, 2, E])
        gsign = sb("gsign", [P, 2, E])
        gabs = sb("gabs", [P, 2, E])
        gneg = sb("gneg", [P, 2, E])
        one_cb = sb("one_cb", [P, 1])
        WROUTE = sb("WROUTE", [P, NE])
        lowerb = sb("lowerb", [P, P], BF16)
        onesb = sb("onesb", [P, P], BF16)
        zeros = sb("zeros", [P, E])
        LM = sb("LM", [P, 4, NT])
        LE = KTM[:, 0, 0:2 * 6 * P].bitcast(F32).rearrange("p (a c) -> p a c", a=6)
        OH = sb("OH", [P, NE, NT])
        OHB = sb("OHB", [P, NE * NT], BF16)
        TOT = sb("TOT", [P, NE, NT])
        CUM = sb("CUM", [P, 1 + NE * NT])
        EN = sb("EN", [P, 6, NE])
        ENI = sb("ENI", [P, 2, NE], I32)
        SLB = sb("SLB", [P, NE, NT])
        SLC = sb("SLC", [P, NE, NT])
        slotF = sb("slotF", [P, NT])
        slot = sb("slot", [P, NT], I32)
        TE = KTM[:, 1, 0:2 * SLOT_TILES * NE].bitcast(F32).rearrange("p (s e) -> p s e", e=NE)
        TEF = sb("TEF", [P, SLOT_TILES])
        TEI = sb("TEI", [P, SLOT_TILES], I32)
        B0 = work[:, 0:7, :].rearrange("p n c -> p (n c)").rearrange("p (h t b) -> p h t b", h=H, t=NT)
        X2 = X[:, :, :]
        GAT, XN2 = [ABUF[:, L * n:L * (n + 1)].rearrange("p (t e) -> p t e", e=E) for n in range(2)]
        WB = QSM[:, :, :].bitcast(F32)
        RELU = QSE[:, :, :].bitcast(F32)
        RL, R2 = RELU[:, 0, :].rearrange("p (a c) -> p a c", a=2), RELU[:, 1, :].rearrange("p (a c) -> p a c", a=2)
        WFC, WPROJ = WB[:, :, 0:HD], WB[:, :, HD:]
        YG = XN[:, :, :]
        HS = KV[:, :, :].rearrange("p t c -> p (t c)")[:, 0:SLOT_TILES * P].rearrange("p (t e) -> p t e", e=E)
        H2T = AT[:, :, :].rearrange("p t e -> p (t e)")
        YS = PR[:, :, :].rearrange("p a c -> p (a c)")[:, 0:SLOT_TILES * P].rearrange("p (t e) -> p t e", e=E)

        ST = ps("ST", [P, 2, 1024])
        SC = ps("SC", [P, RING, 512])
        OP = ps("OP", [P, 512])
        MP, MI = SC[:, 1, :], SC[:, 2, :]

        def bank(pos):
            return SC[:, pos % RING, :]

        def bank16(pos):
            return SC[:, pos % RING, :].bitcast(BF16)

        def cc(name):
            a, b = at[name]
            return C[:, a:b]

        ident, same_head, before = cc("ident"), cc("same_head"), cc("before")
        token, blocks, row_add, steps = cc("token"), cc("blocks"), cc("row_add"), cc("steps")

        dve_step = sem("dve_step")
        pool_step = sem("pool_step")
        tail_step = sem("tail_step")
        const_in = sem("const_in")
        x_in = [sem(f"x_in_{g}") for g in range(4)]
        mod_in = sem("mod_in")
        kv_biased = sem("kv_biased")
        warm = sem("warm")
        w_in = sem("w_in")
        wr2_zero = sem("wr2_zero")
        wr2_in = sem("wr2_in")
        silu_ready = sem("silu_ready")
        mod_done = sem("mod_done")
        mod_ready = sem("mod_ready")
        stats_ready = sem("stats_ready")
        std_ready = sem("std_ready")
        xn_ready = sem("xn_ready")
        xt_done = sem("xt_done")
        ht_ready = sem("ht_ready")
        h1_done = sem("h1_done")
        h1_ready = sem("h1_ready")
        logit_done = sem("logit_done")
        score0 = sem("score0")
        q_done = sem("q_done")
        q_ready = sem("q_ready")
        kv_done = sem("kv_done")
        kv_ready = sem("kv_ready")
        qpart_a = sem("qpart_a")
        qpart_p = sem("qpart_p")
        qparts_out = sem("qparts_out")
        kv_out = sem("kv_out")
        search_dve = sem("search_dve")
        search_pe = sem("search_pe")
        sel_pe = sem("sel_pe")
        pos_done = sem("pos_done")
        pos_ready = sem("pos_ready")
        onehot_ready = sem("onehot_ready")
        idx_mm = sem("idx_mm")
        idx_ready = sem("idx_ready")
        gathered = sem("gathered")
        prep_ready = sem("prep_ready")
        v_ready = sem("v_ready")
        places_taken = sem("places_taken")
        rA_ready = sem("rA_ready")
        bp_ready = sem("bp_ready")
        onehot_odd = sem("onehot_odd")
        apart_ready = sem("apart_ready")
        paced = sem("paced")
        turning = sem("turning")
        k_step = sem("k_step")
        v_step = sem("v_step")
        init_pool = sem("init_pool")
        init_dve = sem("init_dve")
        ktr_done = sem("ktr_done")
        kt_odd = sem("kt_odd")
        kt_even = sem("kt_even")
        kte_ready = sem("kte_ready")
        qsm_even = sem("qsm_even")
        qsm_odd = sem("qsm_odd")
        qse_even = sem("qse_even")
        qse_odd = sem("qse_odd")
        s_filled = sem("s_filled")
        s_reduced = sem("s_reduced")
        m_chain = sem("m_chain")
        m_split_even = sem("m_split_even")
        m_split_odd = sem("m_split_odd")
        mtr_even = sem("mtr_even")
        mtr_odd = sem("mtr_odd")
        mt_even = sem("mt_even")
        mt_odd = sem("mt_odd")
        mrow_even = sem("mrow_even")
        mrow_odd = sem("mrow_odd")
        st_filled = sem("st_filled")
        exp_done = sem("exp_done")
        pv_done = sem("pv_done")
        o_copied = sem("o_copied")
        otr_done = sem("otr_done")
        o_norm = sem("o_norm")
        rec_ready = sem("rec_ready")
        out_in = sem("out_in")
        b_parts = sem("b_parts")
        we_in = sem("we_in")
        slots_zero = sem("slots_zero")
        gate_ready = sem("gate_ready")
        tail_dve = sem("tail_dve")
        gated = sem("gated")
        x2_ready = sem("x2_ready")
        stats2_ready = sem("stats2_ready")
        std2_ready = sem("std2_ready")
        xn2_ready = sem("xn2_ready")
        xt2_done = sem("xt2_done")
        h2_ready = sem("h2_ready")
        route_done = sem("route_done")
        exp2_done = sem("exp2_done")
        oh_ready = sem("oh_ready")
        rank_done = sem("rank_done")
        slot_ready = sem("slot_ready")
        scattered = sem("scattered")
        slots_in = sem("slots_in")
        hst_done = sem("hst_done")
        hst_ready = sem("hst_ready")
        fc_ready = sem("fc_ready")
        proj_ready = sem("proj_ready")
        up_done = sem("up_done")
        relu_done = sem("relu_done")
        sq_done = sem("sq_done")
        down_done = sem("down_done")
        y_ready = sem("y_ready")
        y_out = sem("y_out")
        y_back_0 = sem("y_back_0")
        y_back_1 = sem("y_back_1")
        y_back_2 = sem("y_back_2")
        y_back_3 = sem("y_back_3")
        tile_ready = sem("tile_ready")
        out_ready = sem("out_ready")

        block = ctx.enter_context(nc.Block())
        x_t = x[0].rearrange("(t p) e -> p t e", p=P)
        out_t = out[0].rearrange("(t p) e -> p t e", p=P)
        kv_t = kv_dram.rearrange("(t p h) d -> p t (h d)", p=P, h=H)

        LEAD_UNITS = list(range(36)) + ["turn_m_even"] + list(range(36, LEAD))
        KT1_POS = len(LEAD_UNITS) % RING

        @block.sync
        def _(sp):
            for g in range(4):
                sp.dma_start(X[:, 4 * g:4 * g + 4, :], x_t[:, 4 * g:4 * g + 4, :]).then_inc(x_in[g], 16)
                if g == 1:
                    sp.dma_start(C[:, :], const).then_inc(const_in, 16)
            for dst, src in ((WR1, w_r1), (WR2S, w_r2), (BR1, b_r1), (BR2, b_r2), (WQ, w_q), (WKV, w_kv), (BQ, b_q),
                             (BKV, b_kv), (WROUTE, w_route)):
                sp.dma_start(dst[:, :], src).then_inc(w_in, 16)
            sp.wait_ge(qpart_a, 2)
            sp.wait_ge(qpart_p, 2)
            sp.wait_ge(q_ready, 8)
            for part in range(PARTS):
                sp.dma_start(q_parts_dram[:, part, :, :], QP[:, part, :]).then_inc(qparts_out, 16)
            sp.wait_ge(kv_biased, NT // 2)
            sp.dma_start(kv_t, KV[:, :, :]).then_inc(kv_out, 16)
            sp.wait_ge(qparts_out, 16 * PARTS)
            sp.wait_ge(init_pool, 5)

            def load_q(dst, i, par, loaded):
                for e in range(2):
                    src = q_parts_dram[bass.ds(2 * i + e, 1), :, :, :].rearrange("h a d l -> (h a d) l")
                    for row, n in ((0, 3), (3, 2), (5, 1)):
                        sp.dma_start(dst[64 * e + D * row:64 * e + D * (row + n), par, :],
                                     src[0:D * n, :]).then_inc(loaded, 16)

            def m_rows(i, par, e):
                sp.wait_ge([mt_even, mt_odd][e], i + 1)
                dst = QSE[64 * e + KROWS:64 * e + SROWS, par, :].rearrange("a (t q) -> a t q", q=P)
                sp.dma_start(dst, MT[:, e, :]).then_inc([mrow_even, mrow_odd][e], 16)

            def feed(i, b):
                if has(i, 1):
                    if has(i, -1):
                        sp.wait_ge(st_filled, 2 * STEPS * i)
                    load_q(QSE, i + 1, 1 - b, [qse_even, qse_odd][1 - b])
                m_rows(i, b, 1)
                if has(i, 2):
                    sp.wait_ge(s_filled, SUNITS * (i + 1))
                    load_q(QSM, i + 2, b, [qsm_even, qsm_odd][b])
                if has(i, 1):
                    m_rows(i + 1, 1 - b, 0)

            load_q(QSM, 0, 0, qsm_even)
            load_q(QSE, 0, 0, qse_even)
            load_q(QSM, 1, 1, qsm_odd)
            m_rows(0, 0, 0)
            feed(0, 0)
            with sp.Fori(1, NP - 4, 2) as i:
                feed(i, 1)
                feed(i + 1, 0)
            for i in range(NP - 3, NP):
                feed(i, i % 2)
            for n, w_part in enumerate((w_fc, w_proj)):
                sp.dma_start(WE[:, :, HD * n:HD * (n + 1)], w_part.rearrange("n p c -> p n c"))\
                    .then_inc(we_in, 16)
            sp.wait_ge(scattered, 16 * NT)
            slots_t = slots_dram.rearrange("(t p) e -> p t e", p=P)
            y_t = y_dram.rearrange("(t p) e -> p t e", p=P)
            sp.dma_start(HS[:, :, :], slots_t).then_inc(slots_in, 16)
            for q in range(SLOT_TILES // 4):
                sp.wait_ge(y_ready, 4 * q + 4)
                sp.dma_start(y_t[:, 4 * q:4 * q + 4, :], YS[:, 4 * q:4 * q + 4, :]).then_inc(y_out, 16)
            for g in range(4):
                sp.wait_ge(out_ready, g + 1)
                sp.dma_start(out_t[:, 4 * g:4 * g + 4, :], GAT[:, 4 * g:4 * g + 4, :]).then_inc(out_in, 16)
            sp.wait_ge(out_in, 64)
            sp.wait_ge(slots_zero, 16)

        @block.gpsimd
        def _(pool):
            next_step = itertools.count(1).__next__

            nc.gpsimd.memset(WR2[:, :, :], 0.0).then_inc(wr2_zero, 1)
            nc.gpsimd.memset(zeros[:, :], 0.0).then_inc(wr2_zero, 1)
            nc.gpsimd.memset(KS[:, :, :, :], 0.0).then_inc(pool_step, 1)
            pool.wait_ge(pool_step, next_step())
            nc.gpsimd.memset(VS[:, :, :, :], 0.0).then_inc(pool_step, 1)
            pool.wait_ge(pool_step, next_step())
            nc.gpsimd.memset(RS[:, :, :], 0.0).then_inc(init_pool, 1)
            nc.gpsimd.memset(G[:, :, :, :], 0.0).then_inc(init_pool, 1)
            pool.wait_ge(wr2_zero, 2)
            pool.wait_ge(w_in, 16 * 9)
            for j in range(4):
                for u in range(2):
                    c0 = 32 * j + H * u
                    nc.gpsimd.tensor_copy(WR2[32 * j:32 * j + RH, u, c0:c0 + H], WR2S[32 * j:32 * j + RH, :])\
                        .then_inc(wr2_in, 1)
                    pool.wait_ge(wr2_in, 2 * j + u + 1)
            nc.gpsimd.memset(KTM[:, :, :], 0.0).then_inc(init_pool, 1)
            nc.gpsimd.memset(QSM[:, :, :], 0.0).then_inc(init_pool, 1)
            nc.gpsimd.memset(QSE[:, :, :], 0.0).then_inc(init_pool, 1)
            pool.wait_ge(const_in, 16)
            holds = cc("holds")
            for b in range(2):
                nc.gpsimd.memset(KS[:, b, :, KROWS:SROWS], 1.0).then_inc(pool_step, 1)
                pool.wait_ge(pool_step, next_step())
                nc.gpsimd.tensor_copy(KS[:, b, 6, KROWS:SROWS], holds.to_broadcast([P, PARTS])).then_inc(pool_step, 1)
                pool.wait_ge(pool_step, next_step())
                nc.gpsimd.memset(VS[:, b, 0:6, D:D + 1], 1.0).then_inc(pool_step, 1)
                pool.wait_ge(pool_step, next_step())
                nc.gpsimd.memset(VS[:, b, 7:13, 16 + D:16 + D + 1], 1.0).then_inc(pool_step, 1)
                pool.wait_ge(pool_step, next_step())
                nc.gpsimd.tensor_copy(VS[0:64, b, 6, D:D + 1], holds[0:64, :]).then_inc(pool_step, 1)
                pool.wait_ge(pool_step, next_step())
                nc.gpsimd.tensor_copy(VS[64:128, b, 6, 16 + D:16 + D + 1], holds[64:128, :]).then_inc(pool_step, 1)
                pool.wait_ge(pool_step, next_step())
            pool.wait_ge(w_in, 16 * 9)

            def add_bias(n):
                pool.wait_ge(kv_ready, n + 1)
                kv2 = KV[:, 2 * n:2 * n + 2, :]
                nc.gpsimd.tensor_tensor(kv2, kv2, BKV[:, :].rearrange("p (a c) -> p a c", a=1).to_broadcast([P, 2, 2 * E]),
                                        ALU.add).then_inc(kv_biased, 1)

            pool.wait_ge(q_ready, 8)
            nc.gpsimd.tensor_tensor(QR[:, 0, :], QF[:, :], QP[:, 0, :], ALU.subtract).then_inc(qpart_p, 1)
            for n in range(3):
                add_bias(n)
            pool.wait_ge(qpart_a, 1)
            nc.gpsimd.tensor_tensor(QR[:, 1, :], QR[:, 0, :], QP[:, 1, :], ALU.subtract).then_inc(qpart_p, 1)
            for n in range(3, NT // 2):
                add_bias(n)

            pool.wait_ge(kv_out, 16)
            pool.wait_ge(init_pool, 5)

            def onehot(i, b):
                pool.wait_ge(idx_mm, i - 1)
                pool.wait_ge(prep_ready, i)
                pool.sem_inc(paced, 1)
                nc.gpsimd.tensor_copy(rP[:, :], rF[:, :, bass.ds(2 * i, 1)].rearrange("p t a -> p (t a)"))\
                    .then_inc(places_taken, 1)
                pool.wait_ge(places_taken, i - 1)
                pool.sem_inc(paced, 1)
                for t in range(NT):
                    last = nc.gpsimd.tensor_scalar(A1[:, b, 0, t, :], place16[:, :], rP[:, t:t + 1], None, ALU.is_equal)
                last.then_inc(onehot_ready, 1)

            def gathers(i, b):
                pool.wait_ge(idx_ready, i + 1)
                if has(i, -1):
                    pool.wait_ge(v_ready, i)
                    pool.sem_inc(paced, 1)
                for s in range(STEPS):
                    pool.indirect_dma_start(
                        G[:, b, s, :], None, kv_dram, bass.IndirectOffsetOnAxis(ap=idx[:, b, s:s + 1].bitcast(U32), axis=0),
                        bounds_check=L * H - 1, oob_is_err=False).then_inc(gathered, 16)

            def prep(i, b):
                pool.wait_ge(gathered, 16 * STEPS * (i + 1))
                pool.sem_inc(paced, 1)
                k = G[:, b, :, 0:D]
                if has(i, -2):
                    pool.wait_ge(ktr_done, i - 1)
                    pool.sem_inc(paced, 1)

                def rep(ap, n):
                    return ap.rearrange("p s (a d) -> p s a d", a=1).to_broadcast([P, STEPS, n, D])

                def stack(c, n):
                    return KS[:, b, :, D * c:D * (c + n)].rearrange("p s (a d) -> p s a d", a=n)

                nc.gpsimd.tensor_copy(stack(0, 3), rep(k, 3)).then_inc(k_step, 1)
                pool.wait_ge(k_step, 6 * i + 1)
                pool.sem_inc(paced, 1)
                nc.gpsimd.tensor_tensor(KR[:, b, 0, :, :], k, KS[:, b, :, 0:D], ALU.subtract).then_inc(k_step, 1)
                pool.wait_ge(k_step, 6 * i + 2)
                pool.sem_inc(paced, 1)
                nc.gpsimd.tensor_copy(stack(3, 2), rep(KR[:, b, 0, :, :], 2)).then_inc(k_step, 1)
                pool.wait_ge(k_step, 6 * i + 3)
                pool.sem_inc(paced, 1)
                nc.gpsimd.tensor_tensor(KR[:, b, 1, :, :], KR[:, b, 0, :, :], KS[:, b, :, 3 * D:4 * D],
                                        ALU.subtract).then_inc(k_step, 1)
                pool.wait_ge(k_step, 6 * i + 4)
                pool.sem_inc(paced, 1)
                nc.gpsimd.tensor_copy(stack(5, 1), rep(KR[:, b, 1, :, :], 1)).then_inc(k_step, 1)
                pool.wait_ge(k_step, 6 * i + 5)
                pool.sem_inc(paced, 1)
                nc.gpsimd.tensor_copy(RS[0:64, b, 0:64], KS[0:64, b, 6, :]).then_inc(k_step, 1)
                pool.wait_ge(k_step, 6 * i + 6)
                pool.sem_inc(paced, 1)
                nc.gpsimd.tensor_copy(RS[64:128, b, 64:128], KS[64:128, b, 6, :]).then_inc(prep_ready, 1)

            def prep_v(i, b):
                pool.wait_ge(prep_ready, i + 1)
                if has(i, -2):
                    pool.wait_ge(pv_done, STEPS * (i - 1))
                    pool.sem_inc(paced, 1)
                nc.gpsimd.tensor_copy(VS[:, b, 0:6, 0:D], G[:, b, 0:6, D:2 * D]).then_inc(v_step, 1)
                pool.wait_ge(v_step, 3 * i + 1)
                pool.sem_inc(paced, 1)
                nc.gpsimd.tensor_copy(VS[:, b, 7:13, 16:16 + D], G[:, b, 7:13, D:2 * D]).then_inc(v_step, 1)
                pool.wait_ge(v_step, 3 * i + 2)
                pool.sem_inc(paced, 1)
                nc.gpsimd.tensor_copy(VS[0:64, b, 6, 0:D], G[0:64, b, 6, D:2 * D]).then_inc(v_step, 1)
                pool.wait_ge(v_step, 3 * i + 3)
                pool.sem_inc(paced, 1)
                nc.gpsimd.tensor_copy(VS[64:128, b, 6, 16:16 + D], G[64:128, b, 6, D:2 * D])\
                    .then_inc(v_ready, 1)

            gathers(0, 0)
            prep(0, 0)
            prep_v(0, 0)
            gathers(1, 1)
            prep(1, 1)
            onehot(2, 0)
            prep_v(1, 1)
            def prepare(i, b):
                gathers(i, b)
                prep(i, b)
                if has(i, 1):
                    onehot(i + 1, 1 - b)
                prep_v(i, b)

            with pool.Fori(2, NP - 3, 2) as i:
                prepare(i, 0)
                prepare(i + 1, 1)
            for i in range(NP - 2, NP):
                prepare(i, i % 2)
            pool.wait_ge(gate_ready, 1)
            pool.wait_ge(o_norm, 2 * NP)
            for g in range(4):
                nc.gpsimd.tensor_tensor(GAT[:, 4 * g:4 * g + 4, :], AT[:, 4 * g:4 * g + 4, :],
                                        gate[:, 0:1, :].to_broadcast([P, 4, E]), ALU.mult).then_inc(gated, 1)
            pool.wait_ge(slot_ready, 1)
            pool.wait_ge(slots_zero, 16)
            for t in range(NT):
                pool.indirect_dma_start(
                    slots_dram, bass.IndirectOffsetOnAxis(ap=slot[:, t:t + 1].bitcast(U32), axis=0), XN2[:, t, :], None,
                    bounds_check=SLOT_TILES * P - 1, oob_is_err=False).then_inc(scattered, 16)
            def take_fc(n, b):
                e = pool.value_load(TEI[0:1, bass.ds(n, 1)], min_val=0, max_val=NE - 1)
                if not isinstance(n, int):
                    pool.wait_ge(up_done, n - 1)
                    pool.sem_inc(paced, 1)
                nc.gpsimd.tensor_copy(WFC[:, b, :], WE[:, bass.ds(e, 1), 0:HD].rearrange("p a c -> p (a c)"))\
                    .then_inc(fc_ready, 1)

            pool.wait_ge(tile_ready, 1)
            pool.wait_ge(we_in, 32)
            pool.wait_ge(s_filled, SUNITS * NP)
            take_fc(0, 0)
            take_fc(1, 1)
            with pool.Fori(2, SLOT_TILES - 1, 2) as n:
                take_fc(n, 0)
                take_fc(n + 1, 1)
            pool.wait_ge(y_out, 4 * SLOT_TILES)
            for t in range(NT):
                pool.indirect_dma_start(
                    YG[:, t, :], None, y_dram, bass.IndirectOffsetOnAxis(ap=slot[:, t:t + 1].bitcast(U32), axis=0),
                    bounds_check=SLOT_TILES * P - 1, oob_is_err=False).then_inc([y_back_0, y_back_1, y_back_2, y_back_3][t // 4], 16)

        @block.scalar
        def _(act):
            act.dma_start(ccol[:, :], c_col).then_inc(mod_in, 16)
            act.dma_start(WMOD[:, :], wmod).then_inc(mod_in, 16)
            act.wait_ge(mod_in, 32)
            nc.scalar.activation(csig[:, :], ccol[:, :], ACT.Sigmoid).then_inc(silu_ready, 1)
            for g in range(4):
                act.wait_ge(stats_ready, 8 * g + 8)
                nc.scalar.activation(std[:, 4 * g:4 * g + 4], mv[:, 4 * g:4 * g + 4, 1], ACT.Sqrt,
                                     bias=eps[:, 0:1]).then_inc(std_ready, 1)
            nc.scalar.activation(warmed[:, 0:1], ccol[:, :], ACT.Sigmoid).then_inc(warm, 1)
            act.wait_ge(wr2_zero, 2)
            act.dma_start(slots_dram.rearrange("(t p) e -> p t e", p=P),
                          zeros[:, :].rearrange("p (a e) -> p a e", a=1).to_broadcast([P, SLOT_TILES, E]))\
               .then_inc(slots_zero, 16)
            act.wait_ge(mod_ready, 2)
            for g in range(4):
                act.wait_ge(xt_done, g + 1)
                nc.scalar.activation(HT[:, 512 * g:512 * g + 512], ST[:, g // 2, 512 * (g % 2):512 * (g % 2) + 512],
                                     ACT.Identity, bias=mod_col[:, 0:1], scale=one_ca[:, 0:1])\
                    .then_inc(ht_ready, 1)
            act.wait_ge(w_in, 16 * 9)
            act.wait_ge(h1_done, 1)
            nc.scalar.activation(H1[:, :], SC[:, 0, :], ACT.Relu, bias=BR1[:, 0:1]).then_inc(h1_ready, 1)
            act.wait_ge(logit_done, 1)
            nc.scalar.activation(R0[:, :], SC[:, 1, 0:CT], ACT.Sigmoid, bias=BR2[:, 0:1]).then_inc(score0, 1)
            act.wait_ge(score0, 1)
            nc.scalar.activation(junk[:, :], R0[:, :], ACT.Sigmoid).then_inc(score0, 1)
            for g in range(4):
                act.wait_ge(q_done, g + 1)
                src = ST[:, g // 2, 512 * (g % 2):512 * (g % 2) + 512]
                nc.scalar.activation(QF[:, 512 * g:512 * g + 512], src, ACT.Identity, bias=BQ[:, 0:1])\
                    .then_inc(q_ready, 1)
                nc.scalar.activation(QP[:, 0, 512 * g:512 * g + 512], src, ACT.Identity, bias=BQ[:, 0:1])\
                    .then_inc(q_ready, 1)
            act.wait_ge(warm, 1)
            nc.scalar.activation(warmed[:, 0:1], ccol[:, :], ACT.Exp).then_inc(warm, 1)
            for n in range(NT // 2):
                act.wait_ge(kv_done, n + 1)
                nc.scalar.activation(KV[:, 2 * n:2 * n + 2, :].rearrange("p t c -> p (t c)"),
                                     [OP[:, :], MI][n % 2], ACT.Copy).then_inc(kv_ready, 1)
                if n == 2:
                    act.wait_ge(qpart_p, 1)
                    nc.scalar.activation(QP[:, 1, :], QR[:, 0, :], ACT.Copy).then_inc(qpart_a, 1)
            act.wait_ge(qpart_p, 2)
            nc.scalar.activation(QP[:, 2, :], QR[:, 1, :], ACT.Copy).then_inc(qpart_a, 1)

            def copy_kt(i, b, pos):
                act.wait_ge(ktr_done, i + 1)
                nc.scalar.activation(KTM[64:128, b, 6 * P:13 * P], bank16(pos)[64:128, 0:7 * P], ACT.Copy)\
                    .then_inc(kt_odd, 1)

            def copy_o(i):
                act.wait_ge(pv_done, STEPS * (i + 1))
                if has(i, -1):
                    act.wait_ge(otr_done, i)
                nc.scalar.activation(OS[:, :], OP[:, :], ACT.Copy).then_inc(o_copied, 1)

            KT_STEP = UNITS.index("turn_k") * STEPS // len(UNITS)
            def take_columns(i, b):
                act.wait_ge(onehot_odd, i)
                act.wait_ge(idx_mm, i - 1)
                nc.scalar.activation(rA[:, :], rF[:, :, bass.ds(2 * i + 1, 1)].rearrange("p t a -> p (t a)"), ACT.Copy)\
                    .then_inc(rA_ready, 1)
                nc.scalar.activation(BP[:, b, :, :], B1[:, bass.ds(2 * i, 2), :, :].rearrange("p e t c -> p e (t c)"),
                                     ACT.Copy).then_inc(bp_ready, 1)
                act.wait_ge(rA_ready, i - 1)

            def distances(i, b, t):
                places = rA[:, t:t + 1] if has(i, -2) else rF[:, t, 2 * i + 1:2 * i + 2]
                nc.scalar.activation(apart[:, t, :], place16[:, :], ACT.Abs, scale=-1.0, bias=places)\
                    .then_inc(apart_ready, 1)

            def onehot_of_distances(i, b):
                act.wait_ge(apart_ready, NT * (i + 1))
                if has(i, -2):
                    act.wait_ge(idx_mm, i - 1)
                nc.scalar.activation(A1[:, b, 1, :, :], apart[:, :, :], ACT.Relu, scale=-1.0, bias=ones[:, 0:1])\
                    .then_inc(onehot_odd, 1)

            act.wait_ge(pos_ready, 2)
            for i in range(2):
                if i:
                    act.wait_ge(onehot_odd, i)
                for t in range(NT):
                    distances(i, i, t)
                onehot_of_distances(i, i)
            act.wait_ge(onehot_ready, 4)
            take_columns(2, 0)
            for t in range(NT):
                distances(2, 0, t)
            onehot_of_distances(2, 0)

            copy_kt(0, 0, 2)
            copy_kt(1, 1, KT1_POS)

            def weights(i, b):
                steps_before, halves_before = product(act, STEPS, i), product(act, 2 * STEPS, i)
                for s in range(STEPS):
                    for half in range(2):
                        act.wait_ge(st_filled, halves_before + 2 * s + half + 1)
                        if has(i, -1) or s >= 2:
                            act.wait_ge(pv_done, steps_before + s - 1)
                        nc.scalar.activation(PR[:, (b + s) % 2, 1024 * half:1024 * half + 1024], ST[:, half, :], ACT.Exp,
                                             scale=float(D) ** -0.5).then_inc(exp_done, 1)
                        if half == 0 and s == KT_STEP and has(i, 2):
                            copy_kt(i + 2, b, UNITS.index("turn_k"))
                    if s == 0 and has(i, -1):
                        copy_o(i - 1)
                    if has(i, 3):
                        if s == 0:
                            take_columns(i + 3, 1 - b)
                        if 1 <= s <= NT // 2:
                            distances(i + 3, 1 - b, 2 * s - 2)
                            distances(i + 3, 1 - b, 2 * s - 1)
                        if s == NT // 2 + 1:
                            onehot_of_distances(i + 3, 1 - b)

            weights(0, 0)
            with act.Fori(1, NP - 4, 2) as i:
                weights(i, 1)
                weights(i + 1, 0)
            for i in range(NP - 3, NP):
                weights(i, i % 2)
            copy_o(NP - 1)
            def turned2(g):
                act.wait_ge(xt2_done, g + 1)
                nc.scalar.activation(H2T[:, 512 * g:512 * g + 512], ST[:, g // 2, 512 * (g % 2):512 * (g % 2) + 512],
                                     ACT.Identity, bias=mod_col[:, 3:4], scale=one_cb[:, 0:1])\
                    .then_inc(h2_ready, 1)

            for g in range(4):
                act.wait_ge(stats2_ready, 8 * g + 8)
                nc.scalar.activation(std[:, 4 * g:4 * g + 4], mv[:, 4 * g:4 * g + 4, 1], ACT.Sqrt,
                                     bias=eps[:, 0:1]).then_inc(std2_ready, 1)
                if g:
                    turned2(g - 1)
            turned2(3)
            act.wait_ge(tail_dve, 2)
            nc.scalar.activation(LE[:, 1, :], LE[:, 0, :], ACT.Exp).then_inc(exp2_done, 1)
            for q in range((SLOT_TILES + 3) // 4):
                n = min(4, SLOT_TILES - 4 * q)
                act.wait_ge(hst_done, q + 1)
                nc.scalar.activation(HT[:, 512 * q:512 * q + P * n], ST[:, q % 2, 0:P * n],
                                     ACT.Identity, bias=mod_col[:, 3:4], scale=one_cb[:, 0:1])\
                    .then_inc(hst_ready, 1)
            def relu(n, b):
                act.wait_ge(up_done, n + 1)
                if not isinstance(n, int) or n >= 2:
                    act.wait_ge(sq_done, n - 1)
                nc.scalar.activation(RL[:, b, :], SC[:, b, :], ACT.Relu).then_inc(relu_done, 1)

            def y_out_of_psum(n, b):
                act.wait_ge(down_done, n + 1)
                nc.scalar.activation(YS[:, bass.ds(n, 1), :].rearrange("p a e -> p (a e)"), ST[:, b, 0:E], ACT.Copy)\
                    .then_inc(y_ready, 1)

            relu(0, 0)
            relu(1, 1)
            y_out_of_psum(0, 0)
            with act.Fori(2, SLOT_TILES - 1, 2) as n:
                relu(n, 0)
                y_out_of_psum(n - 1, 1)
                relu(n + 1, 1)
                y_out_of_psum(n, 0)
            y_out_of_psum(SLOT_TILES - 1, 1)

        @block.vector
        def _(dve):
            v = nc.vector
            next_step = itertools.count(1).__next__

            v.memset(ones[:, :], 1.0).then_inc(dve_step, 1)
            dve.wait_ge(dve_step, next_step())
            v.memset(eps[:, :], EPS).then_inc(dve_step, 1)
            dve.wait_ge(dve_step, next_step())

            def statistics(g):
                dve.wait_ge(x_in[g], 16)
                for t in range(4 * g, 4 * g + 4):
                    v.bn_stats(stats[:, t, :], X[:, t, :]).then_inc(stats_ready, 1)
                for t in range(4 * g, 4 * g + 4):
                    dve.wait_ge(stats_ready, 8 * g + t - 4 * g + 1)
                    v.bn_aggr(mv[:, t, :], stats[:, t, :]).then_inc(stats_ready, 1)

            def normalize1(g):
                dve.wait_ge(std_ready, g + 1)
                v.reciprocal(rstd[:, 4 * g:4 * g + 4], std[:, 4 * g:4 * g + 4]).then_inc(dve_step, 1)
                dve.wait_ge(dve_step, next_step())
                for t in range(4 * g, 4 * g + 4):
                    v.tensor_scalar(XN[:, t, :], X[:, t, :], mv[:, t, 0:1], rstd[:, t:t + 1], ALU.subtract,
                                    ALU.mult).then_inc(xn_ready, 1)

            statistics(0)
            statistics(1)
            dve.wait_ge(silu_ready, 1)
            v.tensor_tensor(silu[:, :], ccol[:, :], csig[:, :], ALU.mult).then_inc(dve_step, 1)
            dve.wait_ge(dve_step, next_step())
            v.tensor_scalar(silu_b[:, :], ones[:, :], silu[:, 0:1], None, ALU.mult).then_inc(silu_ready, 1)
            normalize1(0)
            statistics(2)
            normalize1(1)
            statistics(3)
            normalize1(2)
            dve.wait_ge(mod_done, 1)
            v.tensor_copy(mod_col[:, :], OP[:, 0:6]).then_inc(mod_ready, 1)
            dve.wait_ge(mod_ready, 1)
            v.tensor_scalar(one_ca[:, :], mod_col[:, 1:2], 1.0, None, ALU.add).then_inc(mod_ready, 1)
            normalize1(3)
            v.tensor_scalar(one_cb[:, :], mod_col[:, 4:5], 1.0, None, ALU.add).then_inc(dve_step, 1)
            dve.wait_ge(dve_step, next_step())
            g_ps = OP[:, P:3 * P]
            g2 = "p a e -> p (a e)"
            v.tensor_scalar(gsign[:, :, :].rearrange(g2), g_ps, 0.0, 2.0, ALU.is_ge, ALU.mult).then_inc(dve_step, 1)
            dve.wait_ge(dve_step, next_step())
            v.tensor_scalar(gneg[:, :, :].rearrange(g2), g_ps, -1.0, 0.25, ALU.mult, ALU.max).then_inc(dve_step, 1)
            dve.wait_ge(dve_step, next_step())
            v.tensor_tensor(gabs[:, :, :].rearrange(g2), g_ps, gneg[:, :, :].rearrange(g2), ALU.max)\
                .then_inc(dve_step, 1)
            dve.wait_ge(dve_step, next_step())
            v.scalar_tensor_tensor(gate[:, :, :], gsign[:, :, :], -1.0, gabs[:, :, :], ALU.add, ALU.mult)\
                .then_inc(gate_ready, 1)
            v.memset(onesb[:, :], 1.0).then_inc(dve_step, 1)
            dve.wait_ge(dve_step, next_step())
            v.memset(CUM[:, 0:1], 0.0).then_inc(dve_step, 1)
            dve.wait_ge(dve_step, next_step())
            dve.wait_ge(const_in, 16)
            v.tensor_copy(lowerb[:, :], cc("lower")).then_inc(dve_step, 1)
            dve.wait_ge(dve_step, next_step())
            v.tensor_copy(place16[:, :], cc("place")).then_inc(dve_step, 1)
            dve.wait_ge(dve_step, next_step())
            v.tensor_copy(identb[:, :], ident).then_inc(init_dve, 1)
            dve.wait_ge(score0, 2)
            v.tensor_scalar(R[:, :], junk[:, :], 0.5, None, ALU.max).then_inc(dve_step, 1)
            dve.wait_ge(dve_step, next_step())
            v.tensor_scalar(cand[:, 0, :], steps[:, 0:4], 0.5, None, ALU.add).then_inc(dve_step, 1)
            dve.wait_ge(dve_step, next_step())
            for r in range(ROUNDS):
                for k in range(3):
                    v.tensor_scalar(jnk3[:, k, :], R[:, :], cand[:, r, k + 1:k + 2], None, ALU.is_ge, ALU.add,
                                    accum_out=cnt[:, r, k:k + 1]).then_inc(search_dve, 1)
                if r + 1 <= ROUNDS:
                    v.tensor_scalar(etab[:, r, :], steps[:, 4 * (r + 1):4 * (r + 2)], cand[:, r, 0:1], None,
                                    ALU.add).then_inc(dve_step, 1)
                    dve.wait_ge(dve_step, next_step())
                dve.wait_ge(search_pe, r + 1)
                v.tensor_scalar(njunk[:, r, :], SC[:, r % 2, 0:3], KEEP - 0.5, None, ALU.is_ge, ALU.add,
                                accum_out=nge[:, r:r + 1]).then_inc(dve_step, 1)
                dve.wait_ge(dve_step, next_step())
                v.scalar_tensor_tensor(cand[:, r + 1, :], nge[:, r:r + 1].to_broadcast([P, 4]),
                                       2.0 ** -4 * 4.0 ** -r, etab[:, r, :], ALU.mult, ALU.add).then_inc(dve_step, 1)
                dve.wait_ge(dve_step, next_step())
            T = cand[:, ROUNDS, 0:1]
            v.tensor_scalar(GT[:, :], R[:, :], T, None, ALU.is_gt, ALU.add, accum_out=tot[:, 0:1])\
                .then_inc(sel_pe, 1)
            v.tensor_scalar(EQ[:, :], R[:, :], T, None, ALU.is_equal, ALU.add, accum_out=tot[:, 1:2])\
                .then_inc(sel_pe, 1)
            dve.wait_ge(sel_pe, 2)
            v.tensor_tensor_scan(SG[:, :], ones[:, 0:1].to_broadcast([P, CT]), GT[:, :], 0.0, ALU.mult, ALU.add)\
                .then_inc(dve_step, 1)
            dve.wait_ge(dve_step, next_step())
            v.tensor_tensor_scan(SE[:, :], ones[:, 0:1].to_broadcast([P, CT]), EQ[:, :], 0.0, ALU.mult, ALU.add)\
                .then_inc(dve_step, 1)
            dve.wait_ge(dve_step, next_step())
            dve.wait_ge(pos_done, 1)
            v.tensor_copy(offs[:, :], MP[:, 0:4]).then_inc(dve_step, 1)
            dve.wait_ge(dve_step, next_step())
            v.tensor_scalar(need[:, 0:1], offs[:, 2:3], -1.0, float(KEEP), ALU.mult, ALU.add).then_inc(dve_step, 1)
            dve.wait_ge(dve_step, next_step())
            v.tensor_tensor(need[:, 1:2], need[:, 0:1], offs[:, 1:2], ALU.subtract).then_inc(dve_step, 1)
            dve.wait_ge(dve_step, next_step())
            v.scalar_tensor_tensor(W1[:, :], SE[:, :], need[:, 1:2], EQ[:, :], ALU.is_le, ALU.mult)\
                .then_inc(dve_step, 1)
            dve.wait_ge(dve_step, next_step())
            v.tensor_tensor(W2[:, :], GT[:, :], W1[:, :], ALU.add).then_inc(dve_step, 1)
            dve.wait_ge(dve_step, next_step())
            v.tensor_scalar(W3[:, :], SE[:, :], offs[:, 1:2], need[:, 0:1], ALU.add, ALU.min).then_inc(dve_step, 1)
            dve.wait_ge(dve_step, next_step())
            v.scalar_tensor_tensor(W4[:, :], SG[:, :], offs[:, 0:1], W3[:, :], ALU.add, ALU.add).then_inc(dve_step, 1)
            dve.wait_ge(dve_step, next_step())
            v.tensor_scalar(W5[:, :], W4[:, :], cc("gap_from"), float(GAP), ALU.is_gt, ALU.mult).then_inc(dve_step, 1)
            dve.wait_ge(dve_step, next_step())
            v.tensor_tensor(W3[:, :], W4[:, :], W5[:, :], ALU.add).then_inc(dve_step, 1)
            dve.wait_ge(dve_step, next_step())
            v.scalar_tensor_tensor(W1[:, :], W3[:, :], -1.0 - NOT_KEPT, W2[:, :], ALU.add, ALU.mult)\
                .then_inc(dve_step, 1)
            dve.wait_ge(dve_step, next_step())
            v.tensor_scalar(W5[:, :], W1[:, :], NOT_KEPT, None, ALU.add).then_inc(pos_ready, 1)
            dve.wait_ge(pos_done, 2)
            v.tensor_copy(posI[:, :], MP[:, 0:CT]).then_inc(dve_step, 1)
            dve.wait_ge(dve_step, next_step())
            v.tensor_single_scalar(rI[:, :], posI[:, :], P - 1, ALU.bitwise_and).then_inc(dve_step, 1)
            dve.wait_ge(dve_step, next_step())
            v.tensor_single_scalar(aI[:, :], posI[:, :], 7, ALU.logical_shift_right).then_inc(dve_step, 1)
            dve.wait_ge(dve_step, next_step())
            v.tensor_copy(rF[:, :, :].rearrange("p t h -> p (t h)"), rI[:, :]).then_inc(pos_ready, 1)
            v.tensor_copy(aF[:, :, :].rearrange("p t h -> p (t h)"), aI[:, :]).then_inc(pos_ready, 1)

            def index(i, b, pos):
                dve.wait_ge(idx_mm, i + 1)
                if has(i, -2):
                    dve.wait_ge(gathered, 16 * STEPS * (i - 1))
                v.scalar_tensor_tensor(idx[:, b, :], bank(pos)[:, 0:STEPS], float(H),
                                       row_add[:, bass.ds(STEPS * i, STEPS)],
                                       ALU.mult, ALU.add).then_inc(idx_ready, 1)

            def maximum(b, u, pos, units_before):
                e, half = u // 32, u % 2
                a, z = SCORE_COLS[e][half]
                dve.wait_ge(s_filled, units_before + u + 1)
                v.tensor_reduce(MXU[:, b, u:u + 1], bank(pos)[:, 0:z - a], AX.X, ALU.max)\
                    .then_inc(s_reduced, 1)

            def split_max(i, b, e):
                k = 5 * (2 * i + e)
                dve.wait_ge(s_reduced, SUNITS * i + 32 * (e + 1))
                v.tensor_reduce(NM[:, 0, 0:NT], MXU[:, b, 32 * e:32 * e + 32].rearrange("p (n two) -> p n two", two=2),
                                AX.X, ALU.max, negate=True).then_inc(m_chain, 1)
                dve.wait_ge(m_chain, k + 1)
                if has(i, -1):
                    dve.wait_ge([mtr_even, mtr_odd][e], i)
                for part in range(PARTS - 1):
                    v.tensor_copy(SM[:, e, part, :], NM[:, part, 0:NT]).then_inc(m_chain, 1)
                    dve.wait_ge(m_chain, k + 2 * part + 2)
                    v.tensor_tensor(NM[:, part + 1, 0:NT], NM[:, part, 0:NT], SM[:, e, part, :], ALU.subtract)\
                        .then_inc(m_chain, 1)
                    dve.wait_ge(m_chain, k + 2 * part + 3)
                v.tensor_copy(SM[:, e, 2, :], NM[:, 2, 0:NT]).then_inc([m_split_even, m_split_odd][e], 1)

            def copy_mt(i, e, pos):
                dve.wait_ge([mtr_even, mtr_odd][e], i + 1)
                if has(i, -1):
                    dve.wait_ge([mrow_even, mrow_odd][e], 16 * i)
                v.tensor_copy(MT[:, e, :], bank16(pos)[0:PARTS * NT, 0:P]).then_inc([mt_even, mt_odd][e], 1)

            def copy_kt(i, b, pos):
                dve.wait_ge(ktr_done, i + 1)
                v.tensor_copy(KTM[0:64, b, 0:7 * P], bank16(pos)[0:64, 0:7 * P]).then_inc(kt_even, 1)

            def copy_kte(i, b):
                dve.wait_ge(kt_odd, i + 1)
                dve.wait_ge(kt_even, i + 1)
                if has(i, -2):
                    dve.wait_ge(st_filled, 2 * STEPS * (i - 1))
                v.tensor_copy(KTE[:, b, :], KTM[:, b, :]).then_inc(kte_ready, 1)

            def normalize(i, pos):
                dve.wait_ge(otr_done, i + 1)
                t = bank(pos).rearrange("p (b g c) -> p b g c", b=4, g=4)
                if has(i, -1):
                    dve.wait_ge(o_norm, 2 * i)
                v.reciprocal(REC[:, :, :, :], t[:, :, :, D::16]).then_inc(rec_ready, 1)
                dve.wait_ge(rec_ready, i + 1)
                for e in range(2):
                    dst = AT[:, :, bass.ds(2 * D * i + D * e, D)].rearrange("p (g b) d -> p b g d", g=4)
                    v.tensor_tensor(dst, t[:, :, :, 16 * e:16 * e + D],
                                    REC[:, :, :, e:e + 1].to_broadcast([P, 4, 4, D]), ALU.mult)\
                        .then_inc(o_norm, 1)

            def onehot(i, b):
                for t in range(NT):
                    last = v.tensor_scalar(A1[:, b, 0, t, :], place16[:, :], rF[:, t, 2 * i:2 * i + 1], None,
                                           ALU.is_equal)
                last.then_inc(onehot_ready, 1)

            def columns(h0, h1):
                for h in range(h0, h1):
                    e = h % 2
                    v.tensor_tensor(B0[:, h, :, :], aF[:, :, h:h + 1].to_broadcast([P, NT, BLOCKS]),
                                    blocks[:, BLOCKS * e:BLOCKS * (e + 1)].rearrange("p (a n) -> p a n", a=1)
                                    .to_broadcast([P, NT, BLOCKS]), ALU.is_equal).then_inc(b_parts, 1)
                dve.wait_ge(b_parts, h1)
                last = v.tensor_tensor(B1[:, h0:h1, :, :], B0[:, h0:h1, :, :],
                                       token.rearrange("p (a t b) -> p a t b", a=1, b=1)
                                       .to_broadcast([P, h1 - h0, NT, BLOCKS]), ALU.mult)
                last.then_inc(onehot_ready, 1)

            dve.wait_ge(pos_ready, 3)
            columns(0, 2)
            onehot(0, 0)
            index(0, 0, 0)
            onehot(1, 1)
            columns(2, H)
            index(1, 1, 1)
            copy_kt(0, 0, 2)
            copy_kte(0, 0)
            for n, kind in enumerate(LEAD_UNITS):
                if kind == "turn_m_even":
                    copy_mt(0, 0, n)
                else:
                    if kind == 32:
                        split_max(0, 0, 0)
                    maximum(0, kind, n, 0)
            copy_kt(1, 1, KT1_POS)
            def pair(i, b):
                units = product(dve, SUNITS, i)
                last_pair = not has(i, 1)
                for pos, kind in enumerate(UNITS):
                    if kind == "turn_o":
                        if has(i, -1):
                            normalize(i - 1, pos)
                    elif kind == "index":
                        if has(i, 2):
                            index(i + 2, b, pos)
                    elif kind == "turn_m_odd":
                        copy_mt(i, 1, pos)
                        if not last_pair:
                            copy_kte(i + 1, 1 - b)
                    elif kind == "turn_m_even":
                        if not last_pair:
                            copy_mt(i + 1, 0, pos)
                    elif kind == "turn_k":
                        if has(i, 2):
                            copy_kt(i + 2, b, pos)
                    else:
                        u = LEAD + kind
                        if u < SUNITS:
                            maximum(b, u, pos, units)
                            if u == SUNITS - 1:
                                split_max(i, b, 1)
                        elif not last_pair:
                            maximum(1 - b, u - SUNITS, pos, units + SUNITS)
                            if u - SUNITS == 31:
                                split_max(i + 1, 1 - b, 0)

            pair(0, 0)
            with dve.Fori(1, NP - 4, 2) as i:
                pair(i, 1)
                pair(i + 1, 0)
            for i in range(NP - 3, NP):
                pair(i, i % 2)
            normalize(NP - 1, 0)
            next_tail = itertools.count(1).__next__

            def residual_and_stats(g):
                dve.wait_ge(gated, g + 1)
                v.tensor_tensor(X2[:, 4 * g:4 * g + 4, :], GAT[:, 4 * g:4 * g + 4, :], X[:, 4 * g:4 * g + 4, :],
                                ALU.add).then_inc(x2_ready, 1)
                dve.wait_ge(x2_ready, g + 1)
                for t in range(4 * g, 4 * g + 4):
                    v.bn_stats(stats[:, t, :], X2[:, t, :]).then_inc(stats2_ready, 1)
                for t in range(4 * g, 4 * g + 4):
                    dve.wait_ge(stats2_ready, 8 * g + t - 4 * g + 1)
                    v.bn_aggr(mv[:, t, :], stats[:, t, :]).then_inc(stats2_ready, 1)

            def normalize2(g):
                dve.wait_ge(std2_ready, g + 1)
                v.reciprocal(rstd[:, 4 * g:4 * g + 4], std[:, 4 * g:4 * g + 4]).then_inc(tail_step, 1)
                dve.wait_ge(tail_step, next_tail())
                for t in range(4 * g, 4 * g + 4):
                    v.tensor_scalar(XN2[:, t, :], X2[:, t, :], mv[:, t, 0:1], rstd[:, t:t + 1], ALU.subtract,
                                    ALU.mult).then_inc(xn2_ready, 1)

            residual_and_stats(0)
            for g in range(1, 4):
                residual_and_stats(g)
                normalize2(g - 1)
            normalize2(3)
            dve.wait_ge(route_done, 1)

            def te(ap):
                return ap.rearrange("p (t e) -> p t e", e=NE)

            def bc(ap):
                return ap.rearrange("p (t a) -> p t a", a=1).to_broadcast([P, NT, NE])

            LG = OP[:, 0:NT * NE]
            v.tensor_reduce(LM[:, 0, :], te(LG), AX.X, ALU.max).then_inc(tail_dve, 1)
            dve.wait_ge(tail_dve, 1)
            v.tensor_tensor(te(LE[:, 0, :]), te(LG), bc(LM[:, 0, :]), ALU.subtract).then_inc(tail_dve, 1)
            dve.wait_ge(exp2_done, 1)
            v.tensor_reduce(LM[:, 1, :], te(LE[:, 1, :]), AX.X, ALU.add).then_inc(tail_step, 1)
            dve.wait_ge(tail_step, next_tail())
            v.reciprocal(LM[:, 2, :], LM[:, 1, :]).then_inc(tail_step, 1)
            dve.wait_ge(tail_step, next_tail())
            v.tensor_tensor(te(LE[:, 2, :]), te(LE[:, 1, :]), bc(LM[:, 2, :]), ALU.mult).then_inc(tail_step, 1)
            dve.wait_ge(tail_step, next_tail())
            v.tensor_reduce(LM[:, 3, :], te(LE[:, 2, :]), AX.X, ALU.max).then_inc(tail_step, 1)
            dve.wait_ge(tail_step, next_tail())
            v.tensor_tensor(te(LE[:, 3, :]), te(LE[:, 2, :]), bc(LM[:, 3, :]), ALU.is_equal).then_inc(tail_step, 1)
            dve.wait_ge(tail_step, next_tail())
            expert = cc("expert").rearrange("p (e t) -> p t e", e=NE)
            v.tensor_tensor(te(LE[:, 4, :]), te(LE[:, 3, :]), expert, ALU.mult).then_inc(tail_step, 1)
            dve.wait_ge(tail_step, next_tail())
            v.tensor_reduce(slotF[:, :], te(LE[:, 4, :]), AX.X, ALU.min).then_inc(tail_step, 1)
            dve.wait_ge(tail_step, next_tail())
            v.tensor_tensor(OH[:, :, :].rearrange("p e t -> p t e"), expert, bc(slotF[:, :]), ALU.is_equal)\
                .then_inc(tail_step, 1)
            dve.wait_ge(tail_step, next_tail())
            v.tensor_copy(OHB[:, :], OH[:, :, :].rearrange("p e t -> p (e t)")).then_inc(oh_ready, 1)
            dve.wait_ge(rank_done, 1)
            RANK = OP[:, 0:P]
            v.tensor_copy(TOT[:, :, :].rearrange("p e t -> p (e t)"), OP[:, P:2 * P]).then_inc(tail_step, 1)
            dve.wait_ge(tail_step, next_tail())
            v.tensor_tensor_scan(CUM[:, 1:], ones[:, 0:NE * NT], TOT[:, :, :].rearrange("p e t -> p (e t)"), 0.0,
                                 ALU.mult, ALU.add).then_inc(tail_step, 1)
            dve.wait_ge(tail_step, next_tail())
            ends = CUM[:, NT::NT]
            starts = CUM[:, 0:NE * NT:NT]
            v.tensor_tensor(EN[:, 0, :], ends, starts, ALU.subtract).then_inc(tail_step, 1)
            dve.wait_ge(tail_step, next_tail())
            v.tensor_scalar(EN[:, 1, :], EN[:, 0, :], P - 1.0, None, ALU.add).then_inc(tail_step, 1)
            dve.wait_ge(tail_step, next_tail())
            v.tensor_copy(ENI[:, 0, :], EN[:, 1, :]).then_inc(tail_step, 1)
            dve.wait_ge(tail_step, next_tail())
            v.tensor_single_scalar(ENI[:, 1, :], ENI[:, 0, :], 7, ALU.logical_shift_right).then_inc(tail_step, 1)
            dve.wait_ge(tail_step, next_tail())
            v.tensor_copy(EN[:, 2, :], ENI[:, 1, :]).then_inc(tail_step, 1)
            dve.wait_ge(tail_step, next_tail())
            v.tensor_tensor_scan(EN[:, 3, :], ones[:, 0:NE], EN[:, 2, :], 0.0, ALU.mult, ALU.add)\
                .then_inc(tail_step, 1)
            dve.wait_ge(tail_step, next_tail())
            v.tensor_tensor(TE[:, :, :], cc("slot_tile").rearrange("p (s e) -> p s e", e=NE),
                            EN[:, 3:4, :].to_broadcast([P, SLOT_TILES, NE]), ALU.is_ge).then_inc(tail_step, 1)
            dve.wait_ge(tail_step, next_tail())
            v.tensor_reduce(TEF[:, :], TE[:, :, :], AX.X, ALU.add).then_inc(tail_step, 1)
            dve.wait_ge(tail_step, next_tail())
            v.tensor_scalar(TEI[:, :], TEF[:, :], NE - 1.0, None, ALU.min).then_inc(tile_ready, 1)
            v.tensor_tensor(EN[:, 4, :], EN[:, 3, :], EN[:, 2, :], ALU.subtract).then_inc(tail_step, 1)
            dve.wait_ge(tail_step, next_tail())
            v.scalar_tensor_tensor(EN[:, 5, :], EN[:, 4, :], float(P), starts, ALU.mult, ALU.subtract)\
                .then_inc(tail_step, 1)
            dve.wait_ge(tail_step, next_tail())
            v.tensor_tensor(SLB[:, :, :].rearrange("p e t -> p (e t)"), CUM[:, 0:NE * NT], RANK, ALU.add)\
                .then_inc(tail_step, 1)
            dve.wait_ge(tail_step, next_tail())
            v.tensor_tensor(SLC[:, :, :], SLB[:, :, :],
                            EN[:, 5, :].rearrange("p (e a) -> p e a", a=1).to_broadcast([P, NE, NT]), ALU.add)\
                .then_inc(tail_step, 1)
            dve.wait_ge(tail_step, next_tail())
            v.tensor_tensor(SLB[:, :, :], SLC[:, :, :], OH[:, :, :], ALU.mult).then_inc(tail_step, 1)
            dve.wait_ge(tail_step, next_tail())
            v.tensor_reduce(slotF[:, :], SLB[:, :, :].rearrange("p e t -> p t e"), AX.X, ALU.add)\
                .then_inc(tail_step, 1)
            dve.wait_ge(tail_step, next_tail())
            v.tensor_copy(slot[:, :], slotF[:, :]).then_inc(slot_ready, 1)
            dve.wait_ge(tile_ready, 1)
            dve.wait_ge(we_in, 32)
            def expert_of(n):
                return dve.value_load(TEI[0:1, bass.ds(n, 1)], min_val=0, max_val=NE - 1)

            def take_proj(n, b, e):
                if not isinstance(n, int) or n >= 2:
                    dve.wait_ge(down_done, n - 1)
                v.tensor_copy(WPROJ[:, b, :], WE[:, bass.ds(e, 1), HD:].rearrange("p a c -> p (a c)"))\
                    .then_inc(proj_ready, 1)

            def square(n, b):
                dve.wait_ge(relu_done, n + 1)
                if not isinstance(n, int) or n >= 2:
                    dve.wait_ge(down_done, n - 1)
                v.tensor_tensor(R2[:, b, :], RL[:, b, :], RL[:, b, :], ALU.mult).then_inc(sq_done, 1)

            for n in range(2):
                take_proj(n, n, expert_of(n))
            square(0, 0)
            with dve.Fori(2, SLOT_TILES - 1, 2) as n:
                for b in range(2):
                    e = expert_of(n + b)
                    square(n + b - 1, 1 - b)
                    take_proj(n + b, b, e)
            square(SLOT_TILES - 1, 1)
            for g in range(4):
                dve.wait_ge([y_back_0, y_back_1, y_back_2, y_back_3][g], 16 * 4)
                t4 = slice(4 * g, 4 * g + 4)
                v.tensor_tensor(H2T.rearrange("p (t e) -> p t e", e=E)[:, t4, :], YG[:, t4, :],
                                gate[:, 1:2, :].to_broadcast([P, 4, E]), ALU.mult).then_inc(tail_step, 1)
                dve.wait_ge(tail_step, next_tail())
                v.tensor_tensor(GAT[:, t4, :], H2T.rearrange("p (t e) -> p t e", e=E)[:, t4, :], X2[:, t4, :],
                                ALU.add).then_inc(out_ready, 1)

        @block.tensor
        def _(pe):
            mm = nc.tensor.matmul
            pe.wait_ge(const_in, 16)
            pe.wait_ge(silu_ready, 2)
            for c in range(6):
                last = mm(OP[:, c:c + 1], WMOD[:, P * c:P * c + P], silu[:, :], start=True, stop=True)
            for a, c in ((0, 2), (1, 5)):
                last = mm(OP[:, P + P * a:2 * P + P * a], silu_b[:, :], WMOD[:, P * c:P * c + P], start=True, stop=True)
            last.then_inc(mod_done, 1)
            for g in range(4):
                for t in range(4 * g, 4 * g + 4):
                    pe.wait_ge(xn_ready, t + 1)
                    last = nc.tensor.transpose(ST[:, g // 2, 512 * (g % 2) + P * (t % 4):512 * (g % 2) + P * (t % 4) + P],
                                               XN[:, t, :], ident)
                last.then_inc(xt_done, 1)
            pe.wait_ge(w_in, 16 * 9)
            for j in range(4):
                pe.wait_ge(ht_ready, j + 1)
                last = mm(SC[32 * j:32 * j + RH, 0, :], WR1[:, :], HT[:, 512 * j:512 * j + 512], start=True, stop=True)
            last.then_inc(h1_done, 1)
            pe.wait_ge(wr2_in, 8)
            pe.wait_ge(h1_ready, 1)
            mm(SC[:, 1, 0:CT], WR2[:, 0, :], H1[:, 0:CT], start=True, stop=False)
            mm(SC[:, 1, 0:CT], WR2[:, 1, :], H1[:, CT:2 * CT], start=False, stop=True).then_inc(logit_done, 1)
            pe.wait_ge(gate_ready, 1)

            def q_chunk(g):
                mm(ST[:, g // 2, 512 * (g % 2):512 * (g % 2) + 512], WQ[:, :], HT[:, 512 * g:512 * g + 512],
                   start=True, stop=True).then_inc(q_done, 1)

            def kv(n):
                if n >= 2:
                    pe.wait_ge(kv_ready, n - 1)
                to = [OP[:, :], MI][n % 2]
                for t in range(2):
                    last = mm(to[:, 2 * E * t:2 * E * t + 2 * E], HT[:, P * (2 * n + t):P * (2 * n + t) + P], WKV[:, :],
                              start=True, stop=True)
                last.then_inc(kv_done, 1)

            pe.wait_ge(score0, 2)
            for r in range(ROUNDS):
                pe.wait_ge(search_dve, 3 * (r + 1))
                mm(SC[:, r % 2, 0:3], same_head, cnt[:, r, :], start=True, stop=True).then_inc(search_pe, 1)
                if r < 4:
                    q_chunk(r)
                else:
                    kv(r - 4)
            pe.wait_ge(sel_pe, 2)
            mm(MP[:, 0:2], before, tot[:, :], start=True, stop=True)
            mm(MP[:, 2:4], same_head, tot[:, :], start=True, stop=True).then_inc(pos_done, 1)
            kv(NT // 2 - 1)
            pe.wait_ge(pos_ready, 1)
            for u in range(2):
                last = nc.tensor.transpose(MP[:, P * u:P * u + P], W5[:, P * u:P * u + P], ident)
            last.then_inc(pos_done, 1)

            def index_mm(i, b, pos):
                pe.wait_ge(onehot_ready, i + 3 if has(i, -1) else 2)
                pe.wait_ge(onehot_odd, i + 1)
                if has(i, -2):
                    pe.wait_ge(bp_ready, i - 1)
                for e in range(2):
                    for t in range(NT):
                        cols = BP[:, b, e, BLOCKS * t:BLOCKS * (t + 1)] if has(i, -2) else B1[:, 2 * i + e, t, :]
                        last = mm(bank(pos)[:, 6 * e:6 * e + BLOCKS], A1[:, b, e, t, :], cols,
                                  start=(e == 0 and t == 0), stop=(e == 1 and t == NT - 1), skip_group_check=True)
                last.then_inc(idx_mm, 1)

            def turn_k(i, b, pos):
                pe.wait_ge(prep_ready, i + 1)
                pe.sem_inc(turning, 1)
                for s in range(STEPS):
                    col = STEP_COLUMN[s]
                    if s <= 6:
                        o = bank16(pos)[0:64, P * col:P * col + P]
                        last = nc.tensor.transpose(o, RS[:, b, 0:64] if s == 6 else KS[:, b, s, :], identb[:, :])
                    if s >= 6:
                        o = bank16(pos)[64:128, P * (col - 6):P * (col - 6) + P]
                        last = nc.tensor.transpose(o, RS[:, b, 64:128] if s == 6 else KS[:, b, s, :], identb[:, :])
                last.then_inc(ktr_done, 1)

            def turn_m(i, e, pos):
                pe.wait_ge([m_split_even, m_split_odd][e], i + 1)
                pe.sem_inc(turning, 1)
                nc.tensor.transpose(bank16(pos)[0:PARTS * NT, 0:P], SM[:, e, :, :].rearrange("p a t -> p (a t)"),
                                    identb[:, :]).then_inc([mtr_even, mtr_odd][e], 1)

            def turn_o(i, pos):
                pe.wait_ge(o_copied, i + 1)
                for q in range(4):
                    last = nc.tensor.transpose(bank(pos)[:, P * q:P * q + P], OS[:, P * q:P * q + P], ident)
                last.then_inc(otr_done, 1)

            def score_tile(i, b, u, pos):
                e, qt, half = u // 32, u % 32 // 2, u % 2
                a, z = SCORE_COLS[e][half]
                mm(bank(pos)[:, 0:z - a], QSM[:, b, P * qt:P * qt + P], KTM[:, b, a:z],
                   start=True, stop=True).then_inc(s_filled, 1)

            def free_bank(i, pos, units):
                while True:
                    pos -= RING
                    if pos < 0:
                        i, pos, units = i - 1, pos + len(UNITS), units - SUNITS
                    kind = UNITS[pos]
                    if isinstance(i, int) and i < 0:
                        pe.wait_ge(s_reduced, LEAD - len(UNITS) + pos + 1)
                    elif done(i, kind) or (kind == "turn_o" and not has(i, -1)):
                        continue
                    elif kind == "turn_o":
                        pe.wait_ge(o_norm, 2 * i)
                    elif kind == "index":
                        pe.wait_ge(idx_ready, i + 3)
                    elif kind == "turn_k":
                        pe.wait_ge(kt_odd, i + 3)
                        pe.wait_ge(kt_even, i + 3)
                    elif kind == "turn_m_odd":
                        pe.wait_ge(mt_odd, i + 1)
                    elif kind == "turn_m_even":
                        pe.wait_ge(mt_even, i + 2)
                    else:
                        pe.wait_ge(s_reduced, units + LEAD + kind + 1)
                    return

            def scores(i, b, s, c, halves_before):
                half = c // 2
                n = halves_before + 2 * s + half
                if (has(i, -1) or s >= 1) and c % 2 == 0:
                    pe.wait_ge(exp_done, n - 1)
                col = STEP_COLUMN[s]
                rows = 64 + KROWS if s < 6 else P
                last = mm(ST[:, half, 512 * (c % 2):512 * (c % 2) + 512], KTE[0:rows, b, P * col:P * col + P],
                          QSE[0:rows, b, 512 * c:512 * c + 512], start=True, stop=True)
                if c % 2:
                    last.then_inc(st_filled, 1)

            def weigh_v(i, b, s, halves_before, part):
                if part == 0:
                    pe.wait_ge(exp_done, halves_before + 2 * s + 2)
                    if s == 0:
                        pe.wait_ge(v_ready, i + 1)
                        if has(i, -1):
                            pe.wait_ge(o_copied, i)
                for g in range(4):
                    c0 = 256 * part
                    last = mm(OP[32 * g:32 * g + 32, c0:c0 + 256], VS[:, b, s, :],
                              PR[:, (b + s) % 2, 512 * g + c0:512 * g + c0 + 256], start=(s == 0 and part == 0),
                              stop=(s == STEPS - 1 and part == 1),
                              skip_group_check=True)
                if part == 1:
                    last.then_inc(pv_done, 1)

            def done(i, kind):
                if kind in ("index", "turn_k"):
                    return not has(i, 2)
                if kind == "turn_m_odd" or kind == "turn_o":
                    return False
                return not has(i, 1) and (kind == "turn_m_even" or LEAD + kind >= SUNITS)

            def unit(i, b, pos, units):
                kind = UNITS[pos]
                last_pair = not has(i, 1)
                if done(i, kind):
                    return
                free_bank(i, pos, units)
                if kind == "turn_o":
                    if has(i, -1):
                        turn_o(i - 1, pos)
                elif kind == "index":
                    if has(i, 2):
                        index_mm(i + 2, b, pos)
                elif kind == "turn_k":
                    if has(i, 2):
                        turn_k(i + 2, b, pos)
                elif kind == "turn_m_odd":
                    turn_m(i, 1, pos)
                elif kind == "turn_m_even":
                    if not last_pair:
                        turn_m(i + 1, 0, pos)
                else:
                    u = LEAD + kind
                    if u < SUNITS:
                        score_tile(i, b, u, pos)
                    elif not last_pair:
                        if u == SUNITS:
                            pe.wait_ge([qsm_even, qsm_odd][1 - b], 48 * (i + b) + 96)
                            pe.wait_ge(kt_odd, i + 2)
                            pe.wait_ge(kt_even, i + 2)
                        score_tile(i + 1, 1 - b, u - SUNITS, pos)

            index_mm(0, 0, 0)
            pe.wait_ge(pos_ready, 3)
            index_mm(1, 1, 1)
            pe.wait_ge(kv_ready, NT // 2)
            pe.wait_ge(init_dve, 1)
            turn_k(0, 0, 2)
            pe.wait_ge(kt_odd, 1)
            pe.wait_ge(kt_even, 1)
            pe.wait_ge(idx_ready, 2)
            pe.wait_ge(qsm_even, 16 * 6)
            for n, kind in enumerate(LEAD_UNITS):
                if n >= RING:
                    before_it = LEAD_UNITS[n - RING]
                    if before_it == "turn_m_even":
                        pe.wait_ge(mt_even, 1)
                    else:
                        pe.wait_ge(s_reduced, before_it + 1)
                if kind == "turn_m_even":
                    turn_m(0, 0, n)
                else:
                    score_tile(0, 0, kind, n)
            pe.wait_ge(s_reduced, LEAD)
            turn_k(1, 1, KT1_POS)
            pe.wait_ge(kt_odd, 2)
            pe.wait_ge(kt_even, 2)
            def pair(i, b):
                units, halves_before = product(pe, SUNITS, i), product(pe, 2 * STEPS, i)
                pe.wait_ge(kte_ready, i + 1)
                pe.wait_ge([qse_even, qse_odd][b], 48 * (i - b) + 96)
                pe.wait_ge(mrow_even, 16 * (i + 1))
                if not has(i, -1):
                    pe.wait_ge(init_dve, 1)
                at_unit = 0
                for s in range(STEPS):
                    if s == 6:
                        pe.wait_ge(mrow_odd, 16 * (i + 1))
                    pieces = [("scores", c) for c in range(4)] + [("weigh", part) for part in range(2)]
                    for n, (piece, arg) in enumerate(pieces):
                        if piece == "scores":
                            scores(i, b, s, arg, halves_before)
                        elif s > 0:
                            weigh_v(i, b, s - 1, halves_before, arg)
                        elif has(i, -1):
                            weigh_v(i - 1, 1 - b, STEPS - 1, halves_before - 2 * STEPS, arg)
                        while at_unit * STEPS * len(pieces) < len(UNITS) * (s * len(pieces) + n + 1):
                            unit(i, b, at_unit, units)
                            at_unit += 1

            pair(0, 0)
            with pe.Fori(1, NP - 4, 2) as i:
                pair(i, 1)
                pair(i + 1, 0)
            for i in range(NP - 3, NP):
                pair(i, i % 2)
            for part in range(2):
                weigh_v(NP - 1, (NP - 1) % 2, STEPS - 1, 2 * STEPS * (NP - 1), part)
            pe.wait_ge(s_reduced, SUNITS * NP)
            pe.wait_ge(o_norm, 2 * (NP - 1))
            pe.wait_ge(mt_odd, NP)
            turn_o(NP - 1, 0)
            for g in range(4):
                for t in range(4 * g, 4 * g + 4):
                    pe.wait_ge(xn2_ready, t + 1)
                    c0 = 512 * (g % 2) + P * (t % 4)
                    last = nc.tensor.transpose(ST[:, g // 2, c0:c0 + P], XN2[:, t, :], ident)
                last.then_inc(xt2_done, 1)
            for t in range(NT):
                pe.wait_ge(h2_ready, t // 4 + 1)
                last = mm(OP[:, NE * t:NE * t + NE], H2T[:, P * t:P * t + P], WROUTE[:, :], start=True, stop=True)
            last.then_inc(route_done, 1)
            pe.wait_ge(oh_ready, 1)
            mm(OP[:, 0:P], lowerb[:, :], OHB[:, :], start=True, stop=True)
            mm(OP[:, P:2 * P], onesb[:, :], OHB[:, :], start=True, stop=True).then_inc(rank_done, 1)
            pe.wait_ge(slots_in, 16)
            for q in range((SLOT_TILES + 3) // 4):
                if q >= 2:
                    pe.wait_ge(hst_ready, q - 1)
                for t in range(4 * q, min(4 * q + 4, SLOT_TILES)):
                    c0 = P * (t % 4)
                    last = nc.tensor.transpose(ST[:, q % 2, c0:c0 + P], HS[:, t, :], ident)
                last.then_inc(hst_done, 1)
            pe.wait_ge(hst_ready, (SLOT_TILES + 3) // 4)

            def up(n, b):
                pe.wait_ge(fc_ready, n + 1)
                if not isinstance(n, int) or n >= 2:
                    pe.wait_ge(relu_done, n - 1)
                for c in range(4):
                    last = mm(SC[:, b, P * c:P * c + P], WFC[:, b, P * c:P * c + P], HT[:, bass.ds(n * P, P)],
                              start=True, stop=True)
                last.then_inc(up_done, 1)

            def down(n, b):
                pe.wait_ge(proj_ready, n + 1)
                pe.wait_ge(sq_done, n + 1)
                if not isinstance(n, int) or n >= 2:
                    pe.wait_ge(y_ready, n - 1)
                for c in range(4):
                    last = mm(ST[:, b, 0:E], R2[:, b, P * c:P * c + P], WPROJ[:, b, P * c:P * c + P],
                              start=(c == 0), stop=(c == 3))
                last.then_inc(down_done, 1)

            pe.wait_ge(o_norm, 2 * NP)
            up(0, 0)
            up(1, 1)
            down(0, 0)
            with pe.Fori(2, SLOT_TILES - 1, 2) as n:
                up(n, 0)
                down(n - 1, 1)
                up(n + 1, 1)
                down(n, 0)
            down(SLOT_TILES - 1, 1)


def kernel(**inputs):
    import numpy as np
    import concourse.bacc as bacc
    from concourse.bass_utils import run_bass_kernel_spmd

    g = {k: np.asarray(v) for k, v in inputs.items()}
    w = g["L0_attn_qkv_w"].T.reshape(E, 3, H, D)
    b = g["L0_attn_qkv_b"].reshape(3, H, D)
    table, _ = constants()
    arrays = {
        "x": g["L0_attn_hidden_states"],
        "w_q": w[:, 0].reshape(E, E),
        "w_kv": w[:, 1:].transpose(0, 2, 1, 3).reshape(E, 2 * E),
        "b_q": b[0].reshape(E, 1),
        "b_kv": np.tile(b[1:].transpose(1, 0, 2).reshape(1, 2 * E), (P, 1)),
        "w_r1": g["L0_attn_r_w1"].T,
        "b_r1": np.tile(g["L0_attn_r_b1"], 4).reshape(P, 1),
        "w_r2": np.tile(g["L0_attn_r_w2"].T, (4, 1)),
        "b_r2": np.tile(g["L0_attn_r_b2"], CHUNKS).reshape(P, 1),
        "c_col": g["L0_c"].reshape(E, 1),
        "wmod": g["L0_wmod"],
        "w_route": g["L0_ffn_router_w"].T,
        "w_fc": g["L0_ffn_expert_fc"],
        "w_proj": g["L0_ffn_expert_proj"].transpose(0, 2, 1).reshape(NE, 4, P, E).transpose(0, 2, 1, 3)
        .reshape(NE, P, HD),
        "const": table,
    }
    nc = bacc.Bacc("TRN2", target_bir_lowering=False, num_devices=1)
    arrays = {f"in_{k}": np.ascontiguousarray(a) for k, a in arrays.items()}
    args = [nc.dram_tensor(k, a.shape, mybir.dt.from_np(a.dtype), kind="ExternalInput").ap() for k, a in arrays.items()]
    args.append(nc.dram_tensor("out_0", (1, L, E), F32, kind="ExternalOutput").ap())
    build(nc, *args)
    r = run_bass_kernel_spmd(nc, [arrays], core_ids=[0])
    return r.results[0]["out_0"]
```

```python
import itertools
from contextlib import ExitStack

import concourse.bass as bass
from concourse import mybir

P = 128
F32 = mybir.dt.float32
BF16 = mybir.dt.bfloat16
FP16 = mybir.dt.float16
I32 = mybir.dt.int32
U32 = mybir.dt.uint32
ALU = mybir.AluOpType
ACT = mybir.ActivationFunctionType
AX = mybir.AxisListType

L = 2048
E = 128
H = 16
D = E // H
KEEP = int(L * 0.4)
NT = L // P
NP = H // 2
RH = E // 4
EPS = 1e-5

REM = KEEP - 6 * P
GAP = P - REM
BLOCKS = 7
SHARED = 3
STEPS = 13
EVEN_ORDER = [0, 1, 2, 4, 5, 6, 3]
ODD_ORDER = [3, 0, 1, 2, 4, 5, 6]
NOT_KEPT = 1023.0
PARTS = 3
KROWS = 6 * D
SROWS = KROWS + PARTS
SUNITS = 64
TURNED = [4, 5, 6, 0, 1, 2]
STEP_COLUMN = [TURNED.index(x) for x in EVEN_ORDER[:6]] + [6] + [7 + TURNED.index(x) for x in ODD_ORDER[1:]]
SCORE_COLS = [[(3 * P, 6 * P + REM), (0, 3 * P)], [(10 * P, 13 * P), (6 * P + GAP, 10 * P)]]
LEAD = 46
UNITS = list(range(SUNITS))
for after, kind in ((55, "turn_k"), (54, "turn_m_even"), (22, "turn_m_odd"), (16, "index"), (8, "turn_o")):
    UNITS.insert(after + 1, kind)
RING = 3
FIRST_UNITS = [kind for kind in UNITS if kind != "turn_o"]
FIRST_UNITS.insert(FIRST_UNITS.index(SUNITS - LEAD), "turn_second_k")
EARLY = 7
NE = 8
HD = 4 * E
SLOT_TILES = NT + NE
assert len(UNITS) % RING == 0
ROUNDS = 11
CHUNKS = 8
CT = L // CHUNKS


def constants():
    import numpy as np

    p = np.arange(P)
    cols = {}
    cols["ident"] = np.eye(P)
    cols["same_head"] = (p[:, None] % H == p[None, :] % H)
    cols["before"] = (p[:, None] % H == p[None, :] % H) & (p[:, None] // H < p[None, :] // H)
    cols["place"] = np.broadcast_to(p, (P, P))
    u, js = np.arange(NT) // CHUNKS, np.arange(NT) % CHUNKS
    cols["token"] = (CT * js + P * u)[None, :] + p[:, None]
    cols["blocks"] = np.broadcast_to(EVEN_ORDER + ODD_ORDER, (P, 2 * BLOCKS))
    add = np.zeros((P, NP, STEPS))
    for i in range(NP):
        add[:, i, :6] = 2 * i
        add[:, i, 7:] = 2 * i + 1
        add[:, i, 6] = np.where(p < REM, 2 * i, np.where(p >= GAP, 2 * i + 1, 1 << 20))
    cols["row_add"] = add.reshape(P, -1)
    lo = np.where(p % H % 2 == 0, SHARED * P + REM, SHARED * P)
    cols["gap_from"] = lo[:, None]
    holds = ((p < REM) | (p >= GAP))
    cols["holds"] = holds[:, None]
    cols["number"] = P * np.arange(NT)[None, :] + p[:, None]
    cols["lower"] = (p[:, None] < p[None, :])
    cols["expert"] = np.broadcast_to(np.repeat(np.arange(NE), NT) - NE, (P, NE * NT))
    cols["slot_tile"] = np.broadcast_to(np.repeat(np.arange(SLOT_TILES), NE), (P, SLOT_TILES * NE))
    st = np.zeros((ROUNDS + 1, 4))
    for r in range(ROUNDS):
        st[r] = np.arange(4) * (2.0 ** -4) * 4.0 ** -r
    cols["steps"] = np.broadcast_to(st.reshape(1, -1), (P, 4 * (ROUNDS + 1)))
    at, n = {}, 0
    for k, v in cols.items():
        at[k] = (n, n + v.shape[1])
        n += v.shape[1]
    table = np.concatenate([np.asarray(v, np.float32) for v in cols.values()], axis=1)
    return np.ascontiguousarray(table), at


def has(i, step):
    return not isinstance(i, int) or 0 <= i + step < NP


def product(engine, factor, i):
    return factor * i if isinstance(i, int) else engine.snap(factor * i)


def build(nc, x, w_q, w_kv, b_q, b_kv, w_r1, b_r1, w_r2, b_r2, c_col, wmod, w_route, w_fc, w_proj, const, out):
    _, at = constants()
    NCONST = const.shape[1]
    q_parts_dram = nc.dram_tensor("q_parts_dram", (H, PARTS, D, L), BF16, kind="Internal").ap()
    kv_dram = nc.dram_tensor("kv_dram", (L * H, 2 * D), F32, kind="Internal").ap()

    slots_dram = nc.dram_tensor("slots_dram", (SLOT_TILES * P, E + 1), F32, kind="Internal").ap()

    with ExitStack() as ctx:
        def sb(name, shape, dt=F32):
            return ctx.enter_context(nc.sbuf_tensor(name, shape, dt))

        def ps(name, shape, dt=F32):
            return ctx.enter_context(nc.psum_tensor(name, shape, dt))

        def sem(name):
            return ctx.enter_context(nc.semaphore(name))

        X = sb("X", [P, NT, E])
        C = sb("C", [P, NCONST])
        WQ = sb("WQ", [P, E])
        WKV = sb("WKV", [P, 2 * E])
        WR1 = sb("WR1", [P, RH])
        WR2 = sb("WR2", [P, 2, P])
        WR2S = sb("WR2S", [P, H])
        WMOD = sb("WMOD", [P, 6 * E])
        BQ = sb("BQ", [P, 1])
        BKV = sb("BKV", [P, 2 * E])
        BR1 = sb("BR1", [P, 1])
        BR2 = sb("BR2", [P, 1])
        ccol = sb("ccol", [P, 1])
        csig = sb("csig", [P, 1])
        silu = sb("silu", [P, 1])
        silu_b = sb("silu_b", [P, P])
        ones = sb("ones", [P, P])
        eps = sb("eps", [P, 1])
        warmed = sb("warmed", [P, 1])
        mod_col = sb("mod_col", [P, 6])
        one_ca = sb("one_ca", [P, 1])
        stats = sb("stats", [P, NT, 6])
        mv = sb("mv", [P, NT, 2])
        std = sb("std", [P, NT])
        rstd = sb("rstd", [P, NT])
        XN = sb("XN", [P, NT, E])
        HT = sb("HT", [P, SLOT_TILES * P])
        H1 = sb("H1", [P, 512])
        logit_sigmoid = sb("logit_sigmoid", [P, CT])
        scores_r = sb("scores_r", [P, CT])
        QBUF = sb("QBUF", [P, 3 * L + PARTS * L // 2])
        QF = QBUF[:, 0:L]
        QR = QBUF[:, L:3 * L].rearrange("p (a l) -> p a l", a=2)
        QP = QBUF[:, 3 * L:].bitcast(BF16).rearrange("p (a l) -> p a l", a=PARTS)
        WE = QBUF[:, 0:NE * 2 * HD].rearrange("p (n c) -> p n c", n=NE)
        KV = sb("KV", [P, NT, 2 * E])
        raw_score = sb("raw_score", [P, CT])
        candidate = sb("candidate", [P, ROUNDS + 1, 4])
        counts = sb("counts", [P, ROUNDS, 3], BF16)
        same_head16 = sb("same_head16", [P, P], BF16)
        reached = sb("reached", [P, ROUNDS])
        reach_scratch = sb("reach_scratch", [P, ROUNDS, 3])
        next_from = sb("next_from", [P, ROUNDS, 4])
        above = sb("above", [P, CT])
        ties = sb("ties", [P, CT])
        totals = sb("totals", [P, 2])
        offsets = sb("offsets", [P, 4])
        need = sb("need", [P, 2])
        row_of = sb("row_of", [P, NT, H])
        block_of = sb("block_of", [P, NT, H])
        place16 = sb("place16", [P, P], FP16)
        ABUF = sb("ABUF", [P, 2 * L])
        rows_pool = sb("rows_pool", [P, NT])
        rows_act = sb("rows_act", [P, NT])
        pair_columns = sb("pair_columns", [P, 2, 2, NT * BLOCKS], FP16)
        apart = sb("apart", [P, NT, P], FP16)
        A1 = ABUF[:, :].bitcast(FP16).rearrange("p (b e t q) -> p b e t q", b=2, e=2, t=NT)
        B1 = sb("B1", [P, H, NT, BLOCKS], FP16)
        idx = sb("idx", [P, 2, STEPS], I32)
        G = sb("G", [P, 2, STEPS, 2 * D])
        KR = sb("KR", [P, 2, 2, STEPS, D])
        KS = sb("KS", [P, 2, STEPS, 64], BF16)
        RS = sb("RS", [P, 2, P], BF16)
        VS = sb("VS", [P, 2, STEPS, 32])
        KTM = sb("KTM", [P, 2, STEPS * P], BF16)
        KTE = sb("KTE", [P, 2, STEPS * P], BF16)
        QSM = sb("QSM", [P, 2, L], BF16)
        QSE = sb("QSE", [P, 2, L], BF16)
        identb = sb("identb", [P, P], BF16)
        tile_max = sb("tile_max", [P, 2, SUNITS])
        NM = sb("NM", [P, 3, 2 * NT])
        SM = sb("SM", [P, 2, PARTS, NT], BF16)
        MT = sb("MT", [PARTS * NT, 2, P], BF16)
        PR = sb("PR", [P, 2, L])
        work = PR[:, :, :].rearrange("p a (n c) -> p (a n) c", c=CT)
        count_scratch = work[:, 0:3, :]
        SG, SE, W1, W2, W3, W4, W5 = [work[:, 3 + n, :] for n in range(7)]
        place_int, row_int, block_int = [work[:, 10 + n, :].bitcast(I32) for n in range(3)]
        OS = sb("OS", [P, 512])
        REC = sb("REC", [P, 4, 4, 2])
        AT = sb("AT", [P, NT, E])
        gate = sb("gate", [P, 2, E])
        gsign = sb("gsign", [P, 2, E])
        gabs = sb("gabs", [P, 2, E])
        gneg = sb("gneg", [P, 2, E])
        one_cb = sb("one_cb", [P, 1])
        WROUTE = sb("WROUTE", [P, NE])
        lowerb = sb("lowerb", [P, P], BF16)
        onesb = sb("onesb", [P, P], BF16)
        zeros = sb("zeros", [P, E + 1])
        LM = sb("LM", [P, 4, NT])
        LE = KTM[:, 0, 0:2 * 6 * P].bitcast(F32).rearrange("p (a c) -> p a c", a=6)
        OH = sb("OH", [P, NE, NT])
        OHB = sb("OHB", [P, NE * NT], BF16)
        TOT = sb("TOT", [P, NE, NT])
        CUM = sb("CUM", [P, 1 + NE * NT])
        EN = sb("EN", [P, 6, NE])
        ENI = sb("ENI", [P, 2, NE], I32)
        SLB = sb("SLB", [P, NE, NT])
        SLC = sb("SLC", [P, NE, NT])
        slotF = sb("slotF", [P, NT])
        slot = sb("slot", [P, NT], I32)
        owner = sb("owner", [P, SLOT_TILES], I32)
        TE = KTM[:, 1, 0:2 * SLOT_TILES * NE].bitcast(F32).rearrange("p (s e) -> p s e", e=NE)
        TEF = sb("TEF", [P, SLOT_TILES])
        TEI = sb("TEI", [P, SLOT_TILES + 1], I32)
        B0 = work[:, 0:7, :].rearrange("p n c -> p (n c)").rearrange("p (h t b) -> p h t b", h=H, t=NT)
        X2 = X[:, :, :]
        XN2 = ABUF[:, 0:NT * (E + 1)].rearrange("p (t e) -> p t e", e=E + 1)
        GAT = KV[:, :, 0:E]
        WB = QSM[:, :, :].bitcast(F32)
        RELU = QSE[:, :, :].bitcast(F32)
        RL, R2 = RELU[:, 0, :].rearrange("p (a c) -> p a c", a=2), RELU[:, 1, :].rearrange("p (a c) -> p a c", a=2)
        WFC, WPROJ = WB[:, :, 0:HD], WB[:, :, HD:]
        HS = KV[:, :, :].rearrange("p t c -> p (t c)")[:, 0:SLOT_TILES * (E + 1)].rearrange("p (t e) -> p t e", e=E + 1)
        H2T = AT[:, :, :].rearrange("p t e -> p (t e)")
        YS = PR[:, :, :].rearrange("p a c -> p (a c)")[:, 0:SLOT_TILES * P].rearrange("p (t e) -> p t e", e=E)

        ST = ps("ST", [P, 2, 1024])
        SC = ps("SC", [P, RING, 512])
        OP = ps("OP", [P, 512])
        MP, MI = SC[:, 1, :], SC[:, 2, :]

        def bank(pos):
            return SC[:, pos % RING, :]

        def bank16(pos):
            return SC[:, pos % RING, :].bitcast(BF16)

        def cc(name):
            a, b = at[name]
            return C[:, a:b]

        ident, same_head, before = cc("ident"), cc("same_head"), cc("before")
        token, blocks, row_add, steps = cc("token"), cc("blocks"), cc("row_add"), cc("steps")

        dve_step = sem("dve_step")
        pool_step = sem("pool_step")
        tail_step = sem("tail_step")
        const_in = sem("const_in")
        x_in = [sem(f"x_in_{g}") for g in range(4)]
        mod_in = sem("mod_in")
        kv_biased = sem("kv_biased")
        warm = sem("warm")
        w_in = sem("w_in")
        wr2_zero = sem("wr2_zero")
        wr2_in = sem("wr2_in")
        silu_ready = sem("silu_ready")
        mod_done = sem("mod_done")
        mod_ready = sem("mod_ready")
        stats_ready = sem("stats_ready")
        std_ready = sem("std_ready")
        xn_ready = sem("xn_ready")
        xt_done = sem("xt_done")
        ht_ready = sem("ht_ready")
        h1_done = sem("h1_done")
        h1_ready = sem("h1_ready")
        logit_done = sem("logit_done")
        score0 = sem("score0")
        q_done = sem("q_done")
        q_ready = sem("q_ready")
        kv_done = sem("kv_done")
        kv_ready = sem("kv_ready")
        qpart_a = sem("qpart_a")
        qpart_p = sem("qpart_p")
        qparts_out = sem("qparts_out")
        kv_out = sem("kv_out")
        search_dve = sem("search_dve")
        search_pe = sem("search_pe")
        sel_pe = sem("sel_pe")
        pos_done = sem("pos_done")
        pos_ready = sem("pos_ready")
        onehot_ready = sem("onehot_ready")
        idx_mm = sem("idx_mm")
        idx_ready = sem("idx_ready")
        gathered = sem("gathered")
        gathered_early = sem("gathered_early")
        prep_ready = sem("prep_ready")
        prep_early = sem("prep_early")
        v_ready = sem("v_ready")
        places_taken = sem("places_taken")
        rows_act_ready = sem("rows_act_ready")
        pair_columns_ready = sem("pair_columns_ready")
        onehot_odd = sem("onehot_odd")
        apart_ready = sem("apart_ready")
        paced = sem("paced")
        turning = sem("turning")
        k_step = sem("k_step")
        v_step = sem("v_step")
        init_pool = sem("init_pool")
        init_dve = sem("init_dve")
        ktr_done = sem("ktr_done")
        ktr_early = sem("ktr_early")
        kt_odd = sem("kt_odd")
        kt_even = sem("kt_even")
        kte_ready = sem("kte_ready")
        qsm_even = sem("qsm_even")
        qsm_odd = sem("qsm_odd")
        qse_even = sem("qse_even")
        qse_odd = sem("qse_odd")
        s_filled = sem("s_filled")
        s_reduced = sem("s_reduced")
        m_chain = sem("m_chain")
        m_split_even = sem("m_split_even")
        m_split_odd = sem("m_split_odd")
        mtr_even = sem("mtr_even")
        mtr_odd = sem("mtr_odd")
        mt_even = sem("mt_even")
        mt_odd = sem("mt_odd")
        mrow_even = sem("mrow_even")
        mrow_odd = sem("mrow_odd")
        st_filled = sem("st_filled")
        exp_done = sem("exp_done")
        pv_done = sem("pv_done")
        o_copied = sem("o_copied")
        otr_done = sem("otr_done")
        o_norm = sem("o_norm")
        rec_ready = sem("rec_ready")
        out_in = sem("out_in")
        b_parts = sem("b_parts")
        we_in = sem("we_in")
        slots_zero = sem("slots_zero")
        gate_ready = sem("gate_ready")
        tail_dve = sem("tail_dve")
        gated = sem("gated")
        x2_ready = sem("x2_ready")
        stats2_ready = sem("stats2_ready")
        std2_ready = sem("std2_ready")
        xn2_ready = sem("xn2_ready")
        xt2_done = sem("xt2_done")
        h2_ready = sem("h2_ready")
        route_done = sem("route_done")
        exp2_done = sem("exp2_done")
        oh_ready = sem("oh_ready")
        rank_done = sem("rank_done")
        slot_ready = sem("slot_ready")
        scattered = sem("scattered")
        slots_in = sem("slots_in")
        hst_done = sem("hst_done")
        hst_ready = sem("hst_ready")
        owner_ready = sem("owner_ready")
        added = sem("added")
        fc_ready = sem("fc_ready")
        proj_ready = sem("proj_ready")
        up_done = sem("up_done")
        relu_done = sem("relu_done")
        sq_done = sem("sq_done")
        down_done = sem("down_done")
        y_ready = sem("y_ready")
        tile_ready = sem("tile_ready")

        block = ctx.enter_context(nc.Block())
        x_t = x[0].rearrange("(t p) e -> p t e", p=P)
        out_t = out[0].rearrange("(t p) e -> p t e", p=P)
        kv_t = kv_dram.rearrange("(t p h) d -> p t (h d)", p=P, h=H)

        LEAD_UNITS = list(range(36)) + ["turn_m_even"] + list(range(36, LEAD))

        @block.sync
        def _(sp):
            for g in range(4):
                sp.dma_start(X[:, 4 * g:4 * g + 4, :], x_t[:, 4 * g:4 * g + 4, :]).then_inc(x_in[g], 16)
                if g == 1:
                    sp.dma_start(C[:, :], const).then_inc(const_in, 16)
            for dst, src in ((WR1, w_r1), (WR2S, w_r2), (BR1, b_r1), (BR2, b_r2), (WQ, w_q), (WKV, w_kv), (BQ, b_q),
                             (BKV, b_kv), (WROUTE, w_route)):
                sp.dma_start(dst[:, :], src).then_inc(w_in, 16)
            sp.wait_ge(qpart_a, 2)
            sp.wait_ge(qpart_p, 2)
            sp.wait_ge(q_ready, 8)
            for part in range(PARTS):
                sp.dma_start(q_parts_dram[:, part, :, :], QP[:, part, :]).then_inc(qparts_out, 16)
            sp.wait_ge(kv_biased, NT // 2)
            sp.dma_start(kv_t, KV[:, :, :]).then_inc(kv_out, 16)
            sp.wait_ge(qparts_out, 16 * PARTS)
            sp.wait_ge(init_pool, 5)

            def load_q(dst, i, par, loaded):
                for e in range(2):
                    src = q_parts_dram[bass.ds(2 * i + e, 1), :, :, :].rearrange("h a d l -> (h a d) l")
                    for row, n in ((0, 3), (3, 2), (5, 1)):
                        sp.dma_start(dst[64 * e + D * row:64 * e + D * (row + n), par, :],
                                     src[0:D * n, :]).then_inc(loaded, 16)

            def m_rows(i, par, e):
                sp.wait_ge([mt_even, mt_odd][e], i + 1)
                dst = QSE[64 * e + KROWS:64 * e + SROWS, par, :].rearrange("a (t q) -> a t q", q=P)
                sp.dma_start(dst, MT[:, e, :]).then_inc([mrow_even, mrow_odd][e], 16)

            def feed(i, b):
                if has(i, 1):
                    if has(i, -1):
                        sp.wait_ge(st_filled, 2 * STEPS * i)
                    load_q(QSE, i + 1, 1 - b, [qse_even, qse_odd][1 - b])
                m_rows(i, b, 1)
                if has(i, 2):
                    sp.wait_ge(s_filled, SUNITS * (i + 1))
                    load_q(QSM, i + 2, b, [qsm_even, qsm_odd][b])
                if has(i, 1):
                    m_rows(i + 1, 1 - b, 0)

            load_q(QSM, 0, 0, qsm_even)
            load_q(QSE, 0, 0, qse_even)
            load_q(QSM, 1, 1, qsm_odd)
            m_rows(0, 0, 0)
            feed(0, 0)
            with sp.Fori(1, NP - 4, 2) as i:
                feed(i, 1)
                feed(i + 1, 0)
            for i in range(NP - 3, NP):
                feed(i, i % 2)
            for n, w_part in enumerate((w_fc, w_proj)):
                sp.dma_start(WE[:, :, HD * n:HD * (n + 1)], w_part.rearrange("n p c -> p n c"))\
                    .then_inc(we_in, 16)
            sp.wait_ge(x2_ready, 2)
            sp.dma_start(out_t, X2).then_inc(out_in, 16)
            sp.wait_ge(scattered, 16 * NT)
            sp.dma_start(HS[:, :, :], slots_dram.rearrange("(t p) e -> p t e", p=P)).then_inc(slots_in, 16)
            sp.wait_ge(added, 16 * SLOT_TILES)
            sp.wait_ge(slots_zero, 16)

        @block.gpsimd
        def _(pool):
            next_step = itertools.count(1).__next__

            nc.gpsimd.memset(WR2[:, :, :], 0.0).then_inc(wr2_zero, 1)
            nc.gpsimd.memset(zeros[:, 0:E], 0.0).then_inc(wr2_zero, 1)
            nc.gpsimd.memset(zeros[:, E:E + 1], float(1 << 20)).then_inc(wr2_zero, 1)
            nc.gpsimd.memset(KS[:, :, :, :], 0.0).then_inc(pool_step, 1)
            pool.wait_ge(pool_step, next_step())
            nc.gpsimd.memset(VS[:, :, :, :], 0.0).then_inc(pool_step, 1)
            pool.wait_ge(pool_step, next_step())
            nc.gpsimd.memset(RS[:, :, :], 0.0).then_inc(init_pool, 1)
            nc.gpsimd.memset(G[:, :, :, :], 0.0).then_inc(init_pool, 1)
            pool.wait_ge(wr2_zero, 3)
            pool.wait_ge(w_in, 16 * 9)
            for j in range(4):
                for u in range(2):
                    c0 = 32 * j + H * u
                    nc.gpsimd.tensor_copy(WR2[32 * j:32 * j + RH, u, c0:c0 + H], WR2S[32 * j:32 * j + RH, :])\
                        .then_inc(wr2_in, 1)
                    pool.wait_ge(wr2_in, 2 * j + u + 1)
            nc.gpsimd.memset(KTM[:, :, :], 0.0).then_inc(init_pool, 1)
            nc.gpsimd.memset(QSM[:, :, :], 0.0).then_inc(init_pool, 1)
            nc.gpsimd.memset(QSE[:, :, :], 0.0).then_inc(init_pool, 1)
            pool.wait_ge(const_in, 16)
            holds = cc("holds")
            for b in range(2):
                nc.gpsimd.memset(KS[:, b, :, KROWS:SROWS], 1.0).then_inc(pool_step, 1)
                pool.wait_ge(pool_step, next_step())
                nc.gpsimd.tensor_copy(KS[:, b, 6, KROWS:SROWS], holds.to_broadcast([P, PARTS])).then_inc(pool_step, 1)
                pool.wait_ge(pool_step, next_step())
                nc.gpsimd.memset(VS[:, b, 0:6, D:D + 1], 1.0).then_inc(pool_step, 1)
                pool.wait_ge(pool_step, next_step())
                nc.gpsimd.memset(VS[:, b, 7:13, 16 + D:16 + D + 1], 1.0).then_inc(pool_step, 1)
                pool.wait_ge(pool_step, next_step())
                nc.gpsimd.tensor_copy(VS[0:64, b, 6, D:D + 1], holds[0:64, :]).then_inc(pool_step, 1)
                pool.wait_ge(pool_step, next_step())
                nc.gpsimd.tensor_copy(VS[64:128, b, 6, 16 + D:16 + D + 1], holds[64:128, :]).then_inc(pool_step, 1)
                pool.wait_ge(pool_step, next_step())
            pool.wait_ge(w_in, 16 * 9)

            def add_bias(n):
                pool.wait_ge(kv_ready, n + 1)
                kv2 = KV[:, 2 * n:2 * n + 2, :]
                nc.gpsimd.tensor_tensor(kv2, kv2, BKV[:, :].rearrange("p (a c) -> p a c", a=1).to_broadcast([P, 2, 2 * E]),
                                        ALU.add).then_inc(kv_biased, 1)

            pool.wait_ge(q_ready, 8)
            nc.gpsimd.tensor_tensor(QR[:, 0, :], QF[:, :], QP[:, 0, :], ALU.subtract).then_inc(qpart_p, 1)
            for n in range(3):
                add_bias(n)
            pool.wait_ge(qpart_a, 1)
            nc.gpsimd.tensor_tensor(QR[:, 1, :], QR[:, 0, :], QP[:, 1, :], ALU.subtract).then_inc(qpart_p, 1)
            for n in range(3, NT // 2):
                add_bias(n)

            pool.wait_ge(kv_out, 16)
            pool.wait_ge(init_pool, 5)

            def onehot(i, b):
                pool.wait_ge(idx_mm, i - 1)
                pool.wait_ge(prep_ready, i)
                pool.sem_inc(paced, 1)
                nc.gpsimd.tensor_copy(rows_pool[:, :], row_of[:, :, bass.ds(2 * i, 1)].rearrange("p t a -> p (t a)"))\
                    .then_inc(places_taken, 1)
                pool.wait_ge(places_taken, i - 2)
                pool.sem_inc(paced, 1)
                for t in range(NT):
                    last = nc.gpsimd.tensor_scalar(A1[:, b, 0, t, :], place16[:, :], rows_pool[:, t:t + 1], None,
                                                   ALU.is_equal)
                last.then_inc(onehot_ready, 1)

            def gathers(i, b, steps=range(STEPS), fetched=gathered):
                pool.wait_ge(idx_ready, i + 1)
                if has(i, -1):
                    pool.wait_ge(v_ready, i)
                    pool.sem_inc(paced, 1)
                for s in steps:
                    pool.indirect_dma_start(
                        G[:, b, s, :], None, kv_dram,
                        bass.IndirectOffsetOnAxis(ap=idx[:, b, s:s + 1].bitcast(U32), axis=0),
                        bounds_check=L * H - 1, oob_is_err=False).then_inc(fetched, 16)

            def prep(i, b, s0=0, s1=STEPS):
                if s1 < STEPS:
                    pool.wait_ge(gathered_early, 16 * EARLY)
                else:
                    pool.wait_ge(gathered, 16 * (STEPS * (i + 1) - EARLY))
                pool.sem_inc(paced, 1)
                steps_done = 6 if s0 else 6 * i + 4 if has(i, -1) else 0
                k = G[:, b, s0:s1, 0:D]
                if has(i, -2):
                    pool.wait_ge(ktr_done, i - 1)
                    pool.sem_inc(paced, 1)

                def rep(ap, n):
                    return ap.rearrange("p s (a d) -> p s a d", a=1).to_broadcast([P, s1 - s0, n, D])

                def stack(c, n):
                    return KS[:, b, s0:s1, D * c:D * (c + n)].rearrange("p s (a d) -> p s a d", a=n)

                nc.gpsimd.tensor_copy(stack(0, 3), rep(k, 3)).then_inc(k_step, 1)
                pool.wait_ge(k_step, steps_done + 1)
                pool.sem_inc(paced, 1)
                nc.gpsimd.tensor_tensor(KR[:, b, 0, s0:s1, :], k, KS[:, b, s0:s1, 0:D], ALU.subtract).then_inc(k_step, 1)
                pool.wait_ge(k_step, steps_done + 2)
                pool.sem_inc(paced, 1)
                nc.gpsimd.tensor_copy(stack(3, 2), rep(KR[:, b, 0, s0:s1, :], 2)).then_inc(k_step, 1)
                pool.wait_ge(k_step, steps_done + 3)
                pool.sem_inc(paced, 1)
                nc.gpsimd.tensor_tensor(KR[:, b, 1, s0:s1, :], KR[:, b, 0, s0:s1, :], KS[:, b, s0:s1, 3 * D:4 * D],
                                        ALU.subtract).then_inc(k_step, 1)
                pool.wait_ge(k_step, steps_done + 4)
                pool.sem_inc(paced, 1)
                if s0:
                    nc.gpsimd.tensor_copy(stack(5, 1), rep(KR[:, b, 1, s0:s1, :], 1)).then_inc(prep_ready, 1)
                    return
                nc.gpsimd.tensor_copy(stack(5, 1), rep(KR[:, b, 1, s0:s1, :], 1)).then_inc(k_step, 1)
                pool.wait_ge(k_step, steps_done + 5)
                pool.sem_inc(paced, 1)
                nc.gpsimd.tensor_copy(RS[0:64, b, 0:64], KS[0:64, b, 6, :]).then_inc(k_step, 1)
                pool.wait_ge(k_step, steps_done + 6)
                pool.sem_inc(paced, 1)
                nc.gpsimd.tensor_copy(RS[64:128, b, 64:128], KS[64:128, b, 6, :])\
                    .then_inc(prep_early if s1 < STEPS else prep_ready, 1)

            def prep_v(i, b):
                pool.wait_ge(prep_ready, i + 1)
                if has(i, -2):
                    pool.wait_ge(pv_done, STEPS * (i - 1))
                    pool.sem_inc(paced, 1)
                nc.gpsimd.tensor_copy(VS[:, b, 0:6, 0:D], G[:, b, 0:6, D:2 * D]).then_inc(v_step, 1)
                pool.wait_ge(v_step, 3 * i + 1)
                pool.sem_inc(paced, 1)
                nc.gpsimd.tensor_copy(VS[:, b, 7:13, 16:16 + D], G[:, b, 7:13, D:2 * D]).then_inc(v_step, 1)
                pool.wait_ge(v_step, 3 * i + 2)
                pool.sem_inc(paced, 1)
                nc.gpsimd.tensor_copy(VS[0:64, b, 6, 0:D], G[0:64, b, 6, D:2 * D]).then_inc(v_step, 1)
                pool.wait_ge(v_step, 3 * i + 3)
                pool.sem_inc(paced, 1)
                nc.gpsimd.tensor_copy(VS[64:128, b, 6, 16:16 + D], G[64:128, b, 6, D:2 * D])\
                    .then_inc(v_ready, 1)

            gathers(0, 0, range(EARLY), gathered_early)
            prep(0, 0, 0, EARLY)
            pool.wait_ge(prep_early, 1)
            gathers(0, 0, range(EARLY, STEPS))
            prep(0, 0, EARLY, STEPS)
            prep_v(0, 0)
            gathers(1, 1)
            prep(1, 1)
            prep_v(1, 1)
            def prepare(i, b):
                gathers(i, b)
                prep(i, b)
                if has(i, 1):
                    onehot(i + 1, 1 - b)
                prep_v(i, b)

            with pool.Fori(2, NP - 3, 2) as i:
                prepare(i, 0)
                prepare(i + 1, 1)
            for i in range(NP - 2, NP):
                prepare(i, i % 2)
            pool.wait_ge(gate_ready, 1)
            pool.wait_ge(o_norm, 2 * (NP - 1))
            for g in range(4):
                nc.gpsimd.tensor_tensor(GAT[:, 4 * g:4 * g + 4, 0:E - 2 * D], AT[:, 4 * g:4 * g + 4, 0:E - 2 * D],
                                        gate[:, 0:1, 0:E - 2 * D].to_broadcast([P, 4, E - 2 * D]), ALU.mult)\
                    .then_inc(gated, 1)
            pool.wait_ge(slot_ready, 1)
            pool.wait_ge(slots_zero, 16)
            for t in range(NT):
                pool.indirect_dma_start(
                    slots_dram, bass.IndirectOffsetOnAxis(ap=slot[:, t:t + 1].bitcast(U32), axis=0), XN2[:, t, :], None,
                    bounds_check=SLOT_TILES * P - 1, oob_is_err=False).then_inc(scattered, 16)
            pool.wait_ge(owner_ready, 1)
            pool.wait_ge(out_in, 16)
            for n in range(SLOT_TILES):
                pool.wait_ge(y_ready, n + 1)
                pool.indirect_dma_start(
                    out[0], bass.IndirectOffsetOnAxis(ap=owner[:, n:n + 1].bitcast(U32), axis=0), YS[:, n, :], None,
                    bounds_check=L - 1, oob_is_err=False, compute_op=ALU.add).then_inc(added, 16)

        @block.scalar
        def _(act):
            act.dma_start(ccol[:, :], c_col).then_inc(mod_in, 16)
            act.dma_start(WMOD[:, :], wmod).then_inc(mod_in, 16)
            act.wait_ge(mod_in, 32)
            nc.scalar.activation(csig[:, :], ccol[:, :], ACT.Sigmoid).then_inc(silu_ready, 1)
            for g in range(4):
                act.wait_ge(stats_ready, 8 * g + 8)
                nc.scalar.activation(std[:, 4 * g:4 * g + 4], mv[:, 4 * g:4 * g + 4, 1], ACT.Sqrt,
                                     bias=eps[:, 0:1]).then_inc(std_ready, 1)
            nc.scalar.activation(warmed[:, 0:1], ccol[:, :], ACT.Sigmoid).then_inc(warm, 1)
            act.wait_ge(wr2_zero, 3)
            act.dma_start(slots_dram.rearrange("(t p) e -> p t e", p=P),
                          zeros[:, :].rearrange("p (a e) -> p a e", a=1).to_broadcast([P, SLOT_TILES, E + 1]))\
               .then_inc(slots_zero, 16)
            act.wait_ge(mod_ready, 2)
            for g in range(4):
                act.wait_ge(xt_done, g + 1)
                nc.scalar.activation(HT[:, 512 * g:512 * g + 512], ST[:, g // 2, 512 * (g % 2):512 * (g % 2) + 512],
                                     ACT.Identity, bias=mod_col[:, 0:1], scale=one_ca[:, 0:1])\
                    .then_inc(ht_ready, 1)
            act.wait_ge(w_in, 16 * 9)
            act.wait_ge(h1_done, 1)
            nc.scalar.activation(H1[:, :], SC[:, 0, :], ACT.Relu, bias=BR1[:, 0:1]).then_inc(h1_ready, 1)
            act.wait_ge(logit_done, 1)
            nc.scalar.activation(logit_sigmoid[:, :], SC[:, 1, 0:CT], ACT.Sigmoid, bias=BR2[:, 0:1]).then_inc(score0, 1)
            act.wait_ge(score0, 1)
            nc.scalar.activation(raw_score[:, :], logit_sigmoid[:, :], ACT.Sigmoid).then_inc(score0, 1)
            for g in range(4):
                act.wait_ge(q_done, g + 1)
                src = ST[:, g // 2, 512 * (g % 2):512 * (g % 2) + 512]
                nc.scalar.activation(QF[:, 512 * g:512 * g + 512], src, ACT.Identity, bias=BQ[:, 0:1])\
                    .then_inc(q_ready, 1)
                nc.scalar.activation(QP[:, 0, 512 * g:512 * g + 512], src, ACT.Identity, bias=BQ[:, 0:1])\
                    .then_inc(q_ready, 1)
            act.wait_ge(warm, 1)
            nc.scalar.activation(warmed[:, 0:1], ccol[:, :], ACT.Exp).then_inc(warm, 1)
            for n in range(NT // 2):
                act.wait_ge(kv_done, n + 1)
                nc.scalar.activation(KV[:, 2 * n:2 * n + 2, :].rearrange("p t c -> p (t c)"),
                                     [OP[:, :], MI][n % 2], ACT.Copy).then_inc(kv_ready, 1)
                if n == 2:
                    act.wait_ge(qpart_p, 1)
                    nc.scalar.activation(QP[:, 1, :], QR[:, 0, :], ACT.Copy).then_inc(qpart_a, 1)
            act.wait_ge(qpart_p, 2)
            nc.scalar.activation(QP[:, 2, :], QR[:, 1, :], ACT.Copy).then_inc(qpart_a, 1)

            def copy_kt(i, b, pos):
                act.wait_ge(ktr_done, i + 1)
                turned = bank16(pos) if has(i, -1) else OP[:, :].bitcast(BF16)
                nc.scalar.activation(KTM[64:128, b, 6 * P:13 * P], turned[64:128, 0:7 * P], ACT.Copy)\
                    .then_inc(kt_odd, 1)

            def copy_o(i):
                act.wait_ge(pv_done, STEPS * (i + 1))
                if has(i, -1):
                    act.wait_ge(otr_done, i)
                nc.scalar.activation(OS[:, :], OP[:, :], ACT.Copy).then_inc(o_copied, 1)

            KT_STEP = UNITS.index("turn_k") * STEPS // len(UNITS)

            def take_columns(i, b):
                act.wait_ge(onehot_odd, i)
                act.wait_ge(idx_mm, i - 1)
                nc.scalar.activation(rows_act[:, :], row_of[:, :, bass.ds(2 * i + 1, 1)].rearrange("p t a -> p (t a)"),
                                     ACT.Copy).then_inc(rows_act_ready, 1)
                nc.scalar.activation(pair_columns[:, b, :, :],
                                     B1[:, bass.ds(2 * i, 2), :, :].rearrange("p e t c -> p e (t c)"),
                                     ACT.Copy).then_inc(pair_columns_ready, 1)
                act.wait_ge(rows_act_ready, i - 1)

            def distances(i, b, t):
                places = rows_act[:, t:t + 1] if has(i, -2) else row_of[:, t, 2 * i + 1:2 * i + 2]
                nc.scalar.activation(apart[:, t, :], place16[:, :], ACT.Abs, scale=-1.0, bias=places)\
                    .then_inc(apart_ready, 1)

            def onehot_of_distances(i, b):
                act.wait_ge(apart_ready, NT * (i + 1))
                if has(i, -2):
                    act.wait_ge(idx_mm, i - 1)
                nc.scalar.activation(A1[:, b, 1, :, :], apart[:, :, :], ACT.Relu, scale=-1.0, bias=ones[:, 0:1])\
                    .then_inc(onehot_odd, 1)

            act.wait_ge(pos_ready, 2)
            for i in range(2):
                if i:
                    act.wait_ge(onehot_odd, i)
                for t in range(NT):
                    distances(i, i, t)
                onehot_of_distances(i, i)
            act.wait_ge(onehot_ready, 4)
            take_columns(2, 0)
            for t in range(NT):
                distances(2, 0, t)
            onehot_of_distances(2, 0)

            copy_kt(0, 0, 2)

            def weights(i, b):
                steps_before, halves_before = product(act, STEPS, i), product(act, 2 * STEPS, i)
                for s in range(STEPS):
                    for half in range(2):
                        act.wait_ge(st_filled, halves_before + 2 * s + half + 1)
                        if has(i, -1) or s >= 2:
                            act.wait_ge(pv_done, steps_before + s - 1)
                        nc.scalar.activation(PR[:, (b + s) % 2, 1024 * half:1024 * half + 1024], ST[:, half, :], ACT.Exp,
                                             scale=float(D) ** -0.5).then_inc(exp_done, 1)
                        if half == 0 and s == KT_STEP and has(i, 2):
                            copy_kt(i + 2, b, UNITS.index("turn_k"))
                    second = FIRST_UNITS.index("turn_second_k")
                    if not has(i, -1) and s == second * STEPS // len(UNITS):
                        copy_kt(1, 1, second)
                    if s == 0 and has(i, -1):
                        copy_o(i - 1)
                    if has(i, 3):
                        if s == 0:
                            take_columns(i + 3, 1 - b)
                        if 1 <= s <= NT // 2:
                            distances(i + 3, 1 - b, 2 * s - 2)
                            distances(i + 3, 1 - b, 2 * s - 1)
                        if s == NT // 2 + 1:
                            onehot_of_distances(i + 3, 1 - b)

            weights(0, 0)
            with act.Fori(1, NP - 4, 2) as i:
                weights(i, 1)
                weights(i + 1, 0)
            for i in range(NP - 3, NP):
                weights(i, i % 2)
            copy_o(NP - 1)
            def turned2(g):
                act.wait_ge(xt2_done, g + 1)
                nc.scalar.activation(H2T[:, 512 * g:512 * g + 512], ST[:, g // 2, 512 * (g % 2):512 * (g % 2) + 512],
                                     ACT.Identity, bias=mod_col[:, 3:4], scale=one_cb[:, 0:1])\
                    .then_inc(h2_ready, 1)

            for g in range(4):
                act.wait_ge(stats2_ready, 8 * g + 8)
                nc.scalar.activation(std[:, 4 * g:4 * g + 4], mv[:, 4 * g:4 * g + 4, 1], ACT.Sqrt,
                                     bias=eps[:, 0:1]).then_inc(std2_ready, 1)
                if g:
                    turned2(g - 1)
            turned2(3)
            act.wait_ge(tail_dve, 2)
            nc.scalar.activation(LE[:, 1, :], LE[:, 0, :], ACT.Exp).then_inc(exp2_done, 1)
            for q in range((SLOT_TILES + 3) // 4):
                n = min(4, SLOT_TILES - 4 * q)
                act.wait_ge(hst_done, q + 1)
                nc.scalar.activation(HT[:, 512 * q:512 * q + P * n], ST[:, q % 2, 0:P * n],
                                     ACT.Identity, bias=mod_col[:, 3:4], scale=one_cb[:, 0:1])\
                    .then_inc(hst_ready, 1)
            def squared_relu(n, b):
                act.wait_ge(up_done, n + 1)
                if not isinstance(n, int) or n >= 2:
                    act.wait_ge(down_done, n - 1)
                nc.scalar.activation(RL[:, b, :], SC[:, b, :], ACT.Relu).then_inc(relu_done, 1)
                act.wait_ge(relu_done, n + 1)
                nc.scalar.activation(R2[:, b, :], RL[:, b, :], ACT.Square).then_inc(sq_done, 1)

            squared_relu(0, 0)
            squared_relu(1, 1)
            with act.Fori(2, SLOT_TILES - 1, 2) as n:
                squared_relu(n, 0)
                squared_relu(n + 1, 1)

        @block.vector
        def _(dve):
            v = nc.vector
            next_step = itertools.count(1).__next__

            v.memset(ones[:, :], 1.0).then_inc(dve_step, 1)
            dve.wait_ge(dve_step, next_step())
            v.memset(eps[:, :], EPS).then_inc(dve_step, 1)
            dve.wait_ge(dve_step, next_step())

            def statistics(g):
                dve.wait_ge(x_in[g], 16)
                for t in range(4 * g, 4 * g + 4):
                    v.bn_stats(stats[:, t, :], X[:, t, :]).then_inc(stats_ready, 1)
                for t in range(4 * g, 4 * g + 4):
                    dve.wait_ge(stats_ready, 8 * g + t - 4 * g + 1)
                    v.bn_aggr(mv[:, t, :], stats[:, t, :]).then_inc(stats_ready, 1)

            def normalize1(g):
                dve.wait_ge(std_ready, g + 1)
                v.reciprocal(rstd[:, 4 * g:4 * g + 4], std[:, 4 * g:4 * g + 4]).then_inc(dve_step, 1)
                dve.wait_ge(dve_step, next_step())
                for t in range(4 * g, 4 * g + 4):
                    v.tensor_scalar(XN[:, t, :], X[:, t, :], mv[:, t, 0:1], rstd[:, t:t + 1], ALU.subtract,
                                    ALU.mult).then_inc(xn_ready, 1)

            statistics(0)
            statistics(1)
            dve.wait_ge(silu_ready, 1)
            v.tensor_tensor(silu[:, :], ccol[:, :], csig[:, :], ALU.mult).then_inc(dve_step, 1)
            dve.wait_ge(dve_step, next_step())
            v.tensor_scalar(silu_b[:, :], ones[:, :], silu[:, 0:1], None, ALU.mult).then_inc(silu_ready, 1)
            normalize1(0)
            statistics(2)
            normalize1(1)
            statistics(3)
            normalize1(2)
            dve.wait_ge(mod_done, 1)
            v.tensor_copy(mod_col[:, :], OP[:, 0:6]).then_inc(mod_ready, 1)
            dve.wait_ge(mod_ready, 1)
            v.tensor_scalar(one_ca[:, :], mod_col[:, 1:2], 1.0, None, ALU.add).then_inc(mod_ready, 1)
            normalize1(3)
            v.tensor_scalar(one_cb[:, :], mod_col[:, 4:5], 1.0, None, ALU.add).then_inc(dve_step, 1)
            dve.wait_ge(dve_step, next_step())
            g_ps = OP[:, P:3 * P]
            g2 = "p a e -> p (a e)"
            v.tensor_scalar(gsign[:, :, :].rearrange(g2), g_ps, 0.0, 2.0, ALU.is_ge, ALU.mult).then_inc(dve_step, 1)
            dve.wait_ge(dve_step, next_step())
            v.tensor_scalar(gneg[:, :, :].rearrange(g2), g_ps, -1.0, 0.25, ALU.mult, ALU.max).then_inc(dve_step, 1)
            dve.wait_ge(dve_step, next_step())
            v.tensor_tensor(gabs[:, :, :].rearrange(g2), g_ps, gneg[:, :, :].rearrange(g2), ALU.max)\
                .then_inc(dve_step, 1)
            dve.wait_ge(dve_step, next_step())
            v.scalar_tensor_tensor(gate[:, :, :], gsign[:, :, :], -1.0, gabs[:, :, :], ALU.add, ALU.mult)\
                .then_inc(gate_ready, 1)
            v.memset(onesb[:, :], 1.0).then_inc(dve_step, 1)
            dve.wait_ge(dve_step, next_step())
            v.memset(TEI[:, SLOT_TILES:], 0).then_inc(dve_step, 1)
            dve.wait_ge(dve_step, next_step())
            v.memset(CUM[:, 0:1], 0.0).then_inc(dve_step, 1)
            dve.wait_ge(dve_step, next_step())
            dve.wait_ge(const_in, 16)
            v.tensor_copy(lowerb[:, :], cc("lower")).then_inc(dve_step, 1)
            dve.wait_ge(dve_step, next_step())
            v.tensor_copy(same_head16[:, :], same_head).then_inc(dve_step, 1)
            dve.wait_ge(dve_step, next_step())
            v.tensor_copy(place16[:, :], cc("place")).then_inc(dve_step, 1)
            dve.wait_ge(dve_step, next_step())
            v.tensor_copy(identb[:, :], ident).then_inc(init_dve, 1)
            dve.wait_ge(score0, 2)
            v.tensor_scalar(scores_r[:, :], raw_score[:, :], 0.5, None, ALU.max).then_inc(dve_step, 1)
            dve.wait_ge(dve_step, next_step())
            v.tensor_scalar(candidate[:, 0, :], steps[:, 0:4], 0.5, None, ALU.add).then_inc(dve_step, 1)
            dve.wait_ge(dve_step, next_step())
            for r in range(ROUNDS):
                for k in range(3):
                    v.tensor_scalar(count_scratch[:, k, :], scores_r[:, :], candidate[:, r, k + 1:k + 2], None, ALU.is_ge, ALU.add,
                                    accum_out=counts[:, r, k:k + 1]).then_inc(search_dve, 1)
                if r + 1 <= ROUNDS:
                    v.tensor_scalar(next_from[:, r, :], steps[:, 4 * (r + 1):4 * (r + 2)], candidate[:, r, 0:1], None,
                                    ALU.add).then_inc(dve_step, 1)
                    dve.wait_ge(dve_step, next_step())
                dve.wait_ge(search_pe, r + 1)
                v.tensor_scalar(reach_scratch[:, r, :], SC[:, r % 2, 0:3], KEEP - 0.5, None, ALU.is_ge, ALU.add,
                                accum_out=reached[:, r:r + 1]).then_inc(dve_step, 1)
                dve.wait_ge(dve_step, next_step())
                v.scalar_tensor_tensor(candidate[:, r + 1, :], reached[:, r:r + 1].to_broadcast([P, 4]),
                                       2.0 ** -4 * 4.0 ** -r, next_from[:, r, :], ALU.mult, ALU.add).then_inc(dve_step, 1)
                dve.wait_ge(dve_step, next_step())
            T = candidate[:, ROUNDS, 0:1]
            v.tensor_scalar(above[:, :], scores_r[:, :], T, None, ALU.is_gt, ALU.add, accum_out=totals[:, 0:1])\
                .then_inc(sel_pe, 1)
            v.tensor_scalar(ties[:, :], scores_r[:, :], T, None, ALU.is_equal, ALU.add, accum_out=totals[:, 1:2])\
                .then_inc(sel_pe, 1)
            dve.wait_ge(sel_pe, 2)
            v.tensor_tensor_scan(SG[:, :], ones[:, 0:1].to_broadcast([P, CT]), above[:, :], 0.0, ALU.mult, ALU.add)\
                .then_inc(dve_step, 1)
            dve.wait_ge(dve_step, next_step())
            v.tensor_tensor_scan(SE[:, :], ones[:, 0:1].to_broadcast([P, CT]), ties[:, :], 0.0, ALU.mult, ALU.add)\
                .then_inc(dve_step, 1)
            dve.wait_ge(dve_step, next_step())
            dve.wait_ge(pos_done, 1)
            v.tensor_copy(offsets[:, :], MP[:, 0:4]).then_inc(dve_step, 1)
            dve.wait_ge(dve_step, next_step())
            v.tensor_scalar(need[:, 0:1], offsets[:, 2:3], -1.0, float(KEEP), ALU.mult, ALU.add).then_inc(dve_step, 1)
            dve.wait_ge(dve_step, next_step())
            v.tensor_tensor(need[:, 1:2], need[:, 0:1], offsets[:, 1:2], ALU.subtract).then_inc(dve_step, 1)
            dve.wait_ge(dve_step, next_step())
            v.scalar_tensor_tensor(W1[:, :], SE[:, :], need[:, 1:2], ties[:, :], ALU.is_le, ALU.mult)\
                .then_inc(dve_step, 1)
            dve.wait_ge(dve_step, next_step())
            v.tensor_tensor(W2[:, :], above[:, :], W1[:, :], ALU.add).then_inc(dve_step, 1)
            dve.wait_ge(dve_step, next_step())
            v.tensor_scalar(W3[:, :], SE[:, :], offsets[:, 1:2], need[:, 0:1], ALU.add, ALU.min).then_inc(dve_step, 1)
            dve.wait_ge(dve_step, next_step())
            v.scalar_tensor_tensor(W4[:, :], SG[:, :], offsets[:, 0:1], W3[:, :], ALU.add, ALU.add).then_inc(dve_step, 1)
            dve.wait_ge(dve_step, next_step())
            v.tensor_scalar(W5[:, :], W4[:, :], cc("gap_from"), float(GAP), ALU.is_gt, ALU.mult).then_inc(dve_step, 1)
            dve.wait_ge(dve_step, next_step())
            v.tensor_tensor(W3[:, :], W4[:, :], W5[:, :], ALU.add).then_inc(dve_step, 1)
            dve.wait_ge(dve_step, next_step())
            v.scalar_tensor_tensor(W1[:, :], W3[:, :], -1.0 - NOT_KEPT, W2[:, :], ALU.add, ALU.mult)\
                .then_inc(dve_step, 1)
            dve.wait_ge(dve_step, next_step())
            v.tensor_scalar(W5[:, :], W1[:, :], NOT_KEPT, None, ALU.add).then_inc(pos_ready, 1)
            dve.wait_ge(pos_done, 2)
            v.tensor_copy(place_int[:, :], MP[:, 0:CT]).then_inc(dve_step, 1)
            dve.wait_ge(dve_step, next_step())
            v.tensor_single_scalar(row_int[:, :], place_int[:, :], P - 1, ALU.bitwise_and).then_inc(dve_step, 1)
            dve.wait_ge(dve_step, next_step())
            v.tensor_single_scalar(block_int[:, :], place_int[:, :], 7, ALU.logical_shift_right).then_inc(dve_step, 1)
            dve.wait_ge(dve_step, next_step())
            v.tensor_copy(row_of[:, :, :].rearrange("p t h -> p (t h)"), row_int[:, :]).then_inc(pos_ready, 1)
            v.tensor_copy(block_of[:, :, :].rearrange("p t h -> p (t h)"), block_int[:, :]).then_inc(pos_ready, 1)

            def index(i, b, pos):
                dve.wait_ge(idx_mm, i + 1)
                if has(i, -2):
                    dve.wait_ge(gathered, 16 * (STEPS * (i - 1) - EARLY))
                v.scalar_tensor_tensor(idx[:, b, :], bank(pos)[:, 0:STEPS], float(H),
                                       row_add[:, bass.ds(STEPS * i, STEPS)],
                                       ALU.mult, ALU.add).then_inc(idx_ready, 1)

            def maximum(b, u, pos, units_before):
                e, half = u // 32, u % 2
                a, z = SCORE_COLS[e][half]
                dve.wait_ge(s_filled, units_before + u + 1)
                v.tensor_reduce(tile_max[:, b, u:u + 1], bank(pos)[:, 0:z - a], AX.X, ALU.max)\
                    .then_inc(s_reduced, 1)

            def split_max(i, b, e):
                k = 5 * (2 * i + e)
                dve.wait_ge(s_reduced, SUNITS * i + 32 * (e + 1))
                v.tensor_reduce(NM[:, 0, 0:NT], tile_max[:, b, 32 * e:32 * e + 32].rearrange("p (n two) -> p n two", two=2),
                                AX.X, ALU.max, negate=True).then_inc(m_chain, 1)
                dve.wait_ge(m_chain, k + 1)
                if has(i, -1):
                    dve.wait_ge([mtr_even, mtr_odd][e], i)
                for part in range(PARTS - 1):
                    v.tensor_copy(SM[:, e, part, :], NM[:, part, 0:NT]).then_inc(m_chain, 1)
                    dve.wait_ge(m_chain, k + 2 * part + 2)
                    v.tensor_tensor(NM[:, part + 1, 0:NT], NM[:, part, 0:NT], SM[:, e, part, :], ALU.subtract)\
                        .then_inc(m_chain, 1)
                    dve.wait_ge(m_chain, k + 2 * part + 3)
                v.tensor_copy(SM[:, e, 2, :], NM[:, 2, 0:NT]).then_inc([m_split_even, m_split_odd][e], 1)

            def copy_mt(i, e, pos):
                dve.wait_ge([mtr_even, mtr_odd][e], i + 1)
                if has(i, -1):
                    dve.wait_ge([mrow_even, mrow_odd][e], 16 * i)
                v.tensor_copy(MT[:, e, :], bank16(pos)[0:PARTS * NT, 0:P]).then_inc([mt_even, mt_odd][e], 1)

            def copy_kt(i, b, pos):
                if has(i, -1):
                    dve.wait_ge(ktr_done, i + 1)
                else:
                    dve.wait_ge(ktr_early, 1)
                v.tensor_copy(KTM[0:64, b, 0:7 * P], bank16(pos)[0:64, 0:7 * P]).then_inc(kt_even, 1)

            def copy_kte(i, b):
                dve.wait_ge(kt_odd, i + 1)
                dve.wait_ge(kt_even, i + 1)
                if has(i, -2):
                    dve.wait_ge(st_filled, 2 * STEPS * (i - 1))
                v.tensor_copy(KTE[:, b, :], KTM[:, b, :]).then_inc(kte_ready, 1)

            def normalize(i, pos):
                dve.wait_ge(otr_done, i + 1)
                t = bank(pos).rearrange("p (b g c) -> p b g c", b=4, g=4)
                if has(i, -1):
                    dve.wait_ge(o_norm, 2 * i)
                v.reciprocal(REC[:, :, :, :], t[:, :, :, D::16]).then_inc(rec_ready, 1)
                dve.wait_ge(rec_ready, i + 1)
                for e in range(2):
                    dst = AT[:, :, bass.ds(2 * D * i + D * e, D)].rearrange("p (g b) d -> p b g d", g=4)
                    v.tensor_tensor(dst, t[:, :, :, 16 * e:16 * e + D],
                                    REC[:, :, :, e:e + 1].to_broadcast([P, 4, 4, D]), ALU.mult)\
                        .then_inc(o_norm, 1)

            def onehot(i, b):
                for t in range(NT):
                    last = v.tensor_scalar(A1[:, b, 0, t, :], place16[:, :], row_of[:, t, 2 * i:2 * i + 1], None,
                                           ALU.is_equal)
                last.then_inc(onehot_ready, 1)

            def columns(h0, h1):
                for h in range(h0, h1):
                    e = h % 2
                    v.tensor_tensor(B0[:, h, :, :], block_of[:, :, h:h + 1].to_broadcast([P, NT, BLOCKS]),
                                    blocks[:, BLOCKS * e:BLOCKS * (e + 1)].rearrange("p (a n) -> p a n", a=1)
                                    .to_broadcast([P, NT, BLOCKS]), ALU.is_equal).then_inc(b_parts, 1)
                dve.wait_ge(b_parts, h1)
                last = v.tensor_tensor(B1[:, h0:h1, :, :], B0[:, h0:h1, :, :],
                                       token.rearrange("p (a t b) -> p a t b", a=1, b=1)
                                       .to_broadcast([P, h1 - h0, NT, BLOCKS]), ALU.mult)
                last.then_inc(onehot_ready, 1)

            dve.wait_ge(pos_ready, 3)
            columns(0, 2)
            onehot(0, 0)
            index(0, 0, 0)
            onehot(1, 1)
            columns(2, H)
            index(1, 1, 1)
            dve.wait_ge(idx_mm, 1)
            onehot(2, 0)
            copy_kt(0, 0, 2)
            for n, kind in enumerate(LEAD_UNITS):
                if kind == "turn_m_even":
                    copy_mt(0, 0, n)
                else:
                    if kind == 32:
                        split_max(0, 0, 0)
                    if kind == 40:
                        copy_kte(0, 0)
                    maximum(0, kind, n, 0)

            def pair(i, b):
                units = product(dve, SUNITS, i)
                last_pair = not has(i, 1)
                for pos, kind in enumerate(UNITS if has(i, -1) else FIRST_UNITS):
                    if kind == "turn_o":
                        normalize(i - 1, pos)
                    elif kind == "turn_second_k":
                        copy_kt(1, 1, pos)
                    elif kind == "index":
                        if has(i, 2):
                            index(i + 2, b, pos)
                    elif kind == "turn_m_odd":
                        copy_mt(i, 1, pos)
                        if not last_pair:
                            copy_kte(i + 1, 1 - b)
                    elif kind == "turn_m_even":
                        if not last_pair:
                            copy_mt(i + 1, 0, pos)
                    elif kind == "turn_k":
                        if has(i, 2):
                            copy_kt(i + 2, b, pos)
                    else:
                        u = LEAD + kind
                        if u < SUNITS:
                            maximum(b, u, pos, units)
                            if u == SUNITS - 1:
                                split_max(i, b, 1)
                        elif not last_pair:
                            maximum(1 - b, u - SUNITS, pos, units + SUNITS)
                            if u - SUNITS == 31:
                                split_max(i + 1, 1 - b, 0)

            pair(0, 0)
            with dve.Fori(1, NP - 4, 2) as i:
                pair(i, 1)
                pair(i + 1, 0)
            for i in range(NP - 3, NP):
                pair(i, i % 2)
            early_heads, last_heads = slice(0, E - 2 * D), slice(E - 2 * D, E)
            dve.wait_ge(gated, 4)
            v.tensor_tensor(X2[:, :, early_heads], GAT[:, :, early_heads], X[:, :, early_heads], ALU.add)\
                .then_inc(x2_ready, 1)
            normalize(NP - 1, 0)
            next_tail = itertools.count(1).__next__

            def statistics2(g):
                for t in range(4 * g, 4 * g + 4):
                    v.bn_stats(stats[:, t, :], X2[:, t, :]).then_inc(stats2_ready, 1)
                for t in range(4 * g, 4 * g + 4):
                    dve.wait_ge(stats2_ready, 8 * g + t - 4 * g + 1)
                    v.bn_aggr(mv[:, t, :], stats[:, t, :]).then_inc(stats2_ready, 1)

            def normalize2(g):
                dve.wait_ge(std2_ready, g + 1)
                v.reciprocal(rstd[:, 4 * g:4 * g + 4], std[:, 4 * g:4 * g + 4]).then_inc(tail_step, 1)
                dve.wait_ge(tail_step, next_tail())
                for t in range(4 * g, 4 * g + 4):
                    v.tensor_scalar(XN2[:, t, 0:E], X2[:, t, :], mv[:, t, 0:1], rstd[:, t:t + 1], ALU.subtract,
                                    ALU.mult).then_inc(xn2_ready, 1)

            v.tensor_copy(XN2[:, :, E:E + 1], cc("number").rearrange("p (t a) -> p t a", a=1)).then_inc(tail_step, 1)
            dve.wait_ge(tail_step, next_tail())
            dve.wait_ge(o_norm, 2 * NP)
            v.tensor_tensor(GAT[:, :, last_heads], AT[:, :, last_heads],
                            gate[:, 0:1, last_heads].to_broadcast([P, NT, 2 * D]), ALU.mult).then_inc(gated, 1)
            dve.wait_ge(gated, 5)
            v.tensor_tensor(X2[:, :, last_heads], GAT[:, :, last_heads], X[:, :, last_heads], ALU.add)\
                .then_inc(x2_ready, 1)
            dve.wait_ge(x2_ready, 2)
            statistics2(0)
            for g in range(1, 4):
                statistics2(g)
                normalize2(g - 1)
            normalize2(3)
            dve.wait_ge(route_done, 4)

            def te(ap):
                return ap.rearrange("p (t e) -> p t e", e=NE)

            def bc(ap):
                return ap.rearrange("p (t a) -> p t a", a=1).to_broadcast([P, NT, NE])

            LG = OP[:, 0:NT * NE]
            v.tensor_reduce(LM[:, 0, :], te(LG), AX.X, ALU.max).then_inc(tail_dve, 1)
            dve.wait_ge(tail_dve, 1)
            v.tensor_tensor(te(LE[:, 0, :]), te(LG), bc(LM[:, 0, :]), ALU.subtract).then_inc(tail_dve, 1)
            dve.wait_ge(exp2_done, 1)
            v.tensor_reduce(LM[:, 1, :], te(LE[:, 1, :]), AX.X, ALU.add).then_inc(tail_step, 1)
            dve.wait_ge(tail_step, next_tail())
            v.reciprocal(LM[:, 2, :], LM[:, 1, :]).then_inc(tail_step, 1)
            dve.wait_ge(tail_step, next_tail())
            v.tensor_tensor(te(LE[:, 2, :]), te(LE[:, 1, :]), bc(LM[:, 2, :]), ALU.mult).then_inc(tail_step, 1)
            dve.wait_ge(tail_step, next_tail())
            v.tensor_reduce(LM[:, 3, :], te(LE[:, 2, :]), AX.X, ALU.max).then_inc(tail_step, 1)
            dve.wait_ge(tail_step, next_tail())
            v.tensor_tensor(te(LE[:, 3, :]), te(LE[:, 2, :]), bc(LM[:, 3, :]), ALU.is_equal).then_inc(tail_step, 1)
            dve.wait_ge(tail_step, next_tail())
            expert = cc("expert").rearrange("p (e t) -> p t e", e=NE)
            v.tensor_tensor(te(LE[:, 4, :]), te(LE[:, 3, :]), expert, ALU.mult).then_inc(tail_step, 1)
            dve.wait_ge(tail_step, next_tail())
            v.tensor_reduce(slotF[:, :], te(LE[:, 4, :]), AX.X, ALU.min).then_inc(tail_step, 1)
            dve.wait_ge(tail_step, next_tail())
            v.tensor_tensor(OH[:, :, :].rearrange("p e t -> p t e"), expert, bc(slotF[:, :]), ALU.is_equal)\
                .then_inc(tail_step, 1)
            dve.wait_ge(tail_step, next_tail())
            v.tensor_copy(OHB[:, :], OH[:, :, :].rearrange("p e t -> p (e t)")).then_inc(oh_ready, 1)
            dve.wait_ge(rank_done, 1)
            RANK = OP[:, 0:P]
            v.tensor_copy(TOT[:, :, :].rearrange("p e t -> p (e t)"), OP[:, P:2 * P]).then_inc(tail_step, 1)
            dve.wait_ge(tail_step, next_tail())
            v.tensor_tensor_scan(CUM[:, 1:], ones[:, 0:NE * NT], TOT[:, :, :].rearrange("p e t -> p (e t)"), 0.0,
                                 ALU.mult, ALU.add).then_inc(tail_step, 1)
            dve.wait_ge(tail_step, next_tail())
            ends = CUM[:, NT::NT]
            starts = CUM[:, 0:NE * NT:NT]
            v.tensor_tensor(EN[:, 0, :], ends, starts, ALU.subtract).then_inc(tail_step, 1)
            dve.wait_ge(tail_step, next_tail())
            v.tensor_scalar(EN[:, 1, :], EN[:, 0, :], P - 1.0, None, ALU.add).then_inc(tail_step, 1)
            dve.wait_ge(tail_step, next_tail())
            v.tensor_copy(ENI[:, 0, :], EN[:, 1, :]).then_inc(tail_step, 1)
            dve.wait_ge(tail_step, next_tail())
            v.tensor_single_scalar(ENI[:, 1, :], ENI[:, 0, :], 7, ALU.logical_shift_right).then_inc(tail_step, 1)
            dve.wait_ge(tail_step, next_tail())
            v.tensor_copy(EN[:, 2, :], ENI[:, 1, :]).then_inc(tail_step, 1)
            dve.wait_ge(tail_step, next_tail())
            v.tensor_tensor_scan(EN[:, 3, :], ones[:, 0:NE], EN[:, 2, :], 0.0, ALU.mult, ALU.add)\
                .then_inc(tail_step, 1)
            dve.wait_ge(tail_step, next_tail())
            v.tensor_tensor(EN[:, 4, :], EN[:, 3, :], EN[:, 2, :], ALU.subtract).then_inc(tail_step, 1)
            dve.wait_ge(tail_step, next_tail())
            v.scalar_tensor_tensor(EN[:, 5, :], EN[:, 4, :], float(P), starts, ALU.mult, ALU.subtract)\
                .then_inc(tail_step, 1)
            dve.wait_ge(tail_step, next_tail())
            v.tensor_tensor(SLB[:, :, :].rearrange("p e t -> p (e t)"), CUM[:, 0:NE * NT], RANK, ALU.add)\
                .then_inc(tail_step, 1)
            dve.wait_ge(tail_step, next_tail())
            v.tensor_tensor(SLC[:, :, :], SLB[:, :, :],
                            EN[:, 5, :].rearrange("p (e a) -> p e a", a=1).to_broadcast([P, NE, NT]), ALU.add)\
                .then_inc(tail_step, 1)
            dve.wait_ge(tail_step, next_tail())
            v.tensor_tensor(SLB[:, :, :], SLC[:, :, :], OH[:, :, :], ALU.mult).then_inc(tail_step, 1)
            dve.wait_ge(tail_step, next_tail())
            v.tensor_reduce(slotF[:, :], SLB[:, :, :].rearrange("p e t -> p t e"), AX.X, ALU.add)\
                .then_inc(tail_step, 1)
            dve.wait_ge(tail_step, next_tail())
            v.tensor_copy(slot[:, :], slotF[:, :]).then_inc(slot_ready, 1)
            v.tensor_tensor(TE[:, :, :], cc("slot_tile").rearrange("p (s e) -> p s e", e=NE),
                            EN[:, 3:4, :].to_broadcast([P, SLOT_TILES, NE]), ALU.is_ge).then_inc(tail_step, 1)
            dve.wait_ge(tail_step, next_tail())
            v.tensor_reduce(TEF[:, :], TE[:, :, :], AX.X, ALU.add).then_inc(tail_step, 1)
            dve.wait_ge(tail_step, next_tail())
            v.tensor_scalar(TEI[:, 0:SLOT_TILES], TEF[:, :], NE - 1.0, None, ALU.min).then_inc(tile_ready, 1)
            dve.wait_ge(tile_ready, 1)
            dve.wait_ge(we_in, 32)
            dve.wait_ge(slots_in, 16)
            v.tensor_copy(owner[:, :], HS[:, :, E:E + 1].rearrange("p t a -> p (t a)")).then_inc(owner_ready, 1)

            expert_reg = [dve.alloc_register("expert_even"), dve.alloc_register("expert_odd")]

            def load_expert(n, b):
                dve.reg_load(expert_reg[b], TEI[0:1, bass.ds(n, 1)])

            def take_fc(n, b, e):
                if not isinstance(n, int):
                    dve.wait_ge(up_done, n - 1)
                v.tensor_copy(WFC[:, b, :], WE[:, bass.ds(e, 1), 0:HD].rearrange("p a c -> p (a c)"))\
                    .then_inc(fc_ready, 1)

            def take_proj(n, b, e):
                if not isinstance(n, int):
                    dve.wait_ge(down_done, n - 1)
                v.tensor_copy(WPROJ[:, b, :], WE[:, bass.ds(e, 1), HD:].rearrange("p a c -> p (a c)"))\
                    .then_inc(proj_ready, 1)

            def gated_result(n, b):
                dve.wait_ge(down_done, n + 1)
                v.tensor_tensor(YS[:, bass.ds(n, 1), :].rearrange("p a e -> p (a e)"), ST[:, b, 0:E], gate[:, 1, :],
                                ALU.mult).then_inc(y_ready, 1)

            load_expert(0, 0)
            for n in range(2):
                e = dve.snap(expert_reg[n], min_val=0, max_val=NE - 1)
                take_fc(n, n, e)
                load_expert(n + 1, 1 - n)
                take_proj(n, n, e)
            with dve.Fori(2, SLOT_TILES - 1, 2) as n:
                for b in range(2):
                    e = dve.snap(expert_reg[b], min_val=0, max_val=NE - 1)
                    take_fc(n + b, b, e)
                    load_expert(n + b + 1, 1 - b)
                    take_proj(n + b, b, e)
                    gated_result(n + b - 2, b)
            for n in range(SLOT_TILES - 2, SLOT_TILES):
                gated_result(n, n % 2)

        @block.tensor
        def _(pe):
            mm = nc.tensor.matmul
            pe.wait_ge(const_in, 16)
            pe.wait_ge(silu_ready, 2)
            for c in range(6):
                last = mm(OP[:, c:c + 1], WMOD[:, P * c:P * c + P], silu[:, :], start=True, stop=True)
            for a, c in ((0, 2), (1, 5)):
                last = mm(OP[:, P + P * a:2 * P + P * a], silu_b[:, :], WMOD[:, P * c:P * c + P], start=True, stop=True)
            last.then_inc(mod_done, 1)
            for g in range(4):
                for t in range(4 * g, 4 * g + 4):
                    pe.wait_ge(xn_ready, t + 1)
                    last = nc.tensor.transpose(ST[:, g // 2, 512 * (g % 2) + P * (t % 4):512 * (g % 2) + P * (t % 4) + P],
                                               XN[:, t, :], ident)
                last.then_inc(xt_done, 1)
            pe.wait_ge(w_in, 16 * 9)
            for j in range(4):
                pe.wait_ge(ht_ready, j + 1)
                last = mm(SC[32 * j:32 * j + RH, 0, :], WR1[:, :], HT[:, 512 * j:512 * j + 512], start=True, stop=True)
            last.then_inc(h1_done, 1)
            pe.wait_ge(wr2_in, 8)
            pe.wait_ge(h1_ready, 1)
            mm(SC[:, 1, 0:CT], WR2[:, 0, :], H1[:, 0:CT], start=True, stop=False)
            mm(SC[:, 1, 0:CT], WR2[:, 1, :], H1[:, CT:2 * CT], start=False, stop=True).then_inc(logit_done, 1)
            pe.wait_ge(gate_ready, 1)

            def q_chunk(g):
                mm(ST[:, g // 2, 512 * (g % 2):512 * (g % 2) + 512], WQ[:, :], HT[:, 512 * g:512 * g + 512],
                   start=True, stop=True).then_inc(q_done, 1)

            def kv(n):
                if n >= 2:
                    pe.wait_ge(kv_ready, n - 1)
                to = [OP[:, :], MI][n % 2]
                for t in range(2):
                    last = mm(to[:, 2 * E * t:2 * E * t + 2 * E], HT[:, P * (2 * n + t):P * (2 * n + t) + P], WKV[:, :],
                              start=True, stop=True)
                last.then_inc(kv_done, 1)

            pe.wait_ge(score0, 2)
            for r in range(ROUNDS):
                pe.wait_ge(search_dve, 3 * (r + 1))
                mm(SC[:, r % 2, 0:3], same_head16[:, :], counts[:, r, :], start=True, stop=True).then_inc(search_pe, 1)
                if r < 4:
                    q_chunk(r)
                else:
                    kv(r - 4)
            pe.wait_ge(sel_pe, 2)
            mm(MP[:, 0:2], before, totals[:, :], start=True, stop=True)
            mm(MP[:, 2:4], same_head, totals[:, :], start=True, stop=True).then_inc(pos_done, 1)
            kv(NT // 2 - 1)
            pe.wait_ge(pos_ready, 1)
            for u in range(2):
                last = nc.tensor.transpose(MP[:, P * u:P * u + P], W5[:, P * u:P * u + P], ident)
            last.then_inc(pos_done, 1)

            def index_mm(i, b, pos):
                pe.wait_ge(onehot_ready, i + 3 if has(i, -1) else 2)
                pe.wait_ge(onehot_odd, i + 1)
                if has(i, -2):
                    pe.wait_ge(pair_columns_ready, i - 1)
                for e in range(2):
                    for t in range(NT):
                        cols = pair_columns[:, b, e, BLOCKS * t:BLOCKS * (t + 1)] if has(i, -2) else B1[:, 2 * i + e, t, :]
                        last = mm(bank(pos)[:, 6 * e:6 * e + BLOCKS], A1[:, b, e, t, :], cols,
                                  start=(e == 0 and t == 0), stop=(e == 1 and t == NT - 1), skip_group_check=True)
                last.then_inc(idx_mm, 1)

            def turn_k(i, b, pos):
                pe.wait_ge(prep_ready, i + 1)
                pe.sem_inc(turning, 1)
                for s in range(STEPS):
                    col = STEP_COLUMN[s]
                    if s <= 6:
                        o = bank16(pos)[0:64, P * col:P * col + P]
                        last = nc.tensor.transpose(o, RS[:, b, 0:64] if s == 6 else KS[:, b, s, :], identb[:, :])
                    if s >= 6:
                        o = bank16(pos)[64:128, P * (col - 6):P * (col - 6) + P]
                        last = nc.tensor.transpose(o, RS[:, b, 64:128] if s == 6 else KS[:, b, s, :], identb[:, :])
                last.then_inc(ktr_done, 1)

            def turn_m(i, e, pos):
                pe.wait_ge([m_split_even, m_split_odd][e], i + 1)
                pe.sem_inc(turning, 1)
                nc.tensor.transpose(bank16(pos)[0:PARTS * NT, 0:P], SM[:, e, :, :].rearrange("p a t -> p (a t)"),
                                    identb[:, :]).then_inc([mtr_even, mtr_odd][e], 1)

            def turn_o(i, pos):
                pe.wait_ge(o_copied, i + 1)
                for q in range(4):
                    last = nc.tensor.transpose(bank(pos)[:, P * q:P * q + P], OS[:, P * q:P * q + P], ident)
                last.then_inc(otr_done, 1)

            def score_tile(i, b, u, pos, rows=P):
                e, qt, half = u // 32, u % 32 // 2, u % 2
                a, z = SCORE_COLS[e][half]
                mm(bank(pos)[:, 0:z - a], QSM[0:rows, b, P * qt:P * qt + P], KTM[0:rows, b, a:z],
                   start=True, stop=True).then_inc(s_filled, 1)

            def free_bank(i, pos, units):
                while True:
                    pos -= RING
                    if pos < 0:
                        i, pos, units = i - 1, pos + len(UNITS), units - SUNITS
                    kind = (UNITS if has(i, -1) else FIRST_UNITS)[pos]
                    if isinstance(i, int) and i < 0:
                        pe.wait_ge(s_reduced, LEAD - len(UNITS) + pos + 1)
                    elif done(i, kind):
                        continue
                    elif kind == "turn_o":
                        pe.wait_ge(o_norm, 2 * i)
                    elif kind == "index":
                        pe.wait_ge(idx_ready, i + 3)
                    elif kind == "turn_second_k":
                        pe.wait_ge(kt_odd, 2)
                        pe.wait_ge(kt_even, 2)
                    elif kind == "turn_k":
                        pe.wait_ge(kt_odd, i + 3)
                        pe.wait_ge(kt_even, i + 3)
                    elif kind == "turn_m_odd":
                        pe.wait_ge(mt_odd, i + 1)
                    elif kind == "turn_m_even":
                        pe.wait_ge(mt_even, i + 2)
                    else:
                        pe.wait_ge(s_reduced, units + LEAD + kind + 1)
                    return

            def scores(i, b, s, c, halves_before):
                half = c // 2
                n = halves_before + 2 * s + half
                if (has(i, -1) or s >= 1) and c % 2 == 0:
                    pe.wait_ge(exp_done, n - 1)
                col = STEP_COLUMN[s]
                rows = 64 + KROWS if s < 6 else P
                last = mm(ST[:, half, 512 * (c % 2):512 * (c % 2) + 512], KTE[0:rows, b, P * col:P * col + P],
                          QSE[0:rows, b, 512 * c:512 * c + 512], start=True, stop=True)
                if c % 2:
                    last.then_inc(st_filled, 1)

            def weigh_v(i, b, s, halves_before, part):
                if part == 0:
                    pe.wait_ge(exp_done, halves_before + 2 * s + 2)
                    if s == 0:
                        pe.wait_ge(v_ready, i + 1)
                        if has(i, -1):
                            pe.wait_ge(o_copied, i)
                for g in range(4):
                    c0 = 256 * part
                    last = mm(OP[32 * g:32 * g + 32, c0:c0 + 256], VS[:, b, s, :],
                              PR[:, (b + s) % 2, 512 * g + c0:512 * g + c0 + 256], start=(s == 0 and part == 0),
                              stop=(s == STEPS - 1 and part == 1),
                              skip_group_check=True)
                if part == 1:
                    last.then_inc(pv_done, 1)

            def done(i, kind):
                if kind in ("index", "turn_k"):
                    return not has(i, 2)
                if kind in ("turn_m_odd", "turn_o", "turn_second_k"):
                    return False
                return not has(i, 1) and (kind == "turn_m_even" or LEAD + kind >= SUNITS)

            def unit(i, b, pos, units):
                kind = (UNITS if has(i, -1) else FIRST_UNITS)[pos]
                last_pair = not has(i, 1)
                if done(i, kind):
                    return
                free_bank(i, pos, units)
                if kind == "turn_o":
                    turn_o(i - 1, pos)
                elif kind == "turn_second_k":
                    turn_k(1, 1, pos)
                elif kind == "index":
                    if has(i, 2):
                        index_mm(i + 2, b, pos)
                elif kind == "turn_k":
                    if has(i, 2):
                        turn_k(i + 2, b, pos)
                elif kind == "turn_m_odd":
                    turn_m(i, 1, pos)
                elif kind == "turn_m_even":
                    if not last_pair:
                        turn_m(i + 1, 0, pos)
                else:
                    u = LEAD + kind
                    if u < SUNITS:
                        score_tile(i, b, u, pos)
                    elif not last_pair:
                        if u == SUNITS:
                            pe.wait_ge([qsm_even, qsm_odd][1 - b], 48 * (i + b) + 96)
                            pe.wait_ge(kt_odd, i + 2)
                            pe.wait_ge(kt_even, i + 2)
                        score_tile(i + 1, 1 - b, u - SUNITS, pos)

            index_mm(0, 0, 0)
            pe.wait_ge(pos_ready, 3)
            index_mm(1, 1, 1)
            pe.wait_ge(kv_ready, NT // 2)
            pe.wait_ge(init_dve, 1)
            pe.wait_ge(prep_early, 1)
            for s in range(EARLY):
                o = bank16(2)[0:64, P * STEP_COLUMN[s]:P * STEP_COLUMN[s] + P]
                last = nc.tensor.transpose(o, RS[:, 0, 0:64] if s == 6 else KS[:, 0, s, :], identb[:, :])
            last.then_inc(ktr_early, 1)
            pe.wait_ge(kt_even, 1)
            pe.wait_ge(idx_ready, 2)
            pe.wait_ge(qsm_even, 16 * 6)
            for n, kind in enumerate(LEAD_UNITS):
                if n >= RING:
                    before_it = LEAD_UNITS[n - RING]
                    if before_it == "turn_m_even":
                        pe.wait_ge(mt_even, 1)
                    else:
                        pe.wait_ge(s_reduced, before_it + 1)
                if kind == "turn_m_even":
                    turn_m(0, 0, n)
                elif kind < 32:
                    if kind == 28:
                        pe.wait_ge(prep_ready, 1)
                        for s in range(EARLY - 1, STEPS):
                            col = STEP_COLUMN[s] - 6
                            o = OP[:, :].bitcast(BF16)[64:128, P * col:P * col + P]
                            last = nc.tensor.transpose(o, RS[:, 0, 64:128] if s == 6 else KS[:, 0, s, :], identb[:, :])
                        last.then_inc(ktr_done, 1)
                    score_tile(0, 0, kind, n, rows=64)
                else:
                    if kind == 32:
                        pe.wait_ge(kt_odd, 1)
                    score_tile(0, 0, kind, n)
            pe.wait_ge(s_reduced, LEAD)
            def pair(i, b):
                units, halves_before = product(pe, SUNITS, i), product(pe, 2 * STEPS, i)
                pe.wait_ge(kte_ready, i + 1)
                pe.wait_ge([qse_even, qse_odd][b], 48 * (i - b) + 96)
                pe.wait_ge(mrow_even, 16 * (i + 1))
                if not has(i, -1):
                    pe.wait_ge(init_dve, 1)
                at_unit = 0
                for s in range(STEPS):
                    if s == 6:
                        pe.wait_ge(mrow_odd, 16 * (i + 1))
                    pieces = [("scores", c) for c in range(4)] + [("weigh", part) for part in range(2)]
                    for n, (piece, arg) in enumerate(pieces):
                        if piece == "scores":
                            scores(i, b, s, arg, halves_before)
                        elif s > 0:
                            weigh_v(i, b, s - 1, halves_before, arg)
                        elif has(i, -1):
                            weigh_v(i - 1, 1 - b, STEPS - 1, halves_before - 2 * STEPS, arg)
                        while at_unit * STEPS * len(pieces) < len(UNITS) * (s * len(pieces) + n + 1):
                            unit(i, b, at_unit, units)
                            at_unit += 1

            pair(0, 0)
            with pe.Fori(1, NP - 4, 2) as i:
                pair(i, 1)
                pair(i + 1, 0)
            for i in range(NP - 3, NP):
                pair(i, i % 2)
            for part in range(2):
                weigh_v(NP - 1, (NP - 1) % 2, STEPS - 1, 2 * STEPS * (NP - 1), part)
            pe.wait_ge(s_reduced, SUNITS * NP)
            pe.wait_ge(o_norm, 2 * (NP - 1))
            pe.wait_ge(mt_odd, NP)
            turn_o(NP - 1, 0)
            def route(g):
                pe.wait_ge(h2_ready, g + 1)
                for t in range(4 * g, 4 * g + 4):
                    last = mm(OP[:, NE * t:NE * t + NE], H2T[:, P * t:P * t + P], WROUTE[:, :], start=True, stop=True)
                last.then_inc(route_done, 1)

            for g in range(4):
                for t in range(4 * g, 4 * g + 4):
                    pe.wait_ge(xn2_ready, t + 1)
                    c0 = 512 * (g % 2) + P * (t % 4)
                    last = nc.tensor.transpose(ST[:, g // 2, c0:c0 + P], XN2[:, t, 0:E], ident)
                last.then_inc(xt2_done, 1)
                if g:
                    route(g - 1)
            route(3)
            pe.wait_ge(oh_ready, 1)
            mm(OP[:, 0:P], lowerb[:, :], OHB[:, :], start=True, stop=True)
            mm(OP[:, P:2 * P], onesb[:, :], OHB[:, :], start=True, stop=True).then_inc(rank_done, 1)
            pe.wait_ge(slots_in, 16)
            for q in range((SLOT_TILES + 3) // 4):
                if q >= 2:
                    pe.wait_ge(hst_ready, q - 1)
                for t in range(4 * q, min(4 * q + 4, SLOT_TILES)):
                    c0 = P * (t % 4)
                    last = nc.tensor.transpose(ST[:, q % 2, c0:c0 + P], HS[:, t, 0:E], ident)
                last.then_inc(hst_done, 1)
            pe.wait_ge(hst_ready, (SLOT_TILES + 3) // 4)

            def up(n, b):
                pe.wait_ge(fc_ready, n + 1)
                if not isinstance(n, int) or n >= 2:
                    pe.wait_ge(relu_done, n - 1)
                for c in range(4):
                    last = mm(SC[:, b, P * c:P * c + P], WFC[:, b, P * c:P * c + P], HT[:, bass.ds(n * P, P)],
                              start=True, stop=True)
                last.then_inc(up_done, 1)

            def down(n, b):
                pe.wait_ge(proj_ready, n + 1)
                pe.wait_ge(sq_done, n + 1)
                if not isinstance(n, int) or n >= 2:
                    pe.wait_ge(y_ready, n - 1)
                for c in range(4):
                    last = mm(ST[:, b, 0:E], R2[:, b, P * c:P * c + P], WPROJ[:, b, P * c:P * c + P],
                              start=(c == 0), stop=(c == 3))
                last.then_inc(down_done, 1)

            pe.wait_ge(o_norm, 2 * NP)
            up(0, 0)
            up(1, 1)
            down(0, 0)
            with pe.Fori(2, SLOT_TILES - 1, 2) as n:
                up(n, 0)
                down(n - 1, 1)
                up(n + 1, 1)
                down(n, 0)
            down(SLOT_TILES - 1, 1)


def kernel(**inputs):
    import numpy as np
    import concourse.bacc as bacc
    from concourse.bass_utils import run_bass_kernel_spmd

    g = {k: np.asarray(v) for k, v in inputs.items()}
    w = g["L0_attn_qkv_w"].T.reshape(E, 3, H, D)
    b = g["L0_attn_qkv_b"].reshape(3, H, D)
    table, _ = constants()
    arrays = {
        "x": g["L0_attn_hidden_states"],
        "w_q": w[:, 0].reshape(E, E),
        "w_kv": w[:, 1:].transpose(0, 2, 1, 3).reshape(E, 2 * E),
        "b_q": b[0].reshape(E, 1),
        "b_kv": np.tile(b[1:].transpose(1, 0, 2).reshape(1, 2 * E), (P, 1)),
        "w_r1": g["L0_attn_r_w1"].T,
        "b_r1": np.tile(g["L0_attn_r_b1"], 4).reshape(P, 1),
        "w_r2": np.tile(g["L0_attn_r_w2"].T, (4, 1)),
        "b_r2": np.tile(g["L0_attn_r_b2"], CHUNKS).reshape(P, 1),
        "c_col": g["L0_c"].reshape(E, 1),
        "wmod": g["L0_wmod"],
        "w_route": g["L0_ffn_router_w"].T,
        "w_fc": g["L0_ffn_expert_fc"],
        "w_proj": g["L0_ffn_expert_proj"].transpose(0, 2, 1).reshape(NE, 4, P, E).transpose(0, 2, 1, 3)
        .reshape(NE, P, HD),
        "const": table,
    }
    nc = bacc.Bacc("TRN2", target_bir_lowering=False, num_devices=1)
    arrays = {f"in_{k}": np.ascontiguousarray(a) for k, a in arrays.items()}
    args = [nc.dram_tensor(k, a.shape, mybir.dt.from_np(a.dtype), kind="ExternalInput").ap() for k, a in arrays.items()]
    args.append(nc.dram_tensor("out_0", (1, L, E), F32, kind="ExternalOutput").ap())
    build(nc, *args)
    r = run_bass_kernel_spmd(nc, [arrays], core_ids=[0])
    return r.results[0]["out_0"]
```
